# Optimizing a Trainium2 kernel written in Bass

```python
import numpy as np
import jax
import jax.numpy as jnp

def _softmax(x, axis=-1):
    return jax.nn.softmax(x, axis=axis)

def _gelu(x):
    return jax.nn.gelu(x, approximate=True)

def _silu(x):
    return jax.nn.silu(x)

def _sigmoid(x):
    return jax.nn.sigmoid(x)

def _layernorm(x, axis=-1, eps=1e-05):
    m = jnp.mean(x, axis=axis, keepdims=True)
    v = jnp.var(x, axis=axis, keepdims=True)
    return (x - m) / jnp.sqrt(v + eps)

def _scatter_add(tgt, idx, src, axis=0):
    return tgt.at[idx].add(src)

def _segment_sum(src, seg, n):
    return jax.ops.segment_sum(src, seg, n)
kernel_name = 'mk_perceiver_d2_seqx_r8_43f841'

def setup_inputs(seed: int=0):
    np.random.seed(seed)
    _w = jnp.asarray

    def _rec_inputs():
        import jax
        import jax.numpy as jnp
        _rk = jax.random.key(seed)
        x = 7.22e-05 + 1 * jax.random.normal(jax.random.fold_in(_rk, 1), (32, 64, 128), jnp.float32)
        _lenS = 64 - jax.random.randint(jax.random.fold_in(_rk, 7), (32,), 0, max(1, 64 // 4) + 1, jnp.int32)
        _lenS2 = 1601 - jax.random.randint(jax.random.fold_in(_rk, 8), (32,), 0, max(1, 1601 // 4) + 1, jnp.int32)
        _ctx_1024P = jax.random.normal(jax.random.fold_in(_rk, 11), (32, 16, 128), jnp.float32)
        _ctx_1024c = jax.random.dirichlet(jax.random.fold_in(_rk, 511), 0.3 * jnp.ones((16,), jnp.float32), (32, 1601))
        _ctx_1024t = jnp.einsum('bsk,bkd->bsd', _ctx_1024c, _ctx_1024P)
        _ctx_1024t = _ctx_1024t * jax.lax.rsqrt(jnp.mean(jnp.square(_ctx_1024t)) + 1e-12) * 0.953939
        ctx_1024 = 4.13588e-05 + 0.999923 * (_ctx_1024t + 0.3 * jax.random.normal(jax.random.fold_in(_rk, 611), (32, 1601, 128), jnp.float32))
        _validS = jnp.arange(64)[None, :] < _lenS[:, None]
        _validS2 = jnp.arange(1601)[None, :] < _lenS2[:, None]
        _causal = jnp.tril(jnp.ones((64, 64), dtype=bool))
        mask_BxS2_bf1 = jnp.ones((32, 1601), dtype=bool)
        return (x, ctx_1024, mask_BxS2_bf1)
    x, ctx_1024, mask_BxS2_bf1 = _rec_inputs()

    def _L0_xattn_setup():
        import jax, jax.numpy as jnp
        import numpy as np
        C = 128
        B, SQ, SKV = (4, 256, 256)
        key = jax.random.key(seed)
        ks = jax.random.split(key, 10)
        s = 1.0 / np.sqrt(C)
        return {'x': jax.random.normal(ks[0], (B, SQ, C), jnp.float32), 'content_embeddings': jax.random.normal(ks[1], (B, SKV, C), jnp.float32), 'Wq': jax.random.normal(ks[2], (C, C), jnp.float32) * s, 'bq': jnp.zeros((C,), jnp.float32), 'Wk': jax.random.normal(ks[3], (C, C), jnp.float32) * s, 'bk': jnp.zeros((C,), jnp.float32), 'Wv': jax.random.normal(ks[4], (C, C), jnp.float32) * s, 'bv': jnp.zeros((C,), jnp.float32), 'Wo': jax.random.normal(ks[5], (C, C), jnp.float32) * s, 'bo': jnp.zeros((C,), jnp.float32)}
    _L0_xattn_all = _L0_xattn_setup()
    _L0_xattn_in = {k: v for k, v in _L0_xattn_all.items() if k in ('Wq', 'bq', 'Wk', 'bk', 'Wv', 'bv', 'Wo', 'bo')}
    del _L0_xattn_all

    def _L0_attn_setup():
        import math
        import jax, jax.numpy as jnp
        import numpy as np
        N_HEAD = 16

        def _rope_cos_sin(l, head_dim):
            scale = jnp.arange(0, head_dim, 2, dtype=jnp.float32)[:head_dim // 2]
            freqs = 1.0 / 10000.0 ** scale
            angles = jnp.arange(l, dtype=jnp.float32)[:, None] * freqs[None, :]
            return (jnp.cos(angles), jnp.sin(angles))

        def _rope_apply(x, cos, sin):
            b, l, h, hd = x.shape
            xp = x.astype(jnp.float32).reshape(b, l, h, hd // 2, 2)
            xr, xi = (xp[..., 0], xp[..., 1])
            c = cos[None, :, None, :]
            s = sin[None, :, None, :]
            out_r = xr * c - xi * s
            out_i = xr * s + xi * c
            out = jnp.stack([out_r, out_i], axis=-1).reshape(b, l, h, hd)
            return out.astype(x.dtype)
        key = jax.random.key(seed)
        ks = jax.random.split(key, 9)
        b, l, d = (2, 256, 128)
        sc = 1.0 / math.sqrt(d)
        inp = {'x': jax.random.normal(ks[0], (b, l, d), dtype=jnp.float32), 'Wq': jax.random.normal(ks[1], (d, d), dtype=jnp.float32) * sc, 'bq': jnp.zeros((d,), dtype=jnp.float32), 'Wk': jax.random.normal(ks[2], (d, d), dtype=jnp.float32) * sc, 'bk': jnp.zeros((d,), dtype=jnp.float32), 'Wv': jax.random.normal(ks[3], (d, d), dtype=jnp.float32) * sc, 'bv': jnp.zeros((d,), dtype=jnp.float32), 'Wo': jax.random.normal(ks[4], (d, d), dtype=jnp.float32) * sc, 'bo': jnp.zeros((d,), dtype=jnp.float32)}
        return inp
    _L0_attn_all = _L0_attn_setup()
    _L0_attn_in = {k: v for k, v in _L0_attn_all.items() if k in ('Wq', 'bq', 'Wk', 'bk', 'Wv', 'bv', 'Wo', 'bo')}
    del _L0_attn_all

    def _L0_ffn_setup():
        import jax, jax.numpy as jnp
        import numpy as np
        D = 128
        H = 16
        FF = 512
        E = 8
        K = 2
        EH = 128
        B, S = (2, 256)
        EPS = 1e-05

        def rmsnorm(x, w):
            v = jnp.mean(jnp.square(x), axis=-1, keepdims=True)
            return x * jax.lax.rsqrt(v + EPS) * w

        def _dense_path(x, wq, wk, wv, wo, w1, w2, w3, attn_norm_w, ff_norm_w):
            b, s, d = x.shape
            hd = d // H
            q = (x @ wq).reshape(b, s, H, hd)
            k = (x @ wk).reshape(b, s, H, hd)
            v = (x @ wv).reshape(b, s, H, hd)
            scores = jnp.einsum('bqhd,bkhd->bhqk', q, k) / np.sqrt(hd).astype(np.float32)
            causal = jnp.tril(jnp.ones((s, s), bool))
            scores = jnp.where(causal, scores, jnp.finfo(scores.dtype).min)
            attn = jax.nn.softmax(scores, axis=-1)
            o = jnp.einsum('bhqk,bkhd->bqhd', attn, v).reshape(b, s, d)
            h = x + rmsnorm(o @ wo, attn_norm_w)
            ffn = jax.nn.silu(h @ w1) * (h @ w3) @ w2
            return h + rmsnorm(ffn, ff_norm_w)

        def _sparse_path(x, router_w, ew1, ew2, ew3, moe_norm_w):
            b, s, d = x.shape
            xt = x.reshape(-1, d)
            probs = jax.nn.softmax(xt @ router_w, axis=-1)
            topw, topi = jax.lax.top_k(probs, K)
            g = jax.nn.silu(jnp.einsum('td,edh->eth', xt, ew1)) * jnp.einsum('td,edh->eth', xt, ew3)
            eo = jnp.einsum('eth,ehd->ted', g, ew2)
            sel = jnp.take_along_axis(eo, topi[:, :, None], axis=1)
            moe_out = jnp.sum(topw[:, :, None] * sel, axis=1).reshape(b, s, d)
            return rmsnorm(moe_out, moe_norm_w)
        key = jax.random.key(seed)
        ks = jax.random.split(key, 16)
        s = 0.02
        return {'x': jax.random.normal(ks[0], (B, S, D), jnp.float32), 'wq': jax.random.normal(ks[1], (D, D), jnp.float32) * s, 'wk': jax.random.normal(ks[2], (D, D), jnp.float32) * s, 'wv': jax.random.normal(ks[3], (D, D), jnp.float32) * s, 'wo': jax.random.normal(ks[4], (D, D), jnp.float32) * s, 'w1': jax.random.normal(ks[5], (D, FF), jnp.float32) * s, 'w2': jax.random.normal(ks[6], (FF, D), jnp.float32) * s, 'w3': jax.random.normal(ks[7], (D, FF), jnp.float32) * s, 'attn_norm_w': jnp.ones((D,), jnp.float32), 'ff_norm_w': jnp.ones((D,), jnp.float32), 'moe_norm_w': jnp.ones((D,), jnp.float32), 'router_w': jax.random.normal(ks[8], (D, E), jnp.float32) * s, 'ew1': jax.random.normal(ks[9], (E, D, EH), jnp.float32) * s, 'ew2': jax.random.normal(ks[10], (E, EH, D), jnp.float32) * s, 'ew3': jax.random.normal(ks[11], (E, D, EH), jnp.float32) * s}
    _L0_ffn_all = _L0_ffn_setup()
    _L0_ffn_in = {k: v for k, v in _L0_ffn_all.items() if k in ('wq', 'wk', 'wv', 'wo', 'w1', 'w2', 'w3', 'attn_norm_w', 'ff_norm_w', 'moe_norm_w', 'router_w', 'ew1', 'ew2', 'ew3')}
    del _L0_ffn_all

    def _L1_xattn_setup():
        import jax, jax.numpy as jnp
        import numpy as np
        N_HEADS = 16
        D_MODEL = 128
        HEAD_DIM = D_MODEL // N_HEADS
        MASK_FILL = -100000000.0

        def _split_heads(x):
            B, S, _ = x.shape
            return x.reshape(B, S, N_HEADS, HEAD_DIM).transpose(0, 2, 1, 3)
        key = jax.random.key(seed)
        ks = jax.random.split(key, 12)
        B, L, P = (2, 256, 256)
        s = 1.0 / np.sqrt(D_MODEL).astype(np.float32)
        inp = {'q': jax.random.normal(ks[0], (B, L, D_MODEL), dtype=jnp.float32), 'k': jax.random.normal(ks[1], (B, P, D_MODEL), dtype=jnp.float32), 'v': jax.random.normal(ks[2], (B, P, D_MODEL), dtype=jnp.float32), 'attention_mask': jnp.ones((B, P), dtype=bool), 'Wq': jax.random.normal(ks[3], (D_MODEL, D_MODEL), dtype=jnp.float32) * s, 'bq': jnp.zeros((D_MODEL,), dtype=jnp.float32), 'Wk': jax.random.normal(ks[4], (D_MODEL, D_MODEL), dtype=jnp.float32) * s, 'bk': jnp.zeros((D_MODEL,), dtype=jnp.float32), 'Wv': jax.random.normal(ks[5], (D_MODEL, D_MODEL), dtype=jnp.float32) * s, 'bv': jnp.zeros((D_MODEL,), dtype=jnp.float32), 'Wo': jax.random.normal(ks[6], (D_MODEL, D_MODEL), dtype=jnp.float32) * s, 'bo': jnp.zeros((D_MODEL,), dtype=jnp.float32)}
        return inp
    _L1_xattn_all = _L1_xattn_setup()
    _L1_xattn_in = {k: v for k, v in _L1_xattn_all.items() if k in ('Wq', 'bq', 'Wk', 'bk', 'Wv', 'bv', 'Wo', 'bo')}
    del _L1_xattn_all

    def _L1_attn_setup():
        import jax, jax.numpy as jnp
        import numpy as np
        DIM = 128
        HEADS = 16
        EPS = 1e-12
        key = jax.random.key(seed)
        ks = jax.random.split(key, 6)
        b, n, dim, h = (2, 256, DIM, HEADS)
        x = jax.random.normal(ks[0], (b, n, dim), dtype=jnp.float32)
        w_qkv = jax.random.normal(ks[1], (3 * dim, dim), dtype=jnp.float32) / np.sqrt(dim)
        w_out = jax.random.normal(ks[2], (dim, dim), dtype=jnp.float32) / np.sqrt(dim)
        b_out = jax.random.normal(ks[3], (dim,), dtype=jnp.float32) * 0.02
        norm_g = jnp.ones((1, h, 1, 1), dtype=jnp.float32)
        norm_b = jnp.zeros((1, h, 1, 1), dtype=jnp.float32)
        return {'x': x, 'w_qkv': w_qkv, 'w_out': w_out, 'b_out': b_out, 'norm_g': norm_g, 'norm_b': norm_b}
    _L1_attn_all = _L1_attn_setup()
    _L1_attn_in = {k: v for k, v in _L1_attn_all.items() if k in ('w_qkv', 'w_out', 'b_out', 'norm_g', 'norm_b')}
    del _L1_attn_all

    def _L1_ffn_setup():
        import jax, jax.numpy as jnp
        import numpy as np
        B, S, H, E, DFF = (4, 512, 128, 8, 512)
        key = jax.random.key(seed)
        k0, k1, k2, k3 = jax.random.split(key, 4)
        hidden_states = jax.random.normal(k0, (B, S, H), dtype=jnp.float32)
        gate_w = jax.random.normal(k1, (E, H), dtype=jnp.float32) * 0.02
        w1 = jax.random.normal(k2, (E, H, DFF), dtype=jnp.float32) * 0.02
        b1 = jnp.zeros((E, DFF), dtype=jnp.float32)
        w2 = jax.random.normal(k3, (E, DFF, H), dtype=jnp.float32) * 0.02
        b2 = jnp.zeros((E, H), dtype=jnp.float32)
        return {'hidden_states': hidden_states, 'gate_w': gate_w, 'w1': w1, 'b1': b1, 'w2': w2, 'b2': b2}
    _L1_ffn_all = _L1_ffn_setup()
    _L1_ffn_in = {k: v for k, v in _L1_ffn_all.items() if k in ('gate_w', 'w1', 'b1', 'w2', 'b2')}
    del _L1_ffn_all
    return {'x': x, 'ctx_1024': ctx_1024, 'mask_BxS2_bf1': mask_BxS2_bf1, 'L0_xattn_Wq': _L0_xattn_in['Wq'], 'L0_xattn_bq': _L0_xattn_in['bq'], 'L0_xattn_Wk': _L0_xattn_in['Wk'], 'L0_xattn_bk': _L0_xattn_in['bk'], 'L0_xattn_Wv': _L0_xattn_in['Wv'], 'L0_xattn_bv': _L0_xattn_in['bv'], 'L0_xattn_Wo': _L0_xattn_in['Wo'], 'L0_xattn_bo': _L0_xattn_in['bo'], 'L0_attn_Wq': _L0_attn_in['Wq'], 'L0_attn_bq': _L0_attn_in['bq'], 'L0_attn_Wk': _L0_attn_in['Wk'], 'L0_attn_bk': _L0_attn_in['bk'], 'L0_attn_Wv': _L0_attn_in['Wv'], 'L0_attn_bv': _L0_attn_in['bv'], 'L0_attn_Wo': _L0_attn_in['Wo'], 'L0_attn_bo': _L0_attn_in['bo'], 'L0_ffn_wq': _L0_ffn_in['wq'], 'L0_ffn_wk': _L0_ffn_in['wk'], 'L0_ffn_wv': _L0_ffn_in['wv'], 'L0_ffn_wo': _L0_ffn_in['wo'], 'L0_ffn_w1': _L0_ffn_in['w1'], 'L0_ffn_w2': _L0_ffn_in['w2'], 'L0_ffn_w3': _L0_ffn_in['w3'], 'L0_ffn_attn_norm_w': _L0_ffn_in['attn_norm_w'], 'L0_ffn_ff_norm_w': _L0_ffn_in['ff_norm_w'], 'L0_ffn_moe_norm_w': _L0_ffn_in['moe_norm_w'], 'L0_ffn_router_w': _L0_ffn_in['router_w'], 'L0_ffn_ew1': _L0_ffn_in['ew1'], 'L0_ffn_ew2': _L0_ffn_in['ew2'], 'L0_ffn_ew3': _L0_ffn_in['ew3'], 'L1_xattn_Wq': _L1_xattn_in['Wq'], 'L1_xattn_bq': _L1_xattn_in['bq'], 'L1_xattn_Wk': _L1_xattn_in['Wk'], 'L1_xattn_bk': _L1_xattn_in['bk'], 'L1_xattn_Wv': _L1_xattn_in['Wv'], 'L1_xattn_bv': _L1_xattn_in['bv'], 'L1_xattn_Wo': _L1_xattn_in['Wo'], 'L1_xattn_bo': _L1_xattn_in['bo'], 'L1_attn_w_qkv': _L1_attn_in['w_qkv'], 'L1_attn_w_out': _L1_attn_in['w_out'], 'L1_attn_b_out': _L1_attn_in['b_out'], 'L1_attn_norm_g': _L1_attn_in['norm_g'], 'L1_attn_norm_b': _L1_attn_in['norm_b'], 'L1_ffn_gate_w': _L1_ffn_in['gate_w'], 'L1_ffn_w1': _L1_ffn_in['w1'], 'L1_ffn_b1': _L1_ffn_in['b1'], 'L1_ffn_w2': _L1_ffn_in['w2'], 'L1_ffn_b2': _L1_ffn_in['b2']}

def reference(x, ctx_1024, mask_BxS2_bf1, L0_xattn_Wq, L0_xattn_bq, L0_xattn_Wk, L0_xattn_bk, L0_xattn_Wv, L0_xattn_bv, L0_xattn_Wo, L0_xattn_bo, L0_attn_Wq, L0_attn_bq, L0_attn_Wk, L0_attn_bk, L0_attn_Wv, L0_attn_bv, L0_attn_Wo, L0_attn_bo, L0_ffn_wq, L0_ffn_wk, L0_ffn_wv, L0_ffn_wo, L0_ffn_w1, L0_ffn_w2, L0_ffn_w3, L0_ffn_attn_norm_w, L0_ffn_ff_norm_w, L0_ffn_moe_norm_w, L0_ffn_router_w, L0_ffn_ew1, L0_ffn_ew2, L0_ffn_ew3, L1_xattn_Wq, L1_xattn_bq, L1_xattn_Wk, L1_xattn_bk, L1_xattn_Wv, L1_xattn_bv, L1_xattn_Wo, L1_xattn_bo, L1_attn_w_qkv, L1_attn_w_out, L1_attn_b_out, L1_attn_norm_g, L1_attn_norm_b, L1_ffn_gate_w, L1_ffn_w1, L1_ffn_b1, L1_ffn_w2, L1_ffn_b2):
    import jax
    import jax.numpy as jnp

    def _L0_xattn_ref(x, content_embeddings, Wq, bq, Wk, bk, Wv, bv, Wo, bo):
        import jax, jax.numpy as jnp
        import numpy as np
        C = 128
        B, SQ, SKV = (4, 256, 256)
        queries = x @ Wq.T + bq
        keys = content_embeddings @ Wk.T + bk
        values = content_embeddings @ Wv.T + bv
        scale = 1.0 / jnp.sqrt(jnp.asarray(C, x.dtype))
        scores = jnp.einsum('bqc,bkc->bqk', queries, keys) * scale
        attn = jax.nn.softmax(scores, axis=-1)
        attended = jnp.einsum('bqk,bkc->bqc', attn, values)
        out = x + attended
        return out @ Wo.T + bo

    def _L0_attn_ref(x, Wq, bq, Wk, bk, Wv, bv, Wo, bo):
        import math
        import jax, jax.numpy as jnp
        import numpy as np
        N_HEAD = 16

        def _rope_cos_sin(l, head_dim):
            scale = jnp.arange(0, head_dim, 2, dtype=jnp.float32)[:head_dim // 2]
            freqs = 1.0 / 10000.0 ** scale
            angles = jnp.arange(l, dtype=jnp.float32)[:, None] * freqs[None, :]
            return (jnp.cos(angles), jnp.sin(angles))

        def _rope_apply(x, cos, sin):
            b, l, h, hd = x.shape
            xp = x.astype(jnp.float32).reshape(b, l, h, hd // 2, 2)
            xr, xi = (xp[..., 0], xp[..., 1])
            c = cos[None, :, None, :]
            s = sin[None, :, None, :]
            out_r = xr * c - xi * s
            out_i = xr * s + xi * c
            out = jnp.stack([out_r, out_i], axis=-1).reshape(b, l, h, hd)
            return out.astype(x.dtype)
        b, l, d = x.shape
        h = N_HEAD
        hd = d // h
        q = (x @ Wq + bq).reshape(b, l, h, hd)
        k = (x @ Wk + bk).reshape(b, l, h, hd)
        v = (x @ Wv + bv).reshape(b, l, h, hd)
        cos, sin = _rope_cos_sin(l, hd)
        q = _rope_apply(q, cos, sin)
        k = _rope_apply(k, cos, sin)
        score = jnp.einsum('blhd,bmhd->bhlm', q, k) / math.sqrt(hd)
        ctx = jnp.einsum('bhlm,bmhd->blhd', score, v).reshape(b, l, d)
        return ctx @ Wo + bo

    def _L0_ffn_ref(x, wq, wk, wv, wo, w1, w2, w3, attn_norm_w, ff_norm_w, moe_norm_w, router_w, ew1, ew2, ew3):
        import jax, jax.numpy as jnp
        import numpy as np
        D = 128
        H = 16
        FF = 512
        E = 8
        K = 2
        EH = 128
        B, S = (2, 256)
        EPS = 1e-05

        def rmsnorm(x, w):
            v = jnp.mean(jnp.square(x), axis=-1, keepdims=True)
            return x * jax.lax.rsqrt(v + EPS) * w

        def _dense_path(x, wq, wk, wv, wo, w1, w2, w3, attn_norm_w, ff_norm_w):
            b, s, d = x.shape
            hd = d // H
            q = (x @ wq).reshape(b, s, H, hd)
            k = (x @ wk).reshape(b, s, H, hd)
            v = (x @ wv).reshape(b, s, H, hd)
            scores = jnp.einsum('bqhd,bkhd->bhqk', q, k) / np.sqrt(hd).astype(np.float32)
            causal = jnp.tril(jnp.ones((s, s), bool))
            scores = jnp.where(causal, scores, jnp.finfo(scores.dtype).min)
            attn = jax.nn.softmax(scores, axis=-1)
            o = jnp.einsum('bhqk,bkhd->bqhd', attn, v).reshape(b, s, d)
            h = x + rmsnorm(o @ wo, attn_norm_w)
            ffn = jax.nn.silu(h @ w1) * (h @ w3) @ w2
            return h + rmsnorm(ffn, ff_norm_w)

        def _sparse_path(x, router_w, ew1, ew2, ew3, moe_norm_w):
            b, s, d = x.shape
            xt = x.reshape(-1, d)
            probs = jax.nn.softmax(xt @ router_w, axis=-1)
            topw, topi = jax.lax.top_k(probs, K)
            g = jax.nn.silu(jnp.einsum('td,edh->eth', xt, ew1)) * jnp.einsum('td,edh->eth', xt, ew3)
            eo = jnp.einsum('eth,ehd->ted', g, ew2)
            sel = jnp.take_along_axis(eo, topi[:, :, None], axis=1)
            moe_out = jnp.sum(topw[:, :, None] * sel, axis=1).reshape(b, s, d)
            return rmsnorm(moe_out, moe_norm_w)
        dense_out = _dense_path(x, wq, wk, wv, wo, w1, w2, w3, attn_norm_w, ff_norm_w)
        sparse_out = _sparse_path(x, router_w, ew1, ew2, ew3, moe_norm_w)
        return dense_out + sparse_out

    def _L1_xattn_ref(q, k, v, attention_mask, Wq, bq, Wk, bk, Wv, bv, Wo, bo):
        import jax, jax.numpy as jnp
        import numpy as np
        N_HEADS = 16
        D_MODEL = 128
        HEAD_DIM = D_MODEL // N_HEADS
        MASK_FILL = -100000000.0

        def _split_heads(x):
            B, S, _ = x.shape
            return x.reshape(B, S, N_HEADS, HEAD_DIM).transpose(0, 2, 1, 3)
        qm = _split_heads(q @ Wq.T + bq)
        km = _split_heads(k @ Wk.T + bk)
        vm = _split_heads(v @ Wv.T + bv)
        scores = jnp.einsum('bnlh,bnph->bnlp', qm, km) / np.sqrt(HEAD_DIM).astype(np.float32)
        mask = attention_mask[:, None, None, :]
        scores = jnp.where(mask, scores, MASK_FILL)
        attn = jax.nn.softmax(scores, axis=-1)
        out = jnp.einsum('bnlp,bnph->bnlh', attn, vm)
        B, _, L, _ = out.shape
        out = out.transpose(0, 2, 1, 3).reshape(B, L, D_MODEL)
        return out @ Wo.T + bo

    def _L1_attn_ref(x, w_qkv, w_out, b_out, norm_g, norm_b):
        import jax, jax.numpy as jnp
        import numpy as np
        DIM = 128
        HEADS = 16
        EPS = 1e-12
        b, n, dim = x.shape
        h = HEADS
        d = dim // h
        qkv = jnp.einsum('bnm,om->bno', x, w_qkv)
        qkv = qkv.reshape(b, n, 3, h, d)
        q, k, v = [jnp.transpose(qkv[:, :, i], (0, 2, 1, 3)) for i in range(3)]
        dots = jnp.einsum('bhid,bhjd->bhij', q, k)
        norm = jnp.sqrt(jnp.sum(dots * dots, axis=-1, keepdims=True))
        attn = dots / jnp.maximum(norm, EPS) * norm_g + norm_b
        out = jnp.einsum('bhij,bhjd->bhid', attn, v)
        out = jnp.transpose(out, (0, 2, 1, 3)).reshape(b, n, dim)
        return jnp.einsum('bnm,om->bno', out, w_out) + b_out

    def _L1_ffn_ref(hidden_states, gate_w, w1, b1, w2, b2):
        import jax, jax.numpy as jnp
        import numpy as np
        B, S, H, E, DFF = (4, 512, 128, 8, 512)
        b, s, h = hidden_states.shape
        x = hidden_states.reshape(-1, h)
        gate_logits = x @ gate_w.T
        gate_probs = jax.nn.softmax(gate_logits, axis=-1)
        expert_idx = jnp.argmax(gate_probs, axis=-1)
        expert_w = jnp.take_along_axis(gate_probs, expert_idx[:, None], axis=1)[:, 0]
        out = jnp.zeros_like(x)
        n_experts = w1.shape[0]
        for e in range(n_experts):
            ye = jax.nn.relu(x @ w1[e] + b1[e]) @ w2[e] + b2[e]
            sel = (expert_idx == e)[:, None]
            out = out + jnp.where(sel, ye * expert_w[:, None], 0.0)
        return out.reshape(b, s, h)
    x = x + _L0_xattn_ref(_layernorm(x, axis=-1), ctx_1024, L0_xattn_Wq, L0_xattn_bq, L0_xattn_Wk, L0_xattn_bk, L0_xattn_Wv, L0_xattn_bv, L0_xattn_Wo, L0_xattn_bo)
    x = x + _L0_attn_ref(_layernorm(x, axis=-1), L0_attn_Wq, L0_attn_bq, L0_attn_Wk, L0_attn_bk, L0_attn_Wv, L0_attn_bv, L0_attn_Wo, L0_attn_bo)
    x = x + _L0_ffn_ref(_layernorm(x, axis=-1), L0_ffn_wq, L0_ffn_wk, L0_ffn_wv, L0_ffn_wo, L0_ffn_w1, L0_ffn_w2, L0_ffn_w3, L0_ffn_attn_norm_w, L0_ffn_ff_norm_w, L0_ffn_moe_norm_w, L0_ffn_router_w, L0_ffn_ew1, L0_ffn_ew2, L0_ffn_ew3)
    x = x + _L1_xattn_ref(_layernorm(x, axis=-1), ctx_1024, ctx_1024, mask_BxS2_bf1, L1_xattn_Wq, L1_xattn_bq, L1_xattn_Wk, L1_xattn_bk, L1_xattn_Wv, L1_xattn_bv, L1_xattn_Wo, L1_xattn_bo)
    x = x + _L1_attn_ref(_layernorm(x, axis=-1), L1_attn_w_qkv, L1_attn_w_out, L1_attn_b_out, L1_attn_norm_g, L1_attn_norm_b)
    x = x + _L1_ffn_ref(_layernorm(x, axis=-1), L1_ffn_gate_w, L1_ffn_w1, L1_ffn_b1, L1_ffn_w2, L1_ffn_b2)
    return x

_drawn_inputs = setup_inputs


def setup_inputs(seed=0):
    import zlib

    import numpy as np

    out = dict(_drawn_inputs(seed))
    spreads = {'L0_xattn_bq': (0.0, 0.1),
     'L0_xattn_bk': (0.0, 2.0),
     'L0_xattn_bv': (0.0, 0.1),
     'L0_xattn_bo': (0.0, 0.1),
     'L0_attn_bq': (0.0, 0.1),
     'L0_attn_bk': (0.0, 0.1),
     'L0_attn_bv': (0.0, 0.1),
     'L0_attn_bo': (0.0, 0.8),
     'L0_ffn_attn_norm_w': (1.0, 0.6),
     'L0_ffn_ff_norm_w': (1.0, 0.6),
     'L0_ffn_moe_norm_w': (1.0, 0.6),
     'L1_xattn_bq': (0.0, 0.8),
     'L1_xattn_bk': (0.0, 2.0),
     'L1_xattn_bv': (0.0, 0.8),
     'L1_xattn_bo': (0.0, 0.8),
     'L1_attn_norm_g': (1.0, 0.2),
     'L1_attn_norm_b': (0.0, 0.1),
     'L1_ffn_b1': (0.0, 0.8),
     'L1_ffn_b2': (0.0, 0.8)}
    factors = {'L0_ffn_wq': 8.0,
     'L0_ffn_wk': 8.0,
     'L1_xattn_Wq': 3.734,
     'L1_xattn_Wk': 3.622,
     'L1_attn_b_out': 27.711,
     'L1_ffn_gate_w': 8.0,
     'L1_ffn_w1': 8.0,
     'L1_ffn_w2': 8.0}
    for name, (base, spread) in spreads.items():
        noise = np.random.default_rng([zlib.crc32(name.encode()), seed]).standard_normal(out[name].shape)
        drawn = base * np.exp(spread * noise) if base else spread * noise
        out[name] = jnp.asarray(drawn.astype(out[name].dtype))
    for name, factor in factors.items():
        out[name] = (out[name] * factor).astype(out[name].dtype)
    return out
```

```python
from contextlib import ExitStack

import numpy as np

import concourse.bass as bass
from concourse import mybir

F32 = mybir.dt.float32
F32R = mybir.dt.float32r
BF16 = mybir.dt.bfloat16
U8 = mybir.dt.uint8
ALU = mybir.AluOpType
ACT = mybir.ActivationFunctionType
X = mybir.AxisListType.X

P = 128
B, S, D = 32, 64, 128
N_CTX = 1601
NT = B * S // P
NCH = (N_CTX + P - 1) // P
FULL = NCH - 1
TAIL = N_CTX - FULL * P
H, HD = 16, 8
LN_EPS = 1e-5
RMS_EPS = 1e-5
CAUSAL_FILL = -1e30
ROWS = [P] * FULL + [TAIL]
GROUPS = [list(range(i, min(i + 4, NCH))) for i in range(0, NCH, 4)]


class Tally:

    def __init__(self, sem):
        self.sem, self.base, self.n, self.it, self.per = sem, 0, 0, None, 0

    def next(self, k=1):
        self.n += k
        return self.value()

    def value(self):
        return self.base + self.n if self.it is None else self.it * self.per + (self.base + self.n)

    def enter(self, it, per):
        self.base, self.n, self.it, self.per = self.base + self.n, 0, it, per

    def leave(self, times):
        assert self.n == self.per, (self.n, self.per)
        self.base, self.n, self.it = self.base + self.per * times, 0, None


def wait_apart(eng, constant, waits):
    waits = [(sem, value if isinstance(value, int) else eng.to_reg(value)) for sem, value in waits]
    eng.wait_ge(*constant)
    for sem, value in waits:
        eng.wait_ge(sem, value)


class Memory:

    def __init__(self, nc, stack, prefix):
        self.nc, self.stack, self.prefix = nc, stack, prefix

    def sb(self, name, shape, dt=F32):
        return self.stack.enter_context(self.nc.sbuf_tensor(f"{self.prefix}_{name}", shape, dt))

    def psum(self, name, shape, dt=F32):
        return self.stack.enter_context(self.nc.psum_tensor(f"{self.prefix}_{name}", shape, dt))

    def sem(self, name):
        return self.stack.enter_context(self.nc.semaphore(f"{self.prefix}_{name}"))


def over(ap, n):
    return ap.unsqueeze(2).broadcast_to([ap.shape[0], ap.shape[1], n])


def under(ap, n):
    return ap.unsqueeze(1).broadcast_to([ap.shape[0], n, ap.shape[1]])


class Norm:

    def __init__(self, m, name="ln"):
        self.xn = m.sb(name + "_xn", [P, NT, D])
        self.sq = m.sb(name + "_sq", [P, NT, D])
        self.mean = m.sb(name + "_mean", [P, NT])
        self.var = m.sb(name + "_var", [P, NT])
        self.std = m.sb(name + "_std", [P, NT])
        self.rstd = m.sb(name + "_rstd", [P, NT])
        self.var_ready = m.sem(name + "_var_ready")
        self.std_ready = m.sem(name + "_std_ready")
        self.ready = m.sem(name + "_ready")


def norm_vector(dve, nm, x, chain):
    def step(ins):
        ins.then_inc(chain.sem, 1)
        dve.wait_ge(chain.sem, chain.next())

    step(dve.tensor_reduce(nm.mean[:, :], x[:, :, :], X, ALU.add))
    step(dve.tensor_scalar(nm.mean[:, :], nm.mean[:, :], 1.0 / D, None, ALU.mult))
    step(dve.tensor_tensor(nm.xn[:, :, :], x[:, :, :], over(nm.mean[:, :], D), ALU.subtract))
    step(dve.tensor_tensor(nm.sq[:, :, :], nm.xn[:, :, :], nm.xn[:, :, :], ALU.mult))
    step(dve.tensor_reduce(nm.var[:, :], nm.sq[:, :, :], X, ALU.add))
    dve.tensor_scalar(nm.var[:, :], nm.var[:, :], 1.0 / D, LN_EPS, ALU.mult, ALU.add).then_inc(nm.var_ready, 1)
    dve.wait_ge(nm.std_ready, 1)
    step(dve.reciprocal(nm.rstd[:, :], nm.std[:, :]))
    dve.tensor_tensor(nm.xn[:, :, :], nm.xn[:, :, :], over(nm.rstd[:, :], D), ALU.mult).then_inc(nm.ready, 1)


def norm_scalar(act, nm):
    act.wait_ge(nm.var_ready, 1)
    act.activation(nm.std[:, :], nm.var[:, :], ACT.Sqrt).then_inc(nm.std_ready, 1)


def load_ctx(eng, dst, src, sem):
    eng.dma_start(dst[:, 0:FULL, :], src[0:FULL * P, :].rearrange("(p j) c -> p j c", j=FULL)).then_inc(sem, 16)
    eng.dma_start(dst[0:TAIL, FULL, :], src[FULL * P:N_CTX, :]).then_inc(sem, 16)


def cross_attention_0(nc, io, x_tok, ident):
    NG = NT // 4
    with ExitStack() as stack:
        m = Memory(nc, stack, "xa0")
        wq, wk, wv, wo = (m.sb(n, [P, D]) for n in ("wqT", "wk", "wvT", "woT"))
        bq, bk, bv = (m.sb(n, [P, 1]) for n in ("bq", "bk", "bv"))
        bo = m.sb("bo", [P, D])
        nm = Norm(m)
        xnT = m.sb("xnT", [P, NT * P])
        qT = m.sb("qT", [P, NT * P])
        fT = m.sb("fT", [P, NT * P])
        q_bk = m.sb("q_bk", [P, NT])
        ctx = [m.sb(f"ctx{u}", [P, 2, NCH, D]) for u in range(2)]
        ctxT = m.sb("ctxT", [P, 2, N_CTX])
        fold = [m.sb(f"fold{u}", [P, P]) for u in range(2)]
        prob = m.sb("prob", [P, N_CTX])
        probT = m.sb("probT", [P, NCH, P])
        top = m.sb("top", [P, 1])
        shifted = m.sb("shifted", [P, 1])
        shift = m.sb("shift", [P, 1])
        total = m.sb("total", [P, 1])
        inv = m.sb("inv", [P, 1])
        att = m.sb("att", [P, NT, D])

        ps_s = m.psum("ps_s", [P, 4, 512])
        ps_t = m.psum("ps_t", [P, 2, 512])
        ps_o = m.psum("ps_o", [P, 512])
        ps_b = m.psum("ps_b", [P, 512])

        weights = m.sem("weights")
        ctx_loaded = [m.sem(f"ctx_loaded{u}") for u in range(2)]
        chain = m.sem("vector_chain")
        turn_full = [m.sem(f"turn_full{i}") for i in range(2)]
        turn_free = [m.sem(f"turn_free{i}") for i in range(2)]
        q_bk_full = m.sem("q_bk_full")
        q_bk_ready = m.sem("q_bk_ready")
        fold_ready = m.sem("fold_ready")
        scores_full = m.sem("scores_full")
        shift_ready = m.sem("shift_ready")
        prob_ready = m.sem("prob_ready")
        attended = m.sem("attended")
        att_ready = m.sem("att_ready")
        bias_added = m.sem("bias_added")
        mask_tail_cleared = m.sem("mask_tail_cleared")
        block = stack.enter_context(nc.Block())
        PAIR_TURNS = 3 * len(GROUPS)

        @block.sync
        def _(sp):
            for dst, src in ((wq, "L0_xattn_WqT"), (wk, "L0_xattn_Wk"), (wv, "L0_xattn_WvT"), (wo, "L0_xattn_WoT")):
                sp.dma_start(dst[:, :], io[src]).then_inc(weights, 16)
            for dst, src in ((bq, "L0_xattn_bq"), (bk, "L0_xattn_bk"), (bv, "L0_xattn_bv")):
                sp.dma_start(dst[:, :], io[src].rearrange("(p a) -> p a", a=1)).then_inc(weights, 16)
            sp.dma_start(bo[:, :], io["L0_xattn_bo"].rearrange("(a n) -> a n", a=1).broadcast_to([P, D])).then_inc(weights, 16)
            for u in range(2):
                for b in range(2):
                    load_ctx(sp, ctx[u][:, b], io["ctx_1024"][2 * u + b], ctx_loaded[u])
            with sp.Fori(0, NT // 2 - 1) as it:
                for u in range(2):
                    sp.wait_ge(attended, it * 2 + (u + 1))
                    for b in range(2):
                        load_ctx(sp, ctx[u][:, b], io["ctx_1024"][bass.ds(it * 4 + (4 + 2 * u + b), 1)].rearrange("a t c -> (a t) c"),
                                 ctx_loaded[u])

        @block.gpsimd
        def _(pool):
            pool.wait_ge(turn_free[0], 6)
            pool.wait_ge(turn_free[1], 6)
            for u in range(2):
                pool.tensor_copy(fold[u][:, :], fT[:, u * P:(u + 1) * P]).then_inc(fold_ready, 1)
            with pool.Fori(0, NT // 2 - 1) as it:
                for u in range(2):
                    pool.wait_ge(scores_full, it * 2 + (u + 1))
                    pool.tensor_copy(fold[u][:, :], fT[:, bass.ds(it * (2 * P) + (2 + u) * P, P)]).then_inc(fold_ready, 1)
            pool.wait_ge(nm.ready, 1)
            pool.wait_ge(weights, 16 * 8)
            pool.tensor_tensor(x_tok[:, :, :], x_tok[:, :, :], under(bo[:, :], NT), ALU.add).then_inc(bias_added, 1)

        class Turns:

            def __init__(self):
                self.k = 0
                self.free = [Tally(s) for s in turn_free]

            def enter(self, it, per):
                for t in self.free:
                    t.enter(it, per // 2)

            def leave(self, times):
                for t in self.free:
                    t.leave(times)

        @block.tensor
        def _(pe):
            t = Turns()

            def turn(fill):
                i = t.k % 2
                if t.k >= 2:
                    pe.wait_ge(turn_free[i], t.free[i].value())
                t.free[i].next()
                fill(ps_t[:, i, :]).then_inc(turn_full[i], 1)
                t.k += 1

            def transposes(src):
                def fill(bank):
                    for c in range(4):
                        last = pe.transpose(bank[:, c * P:(c + 1) * P], src(c), ident[:, :])
                    return last
                return fill

            def project(w, src):
                return lambda bank: pe.matmul(bank, w[:, :], src, start=True, stop=True)

            pe.wait_ge(nm.ready, 1)
            for g in range(NG):
                turn(transposes(lambda c: nm.xn[:, 4 * g + c, :]))
            pe.wait_ge(weights, 16 * 8)
            for g in range(NG):
                pe.wait_ge(turn_free[g % 2], g // 2 + 1)
                turn(project(wq, xnT[:, g * 512:(g + 1) * 512]))
            for g in range(NG):
                pe.wait_ge(turn_free[g % 2], 2 + g // 2 + 1)
                turn(project(wk, qT[:, g * 512:(g + 1) * 512]))
            for n in range(NT):
                last = pe.matmul(ps_b[:, n:n + 1], qT[:, n * P:(n + 1) * P], bk[:, :], start=True, stop=True)
            last.then_inc(q_bk_full, 1)

            loaded = [Tally(s) for s in ctx_loaded]
            folded = Tally(fold_ready)
            done_p = Tally(prob_ready)
            with pe.Fori(0, NT // 2) as it:
                t.enter(it, 2 * PAIR_TURNS)
                folded.enter(it, 2)
                done_p.enter(it, 2)
                for u in range(2):
                    loaded[u].enter(it, 64)
                    pe.wait_ge(ctx_loaded[u], loaded[u].next(64))
                    for b in range(2):
                        for chunks in GROUPS:
                            def fill(bank):
                                for j in chunks:
                                    r = ROWS[j]
                                    last = pe.transpose(bank[:, (j % 4) * P:(j % 4) * P + r],
                                                        ctx[u][0:r, b, j, :], ident[0:r, 0:r])
                                return last
                            turn(fill)
                    for i in range(2):
                        pe.wait_ge(turn_free[i], t.free[i].value())
                    pe.wait_ge(fold_ready, folded.next())
                    for c in range(0, N_CTX, 512):
                        w = min(512, N_CTX - c)
                        for b in range(2):
                            last = pe.matmul(ps_s[64 * b:64 * b + 64, c // 512, 0:w], fold[u][:, 64 * b:64 * b + 64],
                                             ctxT[:, b, c:c + w], start=True, stop=True)
                    last.then_inc(scores_full, 1)
                    pe.wait_ge(prob_ready, done_p.next())
                    for chunks in GROUPS:
                        def fill(bank):
                            for j in chunks:
                                r = ROWS[j]
                                c0 = chunks[0] * P + (j % 4) * P
                                last = pe.transpose(bank[0:r, (j % 4) * P:(j % 4 + 1) * P],
                                                    prob[:, c0:c0 + r], ident[:, :])
                            return last
                        turn(fill)
                    for i in range(2):
                        pe.wait_ge(turn_free[i], t.free[i].value())
                    for j in range(NCH):
                        r = ROWS[j]
                        for b in range(2):
                            last = pe.matmul(ps_o[64 * b:64 * b + 64, 0:D], probT[0:r, j, 64 * b:64 * b + 64],
                                             ctx[u][0:r, b, j, :], start=(j == 0), stop=(j == NCH - 1))
                    last.then_inc(attended, 1)
                    loaded[u].leave(NT // 2)
                t.leave(NT // 2)
                folded.leave(NT // 2)
                done_p.leave(NT // 2)

            pe.wait_ge(att_ready, NT)
            base = [t.free[i].value() for i in range(2)]
            for g in range(NG):
                turn(transposes(lambda c: att[:, 4 * g + c, :]))
            for g in range(NG):
                pe.wait_ge(turn_free[g % 2], base[g % 2] + g // 2 + 1)
                cols = slice(g * 512, (g + 1) * 512)

                def fill(bank):
                    pe.matmul(bank, wv[:, :], fT[:, cols], start=True, stop=False)
                    return pe.matmul(bank, ident[:, :], xnT[:, cols], start=False, stop=True)
                turn(fill)
            pe.wait_ge(bias_added, 1)
            for g in range(NG):
                pe.wait_ge(turn_free[g % 2], base[g % 2] + 2 + g // 2 + 1)

                def fill(bank):
                    pe.matmul(bank, ident[:, :], x_tok[:, 4 * g:4 * g + 4, :].rearrange("p n d -> p (n d)"),
                              start=True, stop=False, skip_group_check=True)
                    for c in range(4):
                        n = 4 * g + c
                        last = pe.matmul(bank[:, c * P:(c + 1) * P], qT[:, n * P:(n + 1) * P], wo[:, :],
                                         start=False, stop=(c == 3), skip_group_check=True)
                    return last
                turn(fill)

        def empty(eng, t, i, out_of):
            eng.wait_ge(turn_full[i], t.next())
            out_of(ps_t[:, i, :]).then_inc(turn_free[i], 1)

        def common(eng, i, copy, add, mid_q, mid_pair, finish):
            full = Tally(turn_full[i])
            for g in range(i, NG, 2):
                empty(eng, full, i, lambda bank: copy(xnT[:, g * 512:(g + 1) * 512], bank))
            eng.wait_ge(weights, 16 * 8)
            for g in range(i, NG, 2):
                empty(eng, full, i, lambda bank: add(qT[:, g * 512:(g + 1) * 512], bank, bq))
            for g in range(i, NG, 2):
                empty(eng, full, i, lambda bank: copy(fT[:, g * 512:(g + 1) * 512], bank))
            mid_q()
            with eng.Fori(0, NT // 2) as it:
                full.enter(it, PAIR_TURNS)
                for u in range(2):
                    k = 0
                    for b in range(2):
                        for chunks in GROUPS:
                            c0 = chunks[0] * P
                            w = sum(ROWS[j] for j in chunks)
                            if k % 2 == i:
                                empty(eng, full, i, lambda bank: copy(ctxT[:, b, c0:c0 + w], bank[:, 0:w]))
                            k += 1
                    mid_pair(it, u)
                    for chunks in GROUPS:
                        r = ROWS[chunks[0]]
                        w = len(chunks)
                        if k % 2 == i:
                            empty(eng, full, i, lambda bank: copy(probT[0:r, chunks[0]:chunks[0] + w, :],
                                                                  bank[0:r, 0:w * P].rearrange("p (j q) -> p j q", j=w)))
                        k += 1
                    finish(it, u)
                full.leave(NT // 2)
            for g in range(i, NG, 2):
                empty(eng, full, i, lambda bank: copy(fT[:, g * 512:(g + 1) * 512], bank))
            for g in range(i, NG, 2):
                empty(eng, full, i, lambda bank: add(qT[:, g * 512:(g + 1) * 512], bank, bv))
            for g in range(i, NG, 2):
                empty(eng, full, i, lambda bank: copy(x_tok[:, 4 * g:4 * g + 4, :].rearrange("p n d -> p (n d)"), bank))

        @block.scalar
        def _(act):
            norm_scalar(act, nm)

            def copy(dst, src):
                return act.activation(dst, src, ACT.Copy)

            def add(dst, src, bias):
                return act.activation(dst, src, ACT.Identity, bias=bias[:, 0:1])

            def mid_pair(it, u):
                act.wait_ge(shift_ready, it * 2 + (u + 1))
                act.activation(prob[:, :], ps_s[:, :, :].rearrange("p a b -> p (a b)")[:, 0:N_CTX], ACT.Exp,
                               bias=shift[:, 0:1], scale=float(D) ** -0.5,
                               accum_out=total[:, 0:1]).then_inc(prob_ready, 1)

            common(act, 1, copy, add, lambda: None, mid_pair, lambda it, u: None)

        @block.vector
        def _(dve):
            link = Tally(chain)

            def step(ins):
                ins.then_inc(chain, 1)
                dve.wait_ge(chain, link.next())

            norm_vector(dve, nm, x_tok, link)

            def copy(dst, src):
                return dve.tensor_copy(dst, src)

            def add(dst, src, bias):
                return dve.tensor_scalar(dst, src, bias[:, 0:1], None, ALU.add)

            def mid_q():
                dve.wait_ge(q_bk_full, 1)
                dve.tensor_copy(q_bk[:, :], ps_b[:, 0:NT]).then_inc(q_bk_ready, 1)
                dve.wait_ge(q_bk_ready, 1)

            def mid_pair(it, u):
                dve.wait_ge(scores_full, it * 2 + (u + 1))
                if u == 0:
                    link.enter(it, 8)
                n = it * 2 + u
                step(dve.tensor_reduce(top[:, :], ps_s[:, :, :].rearrange("p a b -> p (a b)")[:, 0:N_CTX], X, ALU.max))
                step(dve.tensor_tensor(shifted[:, :], top[:, :], q_bk[:, bass.ds(n, 1)], ALU.add))
                step(dve.tensor_tensor(shift[:, :], q_bk[:, bass.ds(n, 1)], shifted[:, :], ALU.subtract))
                dve.tensor_scalar(shift[:, :], shift[:, :], float(D) ** -0.5, None, ALU.mult).then_inc(shift_ready, 1)

            def finish(it, u):
                n = it * 2 + u
                dve.wait_ge(attended, it * 2 + (u + 1))
                step(dve.reciprocal(inv[:, :], total[:, :]))
                dve.tensor_scalar(att[:, bass.ds(n, 1), :].rearrange("p a d -> p (a d)"), ps_o[:, 0:D], inv[:, 0:1], None,
                                  ALU.mult).then_inc(att_ready, 1)
                if u == 1:
                    link.leave(NT // 2)

            common(dve, 0, copy, add, mid_q, mid_pair, finish)


NG = 4
GT = NT // NG
GB = 2 * GT
GC = GT * P


def flat(ap):
    return ap.rearrange("p a b -> p (a b)")


class Lane:

    def __init__(self, m, name, banks=2):
        self.banks = banks
        self.ps = m.psum(name, [P, banks, 512])
        self.full = m.sem(name + "_full")
        self.free = m.sem(name + "_free")


class Fill:

    def __init__(self, pe, lane):
        self.pe, self.lane, self.k, self.t = pe, lane, 0, Tally(lane.free)

    def __call__(self, matmuls):
        self.pe.wait_ge(self.lane.free, self.t.next())
        matmuls(self.lane.ps[:, self.k % self.lane.banks, :]).then_inc(self.lane.full, 1)
        self.k += 1

    def wait_emptied(self):
        self.pe.wait_ge(self.lane.free, self.t.value() + self.lane.banks)

    def enter(self, it, per):
        assert per % self.lane.banks == 0
        self.t.enter(it, per)

    def leave(self, times):
        self.t.leave(times)


class Take:

    def __init__(self, eng, lane):
        self.eng, self.lane, self.k, self.t = eng, lane, 0, Tally(lane.full)

    def __call__(self, out_of):
        self.eng.wait_ge(self.lane.full, self.t.next())
        out_of(self.lane.ps[:, self.k % self.lane.banks, :]).then_inc(self.lane.free, 1)
        self.k += 1

    def wait_taken(self):
        self.eng.wait_ge(self.lane.free, self.t.value() + self.lane.banks)

    def enter(self, it, per):
        self.t.enter(it, per)

    def leave(self, times):
        self.t.leave(times)


class Chain:

    def __init__(self, eng, sem):
        self.eng, self.sem, self.t = eng, sem, Tally(sem)

    def __call__(self, ins):
        ins.then_inc(self.sem, 1)
        self.eng.wait_ge(self.sem, self.t.next())

    def enter(self, it, per):
        self.t.enter(it, per)

    def leave(self, times):
        self.t.leave(times)


class GroupNorm:

    def __init__(self, m):
        self.xn = m.sb("xn", [P, GT, D])
        self.sq = m.sb("xn_sq", [P, GT, D])
        self.mean, self.var, self.std, self.rstd = (m.sb("ln_" + n, [P, GT]) for n in ("mean", "var", "std", "rstd"))
        self.var_ready, self.std_ready, self.ready = (m.sem("ln_" + n) for n in ("var_ready", "std_ready", "ready"))

    STEPS = 6

    def vector(self, dve, x, step, it):
        step(dve.tensor_reduce(self.mean[:, :], x, X, ALU.add))
        step(dve.tensor_scalar(self.mean[:, :], self.mean[:, :], 1.0 / D, None, ALU.mult))
        step(dve.tensor_tensor(self.xn[:, :, :], x, over(self.mean[:, :], D), ALU.subtract))
        step(dve.tensor_tensor(self.sq[:, :, :], self.xn[:, :, :], self.xn[:, :, :], ALU.mult))
        step(dve.tensor_reduce(self.var[:, :], self.sq[:, :, :], X, ALU.add))
        dve.tensor_scalar(self.var[:, :], self.var[:, :], 1.0 / D, LN_EPS, ALU.mult, ALU.add).then_inc(self.var_ready, 1)
        dve.wait_ge(self.std_ready, it + 1)
        step(dve.reciprocal(self.rstd[:, :], self.std[:, :]))
        dve.tensor_tensor(self.xn[:, :, :], self.xn[:, :, :], over(self.rstd[:, :], D), ALU.mult).then_inc(self.ready, 1)

    def scalar(self, act, it):
        act.wait_ge(self.var_ready, it + 1)
        act.activation(self.std[:, :], self.var[:, :], ACT.Sqrt).then_inc(self.std_ready, 1)


def load_row(eng, dst, src, sem):
    eng.dma_start(dst, src.rearrange("(a n) -> a n", a=1).broadcast_to([P, src.shape[0]])).then_inc(sem, 16)


def linear_attention_0(nc, io, x_tok, ident):
    with ExitStack() as stack:
        m = Memory(nc, stack, "la0")
        wqkv = m.sb("wqkv", [P, 3, D])
        bqkv = m.sb("bqkv", [P, 3, D])
        wo = m.sb("wo", [P, D])
        bo = m.sb("bo", [P, D])
        rope = m.sb("rope", [P, 2, HD])
        own = m.sb("own", [P, D])
        nm = GroupNorm(m)
        xb = m.sb("xb", [P, GT, D])
        xnT = m.sb("xnT", [P, GC])
        qkv = m.sb("qkv", [P, GT, 3 * D])
        cross = m.sb("cross", [P, GT, 2 * D])
        rot = m.sb("rot", [P, GT, 2 * D])
        qT = m.sb("qT", [P, GC])
        kv = m.sb("kv", [P, 2, GT, D])
        ctxT = m.sb("ctxT", [P, GC])
        scratch = m.sb("scratch", [P, 2])
        vl = Lane(m, "vector_lane")
        sl = Lane(m, "scalar_lane")
        consts = m.sem("consts")
        chain = m.sem("vector_chain")
        xb_ready = m.sem("xb_ready")
        rotated = m.sem("rotated")
        block = stack.enter_context(nc.Block())
        N_CONSTS = 10

        def group(it):
            return x_tok[:, bass.ds(it * GT, GT), :]

        @block.sync
        def _(sp):
            for i, n in enumerate("qkv"):
                sp.dma_start(wqkv[:, i, :], io["L0_attn_W" + n]).then_inc(consts, 16)
                load_row(sp, bqkv[:, i, :], io["L0_attn_b" + n], consts)
            sp.dma_start(wo[:, :], io["L0_attn_Wo"]).then_inc(consts, 16)
            load_row(sp, bo[:, :], io["L0_attn_bo"], consts)
            sp.dma_start(rope[:, :, :], io["rope"]).then_inc(consts, 16)
            sp.dma_start(own[:, :], io["own_head_scaled"]).then_inc(consts, 16)

        @block.gpsimd
        def _(pool):
            pool.wait_ge(consts, 16 * N_CONSTS)
            pool.tensor_tensor(xb[:, :, :], x_tok[:, 0:GT, :], under(bo[:, :], GT), ALU.add).then_inc(xb_ready, 1)
            with pool.Fori(0, NG - 1) as it:
                pool.wait_ge(sl.free, it * 4 + (4 + sl.banks))
                pool.tensor_tensor(xb[:, :, :], group(it + 1), under(bo[:, :], GT), ALU.add).then_inc(xb_ready, 1)

        @block.tensor
        def _(pe):
            v, s = Fill(pe, vl), Fill(pe, sl)
            pe.wait_ge(consts, 16 * N_CONSTS)
            with pe.Fori(0, NG) as it:
                v.enter(it, GT + 2)
                s.enter(it, 4)
                pe.wait_ge(nm.ready, it + 1)

                def turn(src):
                    def fill(bank):
                        for c in range(GT):
                            last = pe.transpose(bank[:, c * P:(c + 1) * P], src(c), ident[:, :])
                        return last
                    return fill

                s(turn(lambda c: nm.xn[:, c, :]))
                s.wait_emptied()
                for c in range(GT):
                    v(lambda bank: pe.matmul(bank[:, 0:3 * D], xnT[:, c * P:(c + 1) * P], flat(wqkv[:, :, :]),
                                             start=True, stop=True))
                pe.wait_ge(rotated, it + 1)
                s(turn(lambda c: rot[:, c, 0:D]))
                for u in range(2):
                    def fill(bank):
                        for c in range(GT):
                            rows = slice(64 * u, 64 * u + 64)
                            last = pe.matmul(bank[:, c * D:(c + 1) * D], rot[rows, c, D:2 * D], qkv[rows, c, 2 * D:3 * D],
                                             start=True, stop=True)
                        return last
                    v(fill)
                s.wait_emptied()
                v.wait_emptied()

                def fill(bank):
                    for c in range(GT):
                        for u in range(2):
                            t0 = c * P + 64 * u
                            last = pe.matmul(bank[:, t0:t0 + 64], kv[:, u, c, :], qT[:, t0:t0 + 64], start=True, stop=True)
                    return last
                s(fill)
                s.wait_emptied()
                pe.wait_ge(xb_ready, it + 1)

                def fill(bank):
                    pe.matmul(bank, ident[:, :], flat(xb[:, :, :]), start=True, stop=False, skip_group_check=True)
                    for c in range(GT):
                        last = pe.matmul(bank[:, c * D:(c + 1) * D], ctxT[:, c * P:(c + 1) * P], wo[:, :],
                                         start=False, stop=(c == GT - 1), skip_group_check=True)
                    return last
                s(fill)
                v.leave(NG)
                s.leave(NG)

        @block.scalar
        def _(act):
            take = Take(act, sl)
            act.wait_ge(consts, 16 * N_CONSTS)
            for _ in range(sl.banks):
                act.activation(scratch[:, 0:1], ident[:, 0:1], ACT.Copy).then_inc(sl.free, 1)
                act.wait_ge(sl.free, _ + 1)
            with act.Fori(0, NG) as it:
                take.enter(it, 4)
                nm.scalar(act, it)
                take(lambda bank: act.activation(xnT[:, :], bank, ACT.Copy))
                take(lambda bank: act.activation(qT[:, :], bank, ACT.Copy))
                take(lambda bank: act.activation(ctxT[:, :], bank, ACT.Copy))
                take(lambda bank: act.activation(group(it), bank.rearrange("p (c d) -> p c d", c=GT), ACT.Copy))
                take.leave(NG)

        @block.vector
        def _(dve):
            take, step = Take(dve, vl), Chain(dve, chain)
            for _ in range(vl.banks):
                dve.memset(scratch[:, 1:2], 0.0).then_inc(vl.free, 1)
                dve.wait_ge(vl.free, _ + 1)
            dve.wait_ge(consts, 16 * N_CONSTS)
            with dve.Fori(0, NG) as it:
                step.enter(it, nm.STEPS + 3)
                take.enter(it, GT + 2)
                nm.vector(dve, group(it), step, it)
                for c in range(GT):
                    take(lambda bank: dve.tensor_tensor(qkv[:, c, :], bank[:, 0:3 * D], flat(bqkv[:, :, :]), ALU.add))
                take.wait_taken()
                qk = qkv[:, :, 0:2 * D].rearrange("p c (m i two) -> p c m i two", i=HD // 2, two=2)
                cr = cross[:, :, :].rearrange("p c (m i two) -> p c m i two", i=HD // 2, two=2)
                sin = rope[:, 1, :].rearrange("p (i two) -> p i two", two=2)
                dims = [P, GT, 2 * H, HD // 2]
                for part in range(2):
                    last = dve.tensor_tensor(cr[:, :, :, :, part], qk[:, :, :, :, 1 - part],
                                             sin[:, :, part].unsqueeze(1).unsqueeze(1).broadcast_to(dims), ALU.mult)
                    if part == 0:
                        last.then_inc(chain, 1)
                        step.t.next()
                    else:
                        step(last)
                step(dve.tensor_tensor(rot[:, :, :].rearrange("p c (m e) -> p c m e", e=HD),
                                       qkv[:, :, 0:2 * D].rearrange("p c (m e) -> p c m e", e=HD),
                                       rope[:, 0, :].unsqueeze(1).unsqueeze(1).broadcast_to([P, GT, 2 * H, HD]), ALU.mult))
                dve.tensor_tensor(rot[:, :, :], rot[:, :, :], cross[:, :, :], ALU.add).then_inc(rotated, 1)
                for u in range(2):
                    take(lambda bank: dve.tensor_tensor(kv[:, u, :, :], bank.rearrange("p (c d) -> p c d", c=GT),
                                                        under(own[:, :], GT), ALU.mult))
                take.leave(NG)
                step.leave(NG)


def linear_attention_1(nc, io, x_tok, ident):
    with ExitStack() as stack:
        m = Memory(nc, stack, "la1")
        wqkv = m.sb("wqkv", [P, 3 * D])
        wo = m.sb("wo", [P, D])
        bo = m.sb("bo", [P, D])
        gain = m.sb("gain", [P, H])
        offset = m.sb("offset", [P, H])
        own = m.sb("own", [P, D])
        ones = m.sb("ones", [P, 64])
        nm = GroupNorm(m)
        xb = m.sb("xb", [P, GT, D])
        xnT = m.sb("xnT", [P, GC])
        qkv = m.sb("qkv", [P, GT, 3 * D])
        qT = m.sb("qT", [P, GC])
        gram = m.sb("gram", [P, 2, GT, 2 * D])
        y = m.sb("y", [P, GT, 3 * D])
        prod = m.sb("prod", [P, GT, D])
        square, length, ratio = (m.sb(n, [P, GT * H]) for n in ("square", "length", "ratio"))
        att = m.sb("att", [P, GT, D])
        attT = m.sb("attT", [P, GC])
        scratch = m.sb("scratch", [P, 2])
        vl = Lane(m, "vector_lane")
        sl = Lane(m, "scalar_lane")
        consts = m.sem("consts")
        chain = m.sem("vector_chain")
        xb_ready = m.sem("xb_ready")
        square_ready = m.sem("square_ready")
        length_ready = m.sem("length_ready")
        att_ready = m.sem("att_ready")
        block = stack.enter_context(nc.Block())
        N_CONSTS = 6
        VT, ST = 3 * GT, 4

        def group(it):
            return x_tok[:, bass.ds(it * GT, GT), :]

        @block.sync
        def _(sp):
            sp.dma_start(wqkv[:, :], io["L1_attn_w_qkvT"]).then_inc(consts, 16)
            sp.dma_start(wo[:, :], io["L1_attn_w_outT"]).then_inc(consts, 16)
            load_row(sp, bo[:, :], io["L1_attn_b_out"], consts)
            load_row(sp, gain[:, :], io["L1_attn_norm_g"].rearrange("a h b c -> (a h b c)"), consts)
            load_row(sp, offset[:, :], io["L1_attn_norm_b"].rearrange("a h b c -> (a h b c)"), consts)
            sp.dma_start(own[:, :], io["own_head"]).then_inc(consts, 16)

        @block.gpsimd
        def _(pool):
            pool.wait_ge(consts, 16 * N_CONSTS)
            pool.tensor_tensor(xb[:, :, :], x_tok[:, 0:GT, :], under(bo[:, :], GT), ALU.add).then_inc(xb_ready, 1)
            with pool.Fori(0, NG - 1) as it:
                pool.wait_ge(sl.free, it * ST + (ST + sl.banks))
                pool.tensor_tensor(xb[:, :, :], group(it + 1), under(bo[:, :], GT), ALU.add).then_inc(xb_ready, 1)

        @block.tensor
        def _(pe):
            v, s = Fill(pe, vl), Fill(pe, sl)
            pe.wait_ge(consts, 16 * N_CONSTS)
            with pe.Fori(0, NG) as it:
                v.enter(it, VT)
                s.enter(it, ST)
                pe.wait_ge(nm.ready, it + 1)

                def turn(src):
                    def fill(bank):
                        for c in range(GT):
                            last = pe.transpose(bank[:, c * P:(c + 1) * P], src(c), ident[:, :])
                        return last
                    return fill

                s(turn(lambda c: nm.xn[:, c, :]))
                s.wait_emptied()
                for c in range(GT):
                    v(lambda bank: pe.matmul(bank[:, 0:3 * D], xnT[:, c * P:(c + 1) * P], wqkv[:, :], start=True, stop=True))
                v.wait_emptied()
                s(turn(lambda c: qkv[:, c, 0:D]))
                for u in range(2):
                    for half in range(2):
                        def fill(bank):
                            rows = slice(64 * u, 64 * u + 64)
                            for i in range(GT // 2):
                                c = half * (GT // 2) + i
                                last = pe.matmul(bank[:, i * 2 * D:(i + 1) * 2 * D], qkv[rows, c, D:2 * D],
                                                 qkv[rows, c, D:3 * D], start=True, stop=True)
                            return last
                        v(fill)
                s.wait_emptied()
                v.wait_emptied()
                for c in range(GT):
                    def fill(bank):
                        for u in range(2):
                            rows = slice(64 * u, 64 * u + 64)
                            pe.matmul(bank[rows, 0:2 * D], qT[:, c * P + 64 * u:c * P + 64 * u + 64], gram[:, u, c, :],
                                      start=True, stop=True)
                        for u in range(2):
                            rows = slice(64 * u, 64 * u + 64)
                            last = pe.matmul(bank[rows, 2 * D:3 * D], ones[rows, :], qkv[rows, c, 2 * D:3 * D],
                                             start=True, stop=True)
                        return last
                    v(fill)
                pe.wait_ge(att_ready, it + 1)
                s(turn(lambda c: att[:, c, :]))
                s.wait_emptied()
                pe.wait_ge(xb_ready, it + 1)

                def fill(bank):
                    pe.matmul(bank, ident[:, :], flat(xb[:, :, :]), start=True, stop=False, skip_group_check=True)
                    for c in range(GT):
                        last = pe.matmul(bank[:, c * D:(c + 1) * D], attT[:, c * P:(c + 1) * P], wo[:, :],
                                         start=False, stop=(c == GT - 1), skip_group_check=True)
                    return last
                s(fill)
                v.leave(NG)
                s.leave(NG)

        @block.scalar
        def _(act):
            take = Take(act, sl)
            for _ in range(sl.banks):
                act.activation(scratch[:, 0:1], ident[:, 0:1], ACT.Copy).then_inc(sl.free, 1)
                act.wait_ge(sl.free, _ + 1)
            with act.Fori(0, NG) as it:
                take.enter(it, ST)
                nm.scalar(act, it)
                take(lambda bank: act.activation(xnT[:, :], bank, ACT.Copy))
                take(lambda bank: act.activation(qT[:, :], bank, ACT.Copy))
                act.wait_ge(square_ready, it + 1)
                act.activation(length[:, :], square[:, :], ACT.Sqrt).then_inc(length_ready, 1)
                take(lambda bank: act.activation(attT[:, :], bank, ACT.Copy))
                take(lambda bank: act.activation(group(it), bank.rearrange("p (c d) -> p c d", c=GT), ACT.Copy))
                take.leave(NG)

        @block.vector
        def _(dve):
            take, step = Take(dve, vl), Chain(dve, chain)
            for _ in range(vl.banks):
                dve.memset(ones[:, :], 1.0).then_inc(vl.free, 1)
                dve.wait_ge(vl.free, _ + 1)
            dve.wait_ge(consts, 16 * N_CONSTS)
            with dve.Fori(0, NG) as it:
                step.enter(it, nm.STEPS + 7)
                take.enter(it, VT)
                nm.vector(dve, group(it), step, it)
                for c in range(GT):
                    take(lambda bank: dve.tensor_copy(qkv[:, c, :], bank[:, 0:3 * D]))
                for u in range(2):
                    for half in range(2):
                        c0 = half * (GT // 2)
                        take(lambda bank: dve.tensor_tensor(
                            gram[:, u, c0:c0 + GT // 2, :].rearrange("p c (k d) -> p (c k) d", k=2),
                            bank.rearrange("p (c d) -> p c d", c=4), under(own[:, :], 4), ALU.mult))
                for c in range(GT):
                    take(lambda bank: dve.tensor_copy(y[:, c, :], bank[:, 0:3 * D]))
                take.wait_taken()

                def heads(ap):
                    return ap.rearrange("p c (h d) -> p c h d", d=HD)

                step(dve.tensor_tensor(prod[:, :, :], qkv[:, :, 0:D], y[:, :, 0:D], ALU.mult))
                step(dve.tensor_reduce(square[:, :], heads(prod[:, :, :]), X, ALU.add))
                dve.tensor_scalar(square[:, :], square[:, :], 0.0, None, ALU.max).then_inc(square_ready, 1)
                dve.wait_ge(length_ready, it + 1)
                step(dve.tensor_scalar(length[:, :], length[:, :], 1e-12, None, ALU.max))
                step(dve.reciprocal(ratio[:, :], length[:, :]))
                step(dve.tensor_tensor(ratio[:, :].rearrange("p (c h) -> p c h", h=H),
                                       ratio[:, :].rearrange("p (c h) -> p c h", h=H), under(gain[:, :], GT), ALU.mult))
                step(dve.tensor_tensor(heads(prod[:, :, :]), heads(y[:, :, D:2 * D]),
                                       ratio[:, :].rearrange("p (c h) -> p c h", h=H).unsqueeze(3)
                                       .broadcast_to([P, GT, H, HD]), ALU.mult))
                step(dve.tensor_tensor(heads(att[:, :, :]), heads(y[:, :, 2 * D:3 * D]),
                                       offset[:, :].unsqueeze(1).unsqueeze(3).broadcast_to([P, GT, H, HD]), ALU.mult))
                dve.tensor_tensor(att[:, :, :], att[:, :, :], prod[:, :, :], ALU.add).then_inc(att_ready, 1)
                take.leave(NG)
                step.leave(NG)


E = 8
FF = 512


def first_of_largest(dve, step, score, rank, top, hit, order):
    sh = [P, GT, E]
    step(dve.tensor_reduce(top[:, :], score, X, ALU.max))
    step(dve.tensor_tensor(hit, score, top[:, :].unsqueeze(2).broadcast_to(sh), ALU.is_equal))
    step(dve.tensor_tensor(hit, hit, under(rank[:, :], GT), ALU.mult))
    step(dve.tensor_reduce(order[:, :], hit, X, ALU.max))
    step(dve.tensor_tensor(hit, hit, order[:, :].unsqueeze(2).broadcast_to(sh), ALU.is_equal))


def moe_top1(nc, io, x_tok, ident):
    NF = FF // P
    with ExitStack() as stack:
        m = Memory(nc, stack, "moe1")
        gate = m.sb("gate", [P, E])
        w1 = m.sb("w1", [P, E, FF])
        b1 = m.sb("b1", [P, E * NF])
        w2 = m.sb("w2", [P, E * NF, D])
        b2 = m.sb("b2", [E, D])
        rank = m.sb("rank", [P, E])
        nm = GroupNorm(m)
        xnT = m.sb("xnT", [P, GC])
        logits = m.sb("logits", [P, GT, E])
        probs = m.sb("probs", [P, GT, E])
        hit = m.sb("hit", [P, GT, E])
        top, total, order = (m.sb(n, [P, GT]) for n in ("top", "total", "order"))
        share = m.sb("share", [P, GT, E])
        shareT = m.sb("shareT", [E, GC])
        hidden = m.sb("hidden", [P, 2, NF, GC])
        acc = m.sb("acc", [P, 2, GT, D])
        scratch = m.sb("scratch", [P, 2])
        vl = Lane(m, "vector_lane")
        sl = Lane(m, "scalar_lane")
        consts = m.sem("consts")
        w_loaded = m.sem("w_loaded")
        chain = m.sem("vector_chain")
        logits_ready = m.sem("logits_ready")
        probs_ready = m.sem("probs_ready")
        share_ready = m.sem("share_ready")
        block = stack.enter_context(nc.Block())
        N_CONSTS = 3
        VT, ST = 2 + E, 2 + E * NF

        def group(it):
            return x_tok[:, bass.ds(it * GT, GT), :]

        @block.sync
        def _(sp):
            sp.dma_start(gate[:, :], io["L1_ffn_gate_wT"]).then_inc(consts, 16)
            sp.dma_start(rank[:, :], io["rank"]).then_inc(consts, 16)
            sp.dma_start(b2[:, :], io["L1_ffn_b2"]).then_inc(consts, 16)
            sp.dma_start(b1[:, :], io["L1_ffn_b1T"]).then_inc(w_loaded, 16)
            sp.dma_start(w1[:, :, :], io["L1_ffn_w1"].rearrange("e c f -> c e f")).then_inc(w_loaded, 16)
            sp.dma_start(w2[:, :, :], io["L1_ffn_w2"].rearrange("e (f p) d -> p (e f) d", p=P)).then_inc(w_loaded, 16)

        @block.tensor
        def _(pe):
            v, s = Fill(pe, vl), Fill(pe, sl)
            pe.wait_ge(consts, 16 * N_CONSTS)
            pe.wait_ge(w_loaded, 48)
            with pe.Fori(0, NG) as it:
                v.enter(it, VT)
                s.enter(it, ST)
                pe.wait_ge(nm.ready, it + 1)

                def turn(src, rows=P):
                    def fill(bank):
                        for c in range(GT):
                            last = pe.transpose(bank[0:rows, c * P:(c + 1) * P], src(c), ident[:, :])
                        return last
                    return fill

                s(turn(lambda c: nm.xn[:, c, :]))
                s.wait_emptied()

                def fill(bank):
                    for c in range(GT):
                        last = pe.matmul(bank[:, c * E:(c + 1) * E], xnT[:, c * P:(c + 1) * P], gate[:, :],
                                         start=True, stop=True)
                    return last
                v(fill)

                def up(e):
                    for f in range(NF):
                        s(lambda bank: pe.matmul(bank, w1[:, e, f * P:(f + 1) * P], xnT[:, :], start=True, stop=True))

                def down(e):
                    def fill(bank):
                        for c in range(GT):
                            for f in range(NF):
                                last = pe.matmul(bank[:, c * D:(c + 1) * D], hidden[:, e % 2, f, c * P:(c + 1) * P],
                                                 w2[:, e * NF + f, :], start=(f == 0), stop=(f == NF - 1))
                        return last
                    v(fill)

                up(0)
                pe.wait_ge(share_ready, it + 1)
                s(turn(lambda c: share[:, c, :], E))
                s.wait_emptied()

                def fill(bank):
                    pe.matmul(bank, ident[:, :], group(it).rearrange("p c d -> p (c d)"),
                              start=True, stop=False, skip_group_check=True)
                    for c in range(GT):
                        last = pe.matmul(bank[:, c * D:(c + 1) * D], shareT[:, c * P:(c + 1) * P], b2[:, :],
                                         start=False, stop=(c == GT - 1), skip_group_check=True)
                    return last
                v(fill)
                for e in range(E):
                    if e + 1 < E:
                        up(e + 1)
                        pe.wait_ge(sl.free, s.t.value() + sl.banks - NF)
                    else:
                        s.wait_emptied()
                    down(e)
                v.leave(NG)
                s.leave(NG)

        @block.scalar
        def _(act):
            take = Take(act, sl)
            for _ in range(sl.banks):
                act.activation(scratch[:, 0:1], ident[:, 0:1], ACT.Copy).then_inc(sl.free, 1)
                act.wait_ge(sl.free, _ + 1)
            act.wait_ge(w_loaded, 48)
            with act.Fori(0, NG) as it:
                take.enter(it, ST)
                nm.scalar(act, it)
                take(lambda bank: act.activation(xnT[:, :], bank, ACT.Copy))

                def up(e):
                    for f in range(NF):
                        if f == 0 and e >= 2:
                            act.wait_ge(vl.full, it * VT + (2 + e - 1))
                        take(lambda bank: act.activation(hidden[:, e % 2, f, :], bank, ACT.Relu,
                                                         bias=b1[:, e * NF + f:e * NF + f + 1]))

                up(0)
                act.wait_ge(logits_ready, it + 1)
                act.activation(probs[:, :, :], logits[:, :, :], ACT.Exp).then_inc(probs_ready, 1)
                take(lambda bank: act.activation(shareT[:, :], bank[0:E, :], ACT.Copy))
                for e in range(1, E):
                    up(e)
                take.leave(NG)

        @block.vector
        def _(dve):
            take, step = Take(dve, vl), Chain(dve, chain)
            for _ in range(vl.banks):
                dve.memset(scratch[:, 1:2], 0.0).then_inc(vl.free, 1)
                dve.wait_ge(vl.free, _ + 1)
            dve.wait_ge(consts, 16 * N_CONSTS)
            with dve.Fori(0, NG) as it:
                step.enter(it, nm.STEPS + 9)
                take.enter(it, VT)
                nm.vector(dve, group(it), step, it)
                take(lambda bank: dve.tensor_copy(logits[:, :, :], bank[:, 0:GT * E].rearrange("p (c e) -> p c e", e=E)))
                take.wait_taken()
                step(dve.tensor_reduce(top[:, :], logits[:, :, :], X, ALU.max))
                dve.tensor_tensor(logits[:, :, :], logits[:, :, :], over(top[:, :], E), ALU.subtract).then_inc(logits_ready, 1)
                dve.wait_ge(probs_ready, it + 1)
                step(dve.tensor_reduce(total[:, :], probs[:, :, :], X, ALU.add))
                step(dve.reciprocal(total[:, :], total[:, :]))
                step(dve.tensor_tensor(probs[:, :, :], probs[:, :, :], over(total[:, :], E), ALU.mult))
                first_of_largest(dve, step, probs[:, :, :], rank, top, hit[:, :, :], order)
                dve.tensor_tensor(share[:, :, :], hit[:, :, :], probs[:, :, :], ALU.mult).then_inc(share_ready, 1)
                take(lambda bank: dve.tensor_copy(acc[:, 1, :, :], bank.rearrange("p (c d) -> p c d", c=GT)))
                for e in range(E):
                    take.wait_taken()

                    def out_of(bank):
                        for c in range(GT):
                            dst = acc[:, e % 2, c, :] if e < E - 1 else group(it)[:, c, :]
                            last = dve.scalar_tensor_tensor(out=dst, in0=bank[:, c * D:(c + 1) * D],
                                                            scalar=share[:, c, e:e + 1], in1=acc[:, (e + 1) % 2, c, :],
                                                            op0=ALU.mult, op1=ALU.add)
                        return last
                    take(out_of)
                take.leave(NG)
                step.leave(NG)


class GroupRms:

    def __init__(self, m, name):
        self.sq = m.sb(name + "_sq", [P, GT, D])
        self.var, self.std, self.rstd = (m.sb(name + "_" + n, [P, GT]) for n in ("var", "std", "rstd"))
        self.var_ready, self.std_ready = m.sem(name + "_var_ready"), m.sem(name + "_std_ready")

    STEPS = 5

    def vector(self, dve, src, gain, step, it):
        step(dve.tensor_tensor(self.sq[:, :, :], src, src, ALU.mult))
        step(dve.tensor_reduce(self.var[:, :], self.sq[:, :, :], X, ALU.add))
        dve.tensor_scalar(self.var[:, :], self.var[:, :], 1.0 / D, RMS_EPS, ALU.mult, ALU.add).then_inc(self.var_ready, 1)
        dve.wait_ge(self.std_ready, it + 1)
        step(dve.reciprocal(self.rstd[:, :], self.std[:, :]))
        step(dve.tensor_tensor(src, src, over(self.rstd[:, :], D), ALU.mult))
        step(dve.tensor_tensor(src, src, under(gain, GT), ALU.mult))

    def scalar(self, act, it):
        act.wait_ge(self.var_ready, it + 1)
        act.activation(self.std[:, :], self.var[:, :], ACT.Sqrt).then_inc(self.std_ready, 1)


def ffn_0(nc, io, x_tok, ident):
    with ExitStack() as stack:
        y = Memory(nc, stack, "ffn0").sb("y", [P, NT, D])
        moe_top2(nc, io, x_tok, ident, y)
        dense_path(nc, io, x_tok, ident, y)


def moe_top2(nc, io, x_tok, ident, y):
    with ExitStack() as stack:
        m = Memory(nc, stack, "moe0")
        router = m.sb("router", [P, E])
        w1, w3, w2 = (m.sb(n, [P, E, P]) for n in ("w1", "w3", "w2"))
        gain = m.sb("gain", [P, D])
        rank = m.sb("rank", [P, E])
        nm, rms = GroupNorm(m), GroupRms(m, "rms")
        xnT = m.sb("xnT", [P, GC])
        logits, probs, hit, hit2, rest, share = (m.sb(n, [P, GT, E]) for n in ("logits", "probs", "hit", "hit2", "rest", "share"))
        top, total, order = (m.sb(n, [P, GT]) for n in ("top", "total", "order"))
        gate = m.sb("gate", [P, 2, GC])
        hidden = m.sb("hidden", [P, 2, GC])
        acc = m.sb("acc", [P, 2, GT, D])
        zeros = m.sb("zeros", [P, D])
        scratch = m.sb("scratch", [P, 1])
        vl = Lane(m, "vector_lane")
        sl = Lane(m, "scalar_lane")
        consts = m.sem("consts")
        w_loaded = m.sem("w_loaded")
        chain = m.sem("vector_chain")
        logits_ready = m.sem("logits_ready")
        probs_ready = m.sem("probs_ready")
        block = stack.enter_context(nc.Block())
        N_CONSTS = 3
        V_ORDER = [("up", 0)] + [x for e in range(1, E) for x in (("up", e), ("down", e - 1))] + [("down", E - 1)]
        VT, ST = len(V_ORDER), 2 + E

        def v_at(what):
            return V_ORDER.index(what) + 1

        def group(it):
            return x_tok[:, bass.ds(it * GT, GT), :]

        @block.sync
        def _(sp):
            sp.dma_start(router[:, :], io["L0_ffn_router_w"]).then_inc(consts, 16)
            sp.dma_start(rank[:, :], io["rank"]).then_inc(consts, 16)
            load_row(sp, gain[:, :], io["L0_ffn_moe_norm_w"], consts)
            sp.dma_start(w1[:, :, :], io["L0_ffn_ew1"].rearrange("e c f -> c e f")).then_inc(w_loaded, 16)
            sp.dma_start(w3[:, :, :], io["L0_ffn_ew3"].rearrange("e c f -> c e f")).then_inc(w_loaded, 16)
            sp.dma_start(w2[:, :, :], io["L0_ffn_ew2"].rearrange("e f d -> f e d")).then_inc(w_loaded, 16)

        @block.tensor
        def _(pe):
            v, s = Fill(pe, vl), Fill(pe, sl)
            pe.wait_ge(consts, 16 * N_CONSTS)
            pe.wait_ge(w_loaded, 48)
            with pe.Fori(0, NG) as it:
                v.enter(it, VT)
                s.enter(it, ST)
                pe.wait_ge(nm.ready, it + 1)

                def fill(bank):
                    for c in range(GT):
                        last = pe.transpose(bank[:, c * P:(c + 1) * P], nm.xn[:, c, :], ident[:, :])
                    return last
                s(fill)
                s.wait_emptied()

                def fill(bank):
                    for c in range(GT):
                        last = pe.matmul(bank[:, c * E:(c + 1) * E], xnT[:, c * P:(c + 1) * P], router[:, :],
                                         start=True, stop=True)
                    return last
                s(fill)

                def up(e):
                    s(lambda bank: pe.matmul(bank, w1[:, e, :], xnT[:, :], start=True, stop=True))
                    v(lambda bank: pe.matmul(bank, w3[:, e, :], xnT[:, :], start=True, stop=True))

                def down(e):
                    pe.wait_ge(vl.free, it * VT + (v_at(("up", e)) + vl.banks))

                    def fill(bank):
                        for c in range(GT):
                            last = pe.matmul(bank[:, c * D:(c + 1) * D], hidden[:, e % 2, c * P:(c + 1) * P],
                                             w2[:, e, :], start=True, stop=True)
                        return last
                    v(fill)

                up(0)
                for e in range(1, E):
                    up(e)
                    down(e - 1)
                down(E - 1)
                v.leave(NG)
                s.leave(NG)

        @block.scalar
        def _(act):
            take = Take(act, sl)
            for _ in range(sl.banks):
                act.activation(scratch[:, 0:1], ident[:, 0:1], ACT.Copy).then_inc(sl.free, 1)
                act.wait_ge(sl.free, _ + 1)
            with act.Fori(0, NG) as it:
                take.enter(it, ST)
                nm.scalar(act, it)
                take(lambda bank: act.activation(xnT[:, :], bank, ACT.Copy))
                take(lambda bank: act.activation(logits[:, :, :], bank[:, 0:GT * E].rearrange("p (c e) -> p c e", e=E), ACT.Copy))
                act.wait_ge(logits_ready, it + 1)
                act.activation(probs[:, :, :], logits[:, :, :], ACT.Exp).then_inc(probs_ready, 1)
                for e in range(E):
                    if e >= 2:
                        act.wait_ge(vl.free, it * VT + (v_at(("up", e - 2)) + vl.banks))
                    take(lambda bank: act.activation(gate[:, e % 2, :], bank, ACT.Silu))
                rms.scalar(act, it)
                take.leave(NG)

        @block.vector
        def _(dve):
            take, step = Take(dve, vl), Chain(dve, chain)
            for _ in range(vl.banks):
                dve.memset(zeros[:, :], 0.0).then_inc(vl.free, 1)
                dve.wait_ge(vl.free, _ + 1)
            dve.wait_ge(consts, 16 * N_CONSTS)
            with dve.Fori(0, NG) as it:
                step.enter(it, nm.STEPS + 18 + rms.STEPS)
                take.enter(it, VT)
                nm.vector(dve, group(it), step, it)
                dve.wait_ge(sl.free, it * ST + (2 + sl.banks))
                step(dve.tensor_reduce(top[:, :], logits[:, :, :], X, ALU.max))
                dve.tensor_tensor(logits[:, :, :], logits[:, :, :], over(top[:, :], E), ALU.subtract).then_inc(logits_ready, 1)
                dve.wait_ge(probs_ready, it + 1)
                step(dve.tensor_reduce(total[:, :], probs[:, :, :], X, ALU.add))
                step(dve.reciprocal(total[:, :], total[:, :]))
                step(dve.tensor_tensor(probs[:, :, :], probs[:, :, :], over(total[:, :], E), ALU.mult))
                first_of_largest(dve, step, probs[:, :, :], rank, top, hit[:, :, :], order)
                step(dve.scalar_tensor_tensor(out=rest[:, :, :], in0=hit[:, :, :], scalar=-2.0, in1=probs[:, :, :],
                                              op0=ALU.mult, op1=ALU.add))
                first_of_largest(dve, step, rest[:, :, :], rank, top, hit2[:, :, :], order)
                step(dve.tensor_tensor(hit[:, :, :], hit[:, :, :], hit2[:, :, :], ALU.add))
                step(dve.tensor_tensor(share[:, :, :], hit[:, :, :], probs[:, :, :], ALU.mult))
                for what, e in V_ORDER:
                    if what == "up":
                        dve.wait_ge(sl.free, it * ST + (2 + e + 1 + sl.banks))
                        take(lambda bank: dve.tensor_tensor(hidden[:, e % 2, :], gate[:, e % 2, :], bank, ALU.mult))
                        continue
                    if e > 0:
                        take.wait_taken()

                    def out_of(bank):
                        for c in range(GT):
                            last = dve.scalar_tensor_tensor(out=acc[:, e % 2, c, :], in0=bank[:, c * D:(c + 1) * D],
                                                            scalar=share[:, c, e:e + 1],
                                                            in1=acc[:, (e + 1) % 2, c, :] if e else zeros[:, :],
                                                            op0=ALU.mult, op1=ALU.add)
                        return last
                    take(out_of)
                take.wait_taken()
                out = acc[:, (E - 1) % 2, :, :]
                rms.vector(dve, out, gain[:, :], step, it)
                step(dve.tensor_tensor(y[:, bass.ds(it * GT, GT), :], out, group(it), ALU.add))
                take.leave(NG)
                step.leave(NG)


def dense_path(nc, io, x_tok, ident, y):
    NF = FF // P
    HV = HD + 1
    with ExitStack() as stack:
        m = Memory(nc, stack, "dense")
        wq, wk, wv, wo = (m.sb(n, [P, D]) for n in ("wq", "wk", "wv", "wo"))
        w1, w3 = m.sb("w1", [P, FF]), m.sb("w3", [P, FF])
        w2 = m.sb("w2", [P, NF, D])
        attn_gain, ff_gain = m.sb("attn_gain", [P, D]), m.sb("ff_gain", [P, D])
        own = m.sb("own", [P, D])
        parity = m.sb("parity", [P, H])
        causal = m.sb("causal", [P, S])
        nm, rms1, rms2 = GroupNorm(m), GroupRms(m, "rms1"), GroupRms(m, "rms2")
        xnT = m.sb("xnT", [P, GC])
        qT = m.sb("qT", [P, GC])
        kT = m.sb("kT", [P, GC])
        keys = m.sb("keys", [P, 2 * GT, H, S])
        vals = m.sb("vals", [P, 2 * GT, H, HV])
        sc = m.sb("scores", [P, 2, H, S])
        mx = m.sb("max", [P, 2, H])
        ex = m.sb("exps", [P, 2, H, S])
        exT = m.sb("expsT", [P, 2, H // 2, P])
        denom = m.sb("denom", [P, GT, H])
        o = m.sb("o", [P, GT, D])
        oT = m.sb("oT", [P, GC])
        proj = m.sb("proj", [P, GT, D])
        h = m.sb("h", [P, GT, D])
        hT = m.sb("hT", [P, GC])
        gate = m.sb("gate", [P, NF, GC])
        hidden = m.sb("hidden", [P, NF, GC])
        ffn = m.sb("ffn", [P, GT, D])
        scratch = m.sb("scratch", [P, 2])
        vl = Lane(m, "vector_lane", 3)
        sl = Lane(m, "scalar_lane", 4)
        consts = m.sem("consts")
        ffn_loaded = m.sem("ffn_loaded")
        chain = m.sem("vector_chain")
        keys_even = m.sem("keys_of_even_tiles")
        keys_odd = m.sem("keys_of_odd_tiles")
        scores_ready = m.sem("scores_ready")
        shifted = m.sem("shifted")
        exps_ready = m.sem("exps_ready")
        vals_preset = m.sem("vals_preset")
        h_ready = m.sem("h_ready")
        block = stack.enter_context(nc.Block())
        N_CONSTS = 7
        V_ORDER = ["k", "v0", "v1", "s0", "s0", "s1", "s1", "s2", "s2", "o0", "s3", "s3", "o1", "o2", "o3",
                   "wo"] + ["w3"] * NF + ["w2"]
        S_ORDER = ["xn", "q"] + [f"e{c}" for c in range(GT) for _ in range(2)] + ["o", "h"] + ["w1"] * NF
        VT, ST = len(V_ORDER), len(S_ORDER)

        def v_at(what):
            return V_ORDER.index(what) + V_ORDER.count(what)

        def s_at(what):
            return S_ORDER.index(what) + S_ORDER.count(what)

        def group(it):
            return x_tok[:, bass.ds(it * GT, GT), :]

        def write_keys(eng, c):
            src = kT[:, c * P:(c + 1) * P].rearrange("p (b k) -> p b k", b=2).unsqueeze(2).broadcast_to([P, 2, H, S])
            of_head = own[:, :].rearrange("p (h d) -> p h d", d=HD)[:, :, 0].unsqueeze(1).unsqueeze(3)
            return eng.tensor_tensor(keys[:, 2 * c:2 * c + 2, :, :], src, of_head.broadcast_to([P, 2, H, S]), ALU.mult)

        @block.sync
        def _(sp):
            sp.dma_start(wq[:, :], io["L0_ffn_wq"]).then_inc(consts, 16)
            sp.dma_start(wk[:, :], io["L0_ffn_wk"]).then_inc(consts, 16)
            sp.dma_start(wv[:, :], io["L0_ffn_wv"]).then_inc(consts, 16)
            sp.dma_start(own[:, :], io["own_head"]).then_inc(consts, 16)
            sp.dma_start(parity[:, :], io["head_parity"]).then_inc(consts, 16)
            sp.dma_start(causal[:, :], io["causal"]).then_inc(consts, 16)
            sp.dma_start(wo[:, :], io["L0_ffn_wo"]).then_inc(consts, 16)
            load_row(sp, attn_gain[:, :], io["L0_ffn_attn_norm_w"], ffn_loaded)
            load_row(sp, ff_gain[:, :], io["L0_ffn_ff_norm_w"], ffn_loaded)
            sp.dma_start(w1[:, :], io["L0_ffn_w1"]).then_inc(ffn_loaded, 16)
            sp.dma_start(w3[:, :], io["L0_ffn_w3"]).then_inc(ffn_loaded, 16)
            sp.dma_start(w2[:, :, :], io["L0_ffn_w2"].rearrange("(f p) d -> p f d", p=P)).then_inc(ffn_loaded, 16)

        @block.gpsimd
        def _(pool):
            pool.wait_ge(consts, 16 * N_CONSTS)
            with pool.Fori(0, NG) as it:
                def shift(c):
                    pool.wait_ge(scores_ready, it * GT + (c + 1))
                    pool.tensor_tensor(sc[:, c % 2, :, :], sc[:, c % 2, :, :], over(mx[:, c % 2, :], S),
                                       ALU.subtract).then_inc(shifted, 1)

                pool.wait_ge(vl.free, it * VT + (v_at("k") + vl.banks))
                write_keys(pool, 1).then_inc(keys_odd, 1)
                shift(0)
                write_keys(pool, 3).then_inc(keys_odd, 1)
                for c in range(1, GT):
                    shift(c)

        @block.tensor
        def _(pe):
            v, s = Fill(pe, vl), Fill(pe, sl)
            pe.wait_ge(consts, 16 * N_CONSTS)
            pe.wait_ge(ffn_loaded, 16 * 5)
            with pe.Fori(0, NG) as it:
                v.enter(it, VT)
                s.enter(it, ST)

                def turn(src):
                    def fill(bank):
                        for c in range(GT):
                            last = pe.transpose(bank[:, c * P:(c + 1) * P], src[:, c, :], ident[:, :])
                        return last
                    return fill

                def values(i):
                    def fill(bank):
                        for j in range(4):
                            b = 4 * i + j
                            for half in range(2):
                                last = pe.matmul(bank[64 * half:64 * half + 64, j * D:(j + 1) * D],
                                                 xnT[:, b * S:(b + 1) * S], wv[:, :], start=True, stop=True)
                        return last
                    v(fill)

                def scores(c):
                    if c % 2 == 0:
                        pe.wait_ge(keys_even, it * 2 + (c // 2 + 1))
                    else:
                        pe.wait_ge(keys_odd, it * 2 + (c // 2 + 1))
                    for half in range(2):
                        def fill(bank):
                            for u in range(2):
                                last = pe.matmul(bank[64 * u:64 * u + 64, :], qT[:, c * P + 64 * u:c * P + 64 * u + 64],
                                                 flat(keys[:, 2 * c + u, half * 8:half * 8 + 8, :]), start=True, stop=True)
                            return last
                        v(fill)

                def turn_exps(c):
                    pe.wait_ge(exps_ready, it * GT + (c + 1))
                    pairs = ex[:, c % 2, :, :].rearrange("p (j t) k -> p j (t k)", t=2)
                    for half in range(2):
                        def fill(bank):
                            for i in range(4):
                                last = pe.transpose(bank[:, i * P:(i + 1) * P], pairs[:, half * 4 + i, :], ident[:, :])
                            return last
                        s(fill)

                def attend(c):
                    s.wait_emptied()

                    def fill(bank):
                        for j in range(H // 2):
                            for u in range(2):
                                last = pe.matmul(bank[64 * u:64 * u + 64, j * 2 * HV:(j + 1) * 2 * HV],
                                                 exT[:, c % 2, j, 64 * u:64 * u + 64],
                                                 flat(vals[:, 2 * c + u, 2 * j:2 * j + 2, :]), start=True, stop=True)
                        return last
                    v(fill)

                pe.wait_ge(nm.ready, it + 1)
                s(turn(nm.xn))
                s.wait_emptied()
                v(lambda bank: pe.matmul(bank, wk[:, :], xnT[:, :], start=True, stop=True))
                s(lambda bank: pe.matmul(bank, wq[:, :], xnT[:, :], start=True, stop=True))
                values(0)
                values(1)
                s.wait_emptied()
                scores(0)
                scores(1)
                turn_exps(0)
                scores(2)
                attend(0)
                turn_exps(1)
                scores(3)
                attend(1)
                for c in (2, 3):
                    turn_exps(c)
                    attend(c)
                v.wait_emptied()
                s(turn(o))
                s.wait_emptied()

                def fill(bank):
                    for c in range(GT):
                        last = pe.matmul(bank[:, c * D:(c + 1) * D], oT[:, c * P:(c + 1) * P], wo[:, :], start=True, stop=True)
                    return last
                v(fill)
                pe.wait_ge(h_ready, it + 1)
                s(turn(h))
                s.wait_emptied()
                for f in range(NF):
                    s(lambda bank: pe.matmul(bank, w1[:, f * P:(f + 1) * P], hT[:, :], start=True, stop=True))
                    v(lambda bank: pe.matmul(bank, w3[:, f * P:(f + 1) * P], hT[:, :], start=True, stop=True))
                v.wait_emptied()

                def fill(bank):
                    for c in range(GT):
                        for f in range(NF):
                            last = pe.matmul(bank[:, c * D:(c + 1) * D], hidden[:, f, c * P:(c + 1) * P], w2[:, f, :],
                                             start=(f == 0), stop=(f == NF - 1))
                    return last
                v(fill)
                v.leave(NG)
                s.leave(NG)

        @block.scalar
        def _(act):
            take = Take(act, sl)
            for _ in range(sl.banks):
                act.activation(scratch[:, 0:1], ident[:, 0:1], ACT.Copy).then_inc(sl.free, 1)
                act.wait_ge(sl.free, _ + 1)
            with act.Fori(0, NG) as it:
                take.enter(it, ST)

                def exps(c):
                    act.wait_ge(shifted, it * GT + (c + 1))
                    act.activation(ex[:, c % 2, :, :], sc[:, c % 2, :, :], ACT.Exp,
                                   scale=float(1 / np.sqrt(np.float32(HD)))).then_inc(exps_ready, 1)

                def take_exps(c):
                    if c >= 2:
                        act.wait_ge(vl.full, it * VT + v_at(f"o{c - 2}"))
                    for half in range(2):
                        take(lambda bank: act.activation(exT[:, c % 2, half * 4:half * 4 + 4, :],
                                                         bank.rearrange("p (j q) -> p j q", j=4), ACT.Copy))

                nm.scalar(act, it)
                take(lambda bank: act.activation(xnT[:, :], bank, ACT.Copy))
                take(lambda bank: act.activation(qT[:, :], bank, ACT.Copy))
                exps(0)
                for c in range(GT):
                    if c + 1 < GT:
                        exps(c + 1)
                    take_exps(c)
                take(lambda bank: act.activation(oT[:, :], bank, ACT.Copy))
                rms1.scalar(act, it)
                take(lambda bank: act.activation(hT[:, :], bank, ACT.Copy))
                for f in range(NF):
                    take(lambda bank: act.activation(gate[:, f, :], bank, ACT.Silu))
                rms2.scalar(act, it)
                take.leave(NG)

        @block.vector
        def _(dve):
            take, step = Take(dve, vl), Chain(dve, chain)
            for _ in range(vl.banks):
                dve.memset(scratch[:, 1:2], 0.0).then_inc(vl.free, 1)
                dve.wait_ge(vl.free, _ + 1)
            dve.wait_ge(consts, 16 * N_CONSTS)
            dve.wait_ge(ffn_loaded, 16 * 5)
            dve.tensor_copy(vals[:, :, :, HD], under(parity[:, :], 2 * GT)).then_inc(vals_preset, 1)
            dve.wait_ge(vals_preset, 1)
            with dve.Fori(0, NG) as it:
                step.enter(it, nm.STEPS + rms1.STEPS + rms2.STEPS + GT + 2)
                take.enter(it, VT)

                def take_scores(c):
                    if c >= 2:
                        dve.wait_ge(exps_ready, it * GT + (c - 1))
                    for half in range(2):
                        take(lambda bank: dve.tensor_tensor(sc[:, c % 2, half * 8:half * 8 + 8, :],
                                                            bank.rearrange("p (h k) -> p h k", h=8),
                                                            under(causal[:, :], 8), ALU.add))
                    take.wait_taken()
                    dve.tensor_reduce(mx[:, c % 2, :], sc[:, c % 2, :, :], X, ALU.max).then_inc(scores_ready, 1)

                def take_o(c):
                    def out_of(bank):
                        got = bank[:, 0:H * HV].rearrange("p (h d) -> p h d", d=HV)
                        step(dve.reciprocal(denom[:, c, :], got[:, :, HD]))
                        return dve.tensor_tensor(o[:, c, :].rearrange("p (h d) -> p h d", d=HD), got[:, :, 0:HD],
                                                 over(denom[:, c, :], HD), ALU.mult)
                    take(out_of)

                nm.vector(dve, group(it), step, it)
                take(lambda bank: dve.tensor_copy(kT[:, :], bank))
                take.wait_taken()
                write_keys(dve, 0).then_inc(keys_even, 1)
                for i in range(2):
                    take(lambda bank: dve.tensor_tensor(
                        vals[:, 4 * i:4 * i + 4, :, 0:HD], bank.rearrange("p (b h d) -> p b h d", b=4, d=HD),
                        parity[:, :].unsqueeze(1).unsqueeze(3).broadcast_to([P, 4, H, HD]), ALU.mult))
                write_keys(dve, 2).then_inc(keys_even, 1)
                take_scores(0)
                take_scores(1)
                take_scores(2)
                take_o(0)
                take_scores(3)
                take_o(1)
                take_o(2)
                take_o(3)
                take(lambda bank: dve.tensor_copy(proj[:, :, :], bank.rearrange("p (c d) -> p c d", c=GT)))
                take.wait_taken()
                rms1.vector(dve, proj[:, :, :], attn_gain[:, :], step, it)
                dve.tensor_tensor(h[:, :, :], nm.xn[:, :, :], proj[:, :, :], ALU.add).then_inc(h_ready, 1)
                for f in range(NF):
                    dve.wait_ge(sl.free, it * ST + (s_at("h") + f + 1 + sl.banks))
                    take(lambda bank: dve.tensor_tensor(hidden[:, f, :], gate[:, f, :], bank, ALU.mult))
                take(lambda bank: dve.tensor_copy(ffn[:, :, :], bank.rearrange("p (c d) -> p c d", c=GT)))
                take.wait_taken()
                rms2.vector(dve, ffn[:, :, :], ff_gain[:, :], step, it)
                dve.wait_ge(h_ready, it + 1)
                step(dve.tensor_tensor(ffn[:, :, :], ffn[:, :, :], h[:, :, :], ALU.add))
                step(dve.tensor_tensor(group(it), ffn[:, :, :], y[:, bass.ds(it * GT, GT), :], ALU.add))
                take.leave(NG)
                step.leave(NG)


PIECES = [(c, min(512, N_CTX - c)) for c in range(0, N_CTX, 512)]
NK = N_CTX + N_CTX % 2
MASK_FILL = -float(2 ** 27)
HALF = H // 2
HC = HALF * S


def cross_attention_1(nc, io, x_tok, ident):
    NU = 4 + 2 * len(PIECES) + 4 + 4 * 2 * len(PIECES)
    T_END, K_END, V_END = 4, 4 + 2 * len(PIECES), 4 + 2 * len(PIECES) + 4
    SCALE = float(np.float32(1.0) / np.sqrt(np.float32(HD)))
    with ExitStack() as stack:
        m = Memory(nc, stack, "xa1")
        wq, wk = (m.sb(n, [P, 2, P]) for n in ("wq_twice", "wk_twice"))
        bq, bk = (m.sb(n, [P, 2]) for n in ("bq_twice", "bk_twice"))
        wv, wo = m.sb("wvT", [P, D]), m.sb("woT", [P, D])
        bv, bo = m.sb("bv", [P, 1]), m.sb("bo", [P, D])
        half_head = m.sb("half_head", [P, HALF])
        quad_head = m.sb("quad_head", [P, 4])
        pair_row = m.sb("pair_row", [P, 2, 4])
        nm = Norm(m)
        xnT = m.sb("xnT", [P, NT * P])
        qf = m.sb("qf", [P, 512])
        q_hi = [m.sb(f"q_hi{g}", [P, NT * P], F32R) for g in range(2)]
        q_lo = [m.sb(f"q_lo{g}", [P, NT * P], F32R) for g in range(2)]
        ctx = [m.sb(f"ctx{u}", [P, NCH, D]) for u in range(2)]
        mask_row = [m.sb(f"mask_row{u}", [P, N_CTX], U8) for u in range(2)]
        mask_col = m.sb("mask_col", [P, B, FULL], U8)
        mask_tail = m.sb("mask_tail", [P, B], U8)
        key_fill = m.sb("key_fill", [P, B, NCH])
        bias = [m.sb(f"bias{u}", [P, NCH]) for u in range(2)]
        fill_row = m.sb("fill_row", [P, N_CTX])
        ctxT = m.sb("ctxT", [P, N_CTX])
        kf = [m.sb(f"kf{g}", [P, N_CTX]) for g in range(2)]
        keys = [[m.sb(f"keys{u}{g}", [P, NK], F32R) for g in range(2)] for u in range(2)]
        vals = [m.sb(f"vals{u}", [P, NCH, D]) for u in range(2)]
        qb_hi = [[m.sb(f"qb_hi{u}{g}", [P, HC], F32R) for g in range(2)] for u in range(2)]
        qb_lo = [[m.sb(f"qb_lo{u}{g}", [P, HC], F32R) for g in range(2)] for u in range(2)]
        shift = [[m.sb(f"shift{u}{g}", [P, HC], BF16) for g in range(2)] for u in range(2)]
        prob = [m.sb(f"prob{i}", [P, 2 * HC]) for i in range(2)]
        junk = m.sb("junk", [P, 512])
        tops = m.sb("tops", [P, 2 * HALF // 2, len(PIECES)])
        top = m.sb("top", [P, HALF])
        top_hi, top_lo = m.sb("top_hi", [P, HALF], BF16), m.sb("top_lo", [P, HALF], BF16)
        top_parts = m.sb("top_parts", [P, P])
        topT = m.sb("topT", [P, P], BF16)
        ones = m.sb("ones", [P, 32])
        ones_b = m.sb("ones_b", [P, P], BF16)
        recip = m.sb("recip", [P, 4, S])
        o = m.sb("o", [P, 4, S])
        scratch = m.sb("scratch", [P, 2])
        sl = Lane(m, "setup_lane", 4)
        el = Lane(m, "exp_lane", 2)
        ps_o = m.psum("ps_o", [P, 2, 4 * S])
        ps_m = m.psum("ps_m", [P, 512])
        consts = m.sem("consts")
        chain = m.sem("vector_chain")
        pool_chain = m.sem("pool_chain")
        ctx_loaded = [m.sem(f"ctx_loaded{u}") for u in range(2)]
        q_ready = m.sem("q_ready")
        key_fill_ready = m.sem("key_fill_ready")
        fill_ready = m.sem("fill_ready")
        keys_ready = m.sem("keys_ready")
        blocks_ready = m.sem("blocks_ready")
        top_ready = m.sem("top_ready")
        topT_full = m.sem("topT_full")
        topT_ready = m.sem("topT_ready")
        shift_ready = m.sem("shift_ready")
        prob_used = m.sem("prob_used")
        o_taken = m.sem("o_taken")
        bias_added = m.sem("bias_added")
        mask_tail_cleared = m.sem("mask_tail_cleared")
        block = stack.enter_context(nc.Block())
        N_CONSTS = 13
        LOADS = 48

        def cols(b):
            return bass.ds(b * S, S)

        def batches(eng, enter, body, leave):
            with eng.Fori(0, B // 2 - 1) as it:
                enter(it)
                for u in range(2):
                    body(it * 2 + u, u, True)
                leave(B // 2 - 1)
            body(B - 2, 0, True)
            body(B - 1, 1, False)

        @block.sync
        def _(sp):
            for dst, src in ((wq[:, :, :], "L1_xattn_WqT2"), (wk[:, :, :], "L1_xattn_WkT2"), (bq[:, :], "L1_xattn_bq2"),
                             (bk[:, :], "L1_xattn_bk2"), (wv[:, :], "L1_xattn_WvT"), (wo[:, :], "L1_xattn_WoT"),
                             (half_head[:, :], "half_head"), (quad_head[:, :], "quad_head"),
                             (pair_row[:, :, :], "pair_row")):
                sp.dma_start(dst, io[src]).then_inc(consts, 16)
            sp.dma_start(bv[:, :], io["L1_xattn_bv"].rearrange("(p a) -> p a", a=1)).then_inc(consts, 16)
            load_row(sp, bo[:, :], io["L1_xattn_bo"], consts)
            sp.dma_start(mask_col[:, :, :], io["mask"][:, 0:FULL * P].rearrange("b (p j) -> p b j", j=FULL)).then_inc(consts, 16)
            sp.wait_ge(mask_tail_cleared, 1)
            sp.dma_start(mask_tail[0:TAIL, :], io["mask_tail"]).then_inc(consts, 16)

            def load(b, u):
                src = io["ctx_1024"][b] if isinstance(b, int) else io["ctx_1024"][bass.ds(b, 1)].rearrange("a t c -> (a t) c")
                row = io["mask_row"][b:b + 1, :] if isinstance(b, int) else io["mask_row"][bass.ds(b, 1), :]
                load_ctx(sp, ctx[u][:, :, :], src, ctx_loaded[u])
                sp.dma_start(mask_row[u][:, :], row.broadcast_to([P, N_CTX])).then_inc(ctx_loaded[u], 16)

            load(0, 0)
            load(1, 1)
            with sp.Fori(0, B // 2 - 1) as it:
                for u in range(2):
                    sp.wait_ge(top_ready, it * 2 + (u + 1))
                    load(it * 2 + (2 + u), u)

        @block.gpsimd
        def _(pool):
            pool.memset(mask_tail[:, :], 0).then_inc(mask_tail_cleared, 1)
            step = Chain(pool, pool_chain)
            loaded = [Tally(s) for s in ctx_loaded]
            tops_t, free, turned, own_keys = Tally(top_ready), Tally(sl.free), Tally(topT_ready), Tally(keys_ready)

            def setup(b, u, first=False):
                wait_apart(pool, (consts, 16 * N_CONSTS), [(ctx_loaded[u], loaded[u].next(LOADS))]
                           + ([] if first else [(top_ready, tops_t.next())]))
                pool.tensor_scalar(fill_row[:, :], mask_row[u][:, :], -1.0, -MASK_FILL, ALU.add, ALU.mult).then_inc(fill_ready, 1)
                for g in range(2):
                    k = T_END + (g + 1) * len(PIECES)
                    wait_apart(pool, (consts, 16 * N_CONSTS), [(sl.free, free.value() + (k + sl.banks))])
                    step(pool.tensor_copy(keys[u][g][:, 0:N_CTX], kf[g][:, :]))
                    pool.tensor_tensor(keys[u][g][64:P, 0:N_CTX], kf[g][64:P, :], keys[u][g][64:P, 0:N_CTX],
                                       ALU.subtract).then_inc(keys_ready, 1)
                    pool.wait_ge(keys_ready, own_keys.next())
                    if g == 0:
                        for h in range(2):
                            for dst, src in ((qb_hi, q_hi), (qb_lo, q_lo)):
                                pool.tensor_tensor(
                                    dst[u][h][:, :].rearrange("p (a q) -> p a q", q=S),
                                    src[h][:, cols(b)].unsqueeze(1).broadcast_to([P, HALF, S]),
                                    over(half_head[:, :], S), ALU.mult).then_inc(blocks_ready, 1)
                        pool.tensor_copy(bias[u][:, :], key_fill[:, bass.ds(b, 1), :].rearrange("p a j -> p (a j)")).then_inc(blocks_ready, 1)
                free.next(NU)
                pool.wait_ge(topT_ready, turned.next())
                for g in range(2):
                    pool.tensor_tensor(shift[u][g][:, :].rearrange("p (a q) -> p a q", q=P), under(topT[:, :], 4),
                                       over(pair_row[:, g, :], P), ALU.mult).then_inc(shift_ready, 1)

            pool.memset(ones[:, :], 1.0).then_inc(q_ready, 1)
            pool.memset(ones_b[:, :], 1.0).then_inc(q_ready, 1)
            pool.memset(top_parts[:, :], 0.0).then_inc(q_ready, 1)
            for u in range(2):
                for g in range(2):
                    pool.memset(keys[u][g][:, :].bitcast(F32), 0.0).then_inc(pool_chain, 1)
                    pool.wait_ge(pool_chain, step.t.next())
            pool.wait_ge(consts, 16 * N_CONSTS)
            pool.wait_ge(key_fill_ready, 10)
            free.next(12)
            setup(0, 0, first=True)

            tallies = (step.t, tops_t, free, turned, own_keys)

            def enter(it):
                for t, per in zip(tallies, (4, 2, 2 * NU, 2, 4)):
                    t.enter(it, per)
                for t in loaded:
                    t.enter(it, LOADS)

            def leave(n):
                for t in (*tallies, *loaded):
                    t.leave(n)

            batches(pool, enter, lambda b, u, more: setup(b + 1, 1 - u) if more else None, leave)
            pool.tensor_tensor(x_tok[:, :, :], x_tok[:, :, :], under(bo[:, :], NT), ALU.add).then_inc(bias_added, 1)

        @block.tensor
        def _(pe):
            s, e = Fill(pe, sl), Fill(pe, el)
            loaded = [Tally(t) for t in ctx_loaded]
            keys_t, blocks_t, top_t, shift_t, taken_t = (Tally(t) for t in (keys_ready, blocks_ready, top_ready, shift_ready, o_taken))
            pe.wait_ge(nm.ready, 1)
            for g in range(NG):
                def fill(bank):
                    for c in range(GT):
                        last = pe.transpose(bank[:, c * P:(c + 1) * P], nm.xn[:, GT * g + c, :], ident[:, :])
                    return last
                s(fill)
            s.wait_emptied()
            pe.wait_ge(consts, 16 * N_CONSTS)
            for h in range(2):
                for g in range(NG):
                    s(lambda bank: pe.matmul(bank, wq[:, h, :], xnT[:, g * GC:(g + 1) * GC], start=True, stop=True))
            pe.wait_ge(q_ready, 3)
            for _ in range(2):
                pe.matmul(ps_m[0:32, 0:32], ones[:, :], ones[:, :], start=True, stop=True).then_inc(prob_used, 1)

            def setup_parts(u):
                def turn_ctx():
                    pe.wait_ge(ctx_loaded[u], loaded[u].next(LOADS))
                    for chunks in GROUPS:
                        def fill(bank):
                            for j in chunks:
                                r = ROWS[j]
                                last = pe.transpose(bank[:, (j % 4) * P:(j % 4) * P + r], ctx[u][0:r, j, :], ident[0:r, 0:r])
                            return last
                        s(fill)
                    s.wait_emptied()

                def project_keys(g):
                    for c, w in PIECES:
                        s(lambda bank: pe.matmul(bank[:, 0:w], wk[:, g, :], ctxT[:, c:c + w], start=True, stop=True))

                def project_values():
                    for chunks in GROUPS:
                        def fill(bank):
                            for j in chunks:
                                r = ROWS[j]
                                last = pe.matmul(bank[0:r, (j % 4) * D:(j % 4 + 1) * D], ctxT[:, j * P:j * P + r], wv[:, :],
                                                 start=True, stop=True)
                            return last
                        s(fill)

                def pair_scores(pair):
                    g, a = divmod(pair, HALF // 2)
                    if pair == 0:
                        pe.wait_ge(blocks_ready, blocks_t.next(5))
                    if a == 0:
                        pe.wait_ge(keys_ready, keys_t.next())
                    for c, w in PIECES:
                        w += w % 2
                        s(lambda bank: pe.matmul(bank[:, 0:w], qb_hi[u][g][:, a * P:(a + 1) * P], keys[u][g][:, c:c + w],
                                                 start=True, stop=True))

                return [turn_ctx, lambda: project_keys(0), lambda: project_keys(1), project_values,
                        *[lambda pair=pair: pair_scores(pair) for pair in range(HALF)]]

            def turn_top():
                pe.wait_ge(top_ready, top_t.next())
                pe.transpose(ps_m[:, 0:P], top_parts[:, :], ident[:, :]).then_inc(topT_full, 1)

            for part in setup_parts(0):
                part()
            turn_top()

            def weigh(u, c, j):
                r = ROWS[j]
                pe.wait_ge(el.free, e.t.value() + el.banks - (2 if j < NCH - 1 else 0))
                for part in range(2):
                    for q in range(4):
                        w = vals[u][0:r, j, 32 * q:32 * q + 32] if part == 0 else ones[0:r, :]
                        last = pe.matmul(ps_o[32 * q:32 * q + 32, part, :], w, prob[c % 2][0:r, 4 * S * q:4 * S * (q + 1)],
                                         start=(j == 0 and part == 0), stop=(j == NCH - 1), skip_group_check=True)
                last.then_inc(prob_used, 1)
                return last

            def attend(b, u, more):
                parts = setup_parts(1 - u) if more else []
                pe.wait_ge(shift_ready, shift_t.next(2))
                for j in range(NCH):
                    r = ROWS[j]
                    for g in range(2):
                        def fill(bank):
                            k = keys[u][g][:, j * P:j * P + r]
                            pe.matmul(bank[0:r, :], k, qb_hi[u][g][:, :], start=True, stop=False)
                            pe.matmul(bank[0:r, :], k, qb_lo[u][g][:, :], start=False, stop=False)
                            return pe.matmul(bank[0:r, :], ones_b[:, 0:r], shift[u][g][:, :], start=False, stop=True)
                        e(fill)
                    if j == 1:
                        pe.wait_ge(o_taken, taken_t.next())
                    if j > 0:
                        weigh(u, u * NCH + j - 1, j - 1)
                    if j < len(parts):
                        parts[j]()
                if more:
                    turn_top()
                pe.wait_ge(el.free, e.t.value() + el.banks)
                weigh(u, u * NCH + NCH - 1, NCH - 1)

            tallies = (keys_t, blocks_t, top_t, shift_t, taken_t)

            def enter(it):
                s.enter(it, 2 * NU)
                e.enter(it, 4 * NCH)
                for t, per in zip(tallies, (4, 10, 2, 4, 2)):
                    t.enter(it, per)
                for t in loaded:
                    t.enter(it, LOADS)

            def leave(n):
                for t in (s, e, *tallies, *loaded):
                    t.leave(n)

            batches(pe, enter, attend, leave)
            pe.wait_ge(o_taken, B + 2)
            pe.wait_ge(bias_added, 1)
            for g in range(NG):
                def fill(bank):
                    pe.matmul(bank, ident[:, :], x_tok[:, GT * g:GT * (g + 1), :].rearrange("p c d -> p (c d)"),
                              start=True, stop=False, skip_group_check=True)
                    for c in range(GT):
                        n = GT * g + c
                        last = pe.matmul(bank[:, c * D:(c + 1) * D], xnT[:, n * P:(n + 1) * P], wo[:, :],
                                         start=False, stop=(c == GT - 1), skip_group_check=True)
                    return last
                s(fill)

        @block.scalar
        def _(act):
            take = Take(act, el)
            norm_scalar(act, nm)
            for _ in range(el.banks):
                act.activation(scratch[:, 0:1], ident[:, 0:1], ACT.Copy).then_inc(el.free, 1)
                act.wait_ge(el.free, _ + 1)
            blocks_t, used = Tally(blocks_ready), Tally(prob_used)

            def attend(b, u, more):
                act.wait_ge(blocks_ready, blocks_t.next(5))
                for j in range(NCH):
                    r = ROWS[j]
                    i = (u * NCH + j) % 2
                    act.wait_ge(prob_used, used.next())
                    for g in range(2):
                        take(lambda bank: act.activation(prob[i][0:r, g * HC:(g + 1) * HC], bank[0:r, :], ACT.Exp,
                                                         bias=bias[u][0:r, j:j + 1], scale=SCALE))

            def enter(it):
                take.enter(it, 4 * NCH)
                blocks_t.enter(it, 10)
                used.enter(it, 2 * NCH)

            def leave(n):
                for t in (take, blocks_t, used):
                    t.leave(n)

            batches(act, enter, attend, leave)

        @block.vector
        def _(dve):
            take, step = Take(dve, sl), Chain(dve, chain)
            loaded = [Tally(t) for t in ctx_loaded]
            fill_t, topT_t, o_t = Tally(fill_ready), Tally(topT_full), Tally(prob_used)
            o_t.next(2)
            for _ in range(sl.banks):
                dve.memset(scratch[:, 1:2], 0.0).then_inc(sl.free, 1)
                dve.wait_ge(sl.free, _ + 1)
            dve.memset(scratch[:, 1:2], 0.0).then_inc(o_taken, 1)
            norm_vector(dve, nm, x_tok, step.t)
            for g in range(NG):
                take(lambda bank: dve.tensor_copy(xnT[:, g * GC:(g + 1) * GC], bank))
            dve.wait_ge(consts, 16 * N_CONSTS)
            dve.tensor_scalar(key_fill[:, :, 0:FULL], mask_col[:, :, :], -1.0, -MASK_FILL * SCALE, ALU.add,
                              ALU.mult).then_inc(key_fill_ready, 1)
            dve.tensor_scalar(key_fill[:, :, FULL], mask_tail[:, :], -1.0, -MASK_FILL * SCALE, ALU.add,
                              ALU.mult).then_inc(key_fill_ready, 1)
            for h in range(2):
                for g in range(NG):
                    part = slice(g * GC, (g + 1) * GC)
                    take(lambda bank: dve.tensor_scalar(qf[:, :], bank, bq[:, h:h + 1], None, ALU.add))
                    take.wait_taken()
                    step(dve.tensor_copy(q_hi[h][:, part], qf[:, :]))
                    dve.tensor_tensor(q_lo[h][:, part], qf[:, :], q_hi[h][:, part], ALU.subtract).then_inc(key_fill_ready, 1)
                    dve.wait_ge(key_fill_ready, 2 + h * NG + g + 1)

            def setup(u):
                for chunks in GROUPS:
                    c0, w = chunks[0] * P, sum(ROWS[j] for j in chunks)
                    take(lambda bank: dve.tensor_copy(ctxT[:, c0:c0 + w], bank[:, 0:w]))
                dve.wait_ge(ctx_loaded[u], loaded[u].next(LOADS))
                for g in range(2):
                    for c, w in PIECES:
                        take(lambda bank: dve.scalar_tensor_tensor(out=kf[g][:, c:c + w], in0=bank[:, 0:w], scalar=bk[:, g:g + 1],
                                                                   in1=mask_row[u][:, c:c + w], op0=ALU.add, op1=ALU.mult))
                for chunks in GROUPS:
                    r, w = ROWS[chunks[0]], len(chunks)
                    take(lambda bank: dve.tensor_copy(vals[u][0:r, chunks[0]:chunks[0] + w, :],
                                                      bank[0:r, 0:w * D].rearrange("p (j d) -> p j d", j=w)))
                dve.wait_ge(fill_ready, fill_t.next())
                for pair in range(HALF):
                    for i, (c, w) in enumerate(PIECES):
                        wait_apart(dve, (consts, 16 * N_CONSTS), [(sl.full, take.t.next()), (sl.free, take.t.value() + (sl.banks - 1))])
                        dve.tensor_tensor_reduce(junk[:, 0:w], sl.ps[:, take.k % sl.banks, 0:w], fill_row[:, c:c + w], 1.0,
                                                 -3.0e38, ALU.add, ALU.max, tops[:, pair, i:i + 1]).then_inc(sl.free, 1)
                        take.k += 1
                take.wait_taken()
                step(dve.tensor_reduce(top[:, :], tops[:, :, :], X, ALU.max))
                step(dve.tensor_scalar(top_hi[:, :], top[:, :], -1.0, None, ALU.mult))
                step(dve.scalar_tensor_tensor(out=top_lo[:, :], in0=top[:, :], scalar=-1.0, in1=top_hi[:, :],
                                              op0=ALU.mult, op1=ALU.subtract))
                slots = top_parts[:, :].rearrange("p (g i) -> p g i", g=2)[:, :, 0:8].rearrange("p g (a part) -> p g a part", part=2)
                step(dve.tensor_copy(slots[:, :, :, 0], top_hi[:, :].rearrange("p (g a) -> p g a", g=2)))
                dve.tensor_copy(slots[:, :, :, 1], top_lo[:, :].rearrange("p (g a) -> p g a", g=2)).then_inc(top_ready, 1)
                dve.wait_ge(topT_full, topT_t.next())
                dve.tensor_copy(topT[:, :], ps_m[:, 0:P]).then_inc(topT_ready, 1)

            dve.wait_ge(q_ready, 3)
            setup(0)

            def attend(b, u, more):
                if more:
                    setup(1 - u)
                dve.wait_ge(prob_used, o_t.next(NCH))
                quads = [P, 4, S]
                step(dve.reciprocal(recip[:, :, :], ps_o[:, 1, :].rearrange("p (a q) -> p a q", a=4)))
                step(dve.tensor_tensor(recip[:, :, :], recip[:, :, :], over(quad_head[:, :], S), ALU.mult))
                dve.tensor_tensor(o[:, :, :], ps_o[:, 0, :].rearrange("p (a q) -> p a q", a=4), recip[:, :, :],
                                  ALU.mult).then_inc(o_taken, 1)
                dve.wait_ge(o_taken, taken.next())
                step(dve.tensor_reduce(xnT[:, cols(b)], o[:, :, :].rearrange("p a q -> p q a"), X, ALU.add))

            taken = Tally(o_taken)
            taken.next()
            tallies = (take, step, *loaded, fill_t, topT_t, o_t, taken)

            def enter(it):
                for t, per in zip(tallies, (2 * NU, 14, LOADS, LOADS, 2, 2, 2 * NCH, 2)):
                    t.enter(it, per)

            def leave(n):
                for t in tallies:
                    t.leave(n)

            batches(dve, enter, attend, leave)
            step(dve.tensor_scalar(xnT[:, :], xnT[:, :], bv[:, 0:1], None, ALU.add))
            dve.tensor_copy(scratch[:, 1:2], xnT[:, 0:1]).then_inc(o_taken, 1)
            for g in range(NG):
                take(lambda bank: dve.tensor_copy(x_tok[:, GT * g:GT * (g + 1), :], bank.rearrange("p (c d) -> p c d", c=GT)))


def program(nc, io):
    with ExitStack() as stack:
        m = Memory(nc, stack, "all")
        ident = m.sb("ident", [P, P])
        x_tok = m.sb("x_tok", [P, NT, D])
        loaded = m.sem("loaded")
        stored = m.sem("stored")
        x_dram = io["x"].rearrange("b s d -> (b s) d").rearrange("(n p) d -> p n d", p=P)
        with nc.Block() as block:
            @block.sync
            def _(sp):
                sp.dma_start(ident[:, :], io["ident"]).then_inc(loaded, 16)
                sp.dma_start(x_tok[:, :, :], x_dram).then_inc(loaded, 16)
                sp.wait_ge(loaded, 32)
        for part in PARTS:
            part(nc, io, x_tok, ident)
        with nc.Block() as block:
            @block.sync
            def _(sp):
                sp.dma_start(io["out"].rearrange("b s d -> (b s) d").rearrange("(n p) d -> p n d", p=P), x_tok[:, :, :]).then_inc(stored, 16)
                sp.wait_ge(stored, 16)


PARTS = (cross_attention_0, linear_attention_0, ffn_0, cross_attention_1, linear_attention_1, moe_top1)


def constants():
    pos = np.arange(P)[:, None] % S
    freq = (1.0 / np.float32(10000.0) ** np.arange(0, HD, 2, dtype=np.float32)).astype(np.float32)
    angle = (pos.astype(np.float32) * freq[None, :]).astype(np.float32)
    rope = np.zeros((P, 2, HD), np.float32)
    rope[:, 0, 0::2] = rope[:, 0, 1::2] = np.cos(angle)
    rope[:, 1, 0::2], rope[:, 1, 1::2] = -np.sin(angle), np.sin(angle)
    head = np.arange(D) // HD
    own = (head[:, None] == head[None, :]).astype(np.float32)
    row = np.arange(P)
    half_head = (row[:, None] % 64 // HD == np.arange(H // 2)[None, :]).astype(np.float32)
    quad_head = (row[:, None] % 32 // HD == np.arange(4)[None, :]).astype(np.float32)
    pair_row = np.zeros((P, 2, 4), np.float32)
    for g in range(2):
        for a in range(4):
            pair_row[64 * g + 2 * a:64 * g + 2 * a + 2, g, a] = 1
    causal = np.where(np.arange(S)[None, :] <= row[:, None] % S, 0.0, CAUSAL_FILL).astype(np.float32)
    parity = (np.arange(H)[None, :] % 2 == row[:, None] // 64).astype(np.float32)
    return {"causal": causal, "head_parity": parity, "half_head": half_head, "quad_head": quad_head, "pair_row": pair_row,
            "ident": np.eye(P, dtype=np.float32), "rope": rope, "own_head": own,
            "rank": np.tile(np.arange(E, 0, -1, dtype=np.float32), (P, 1)),
            "own_head_scaled": (own / np.sqrt(np.float32(HD))).astype(np.float32)}


def layout(inputs):
    a = {k: np.asarray(v) for k, v in inputs.items()}
    for name in ("L0_xattn_Wq", "L0_xattn_Wv", "L0_xattn_Wo", "L1_attn_w_qkv", "L1_attn_w_out", "L1_ffn_gate_w", "L1_xattn_Wv", "L1_xattn_Wo"):
        a[name + "T"] = np.ascontiguousarray(a.pop(name).T)
    a["L1_ffn_b1T"] = np.ascontiguousarray(a.pop("L1_ffn_b1").reshape(E, FF // P, P).transpose(2, 0, 1).reshape(P, -1))
    for n in "qk":
        wt = a.pop(f"L1_xattn_W{n}").T.reshape(D, 2, 1, D // 2)
        a[f"L1_xattn_W{n}T2"] = np.ascontiguousarray(np.repeat(wt, 2, axis=2).reshape(D, 2, D))
        bt = a.pop(f"L1_xattn_b{n}").reshape(2, 1, D // 2)
        a[f"L1_xattn_b{n}2"] = np.ascontiguousarray(np.repeat(bt, 2, axis=1).reshape(2, D).T)
    mask = a.pop("mask_BxS2_bf1").view(np.uint8)
    full = mask[:, :FULL * P].reshape(B, P, FULL)
    a["mask_row"] = np.ascontiguousarray(np.concatenate([full.transpose(0, 2, 1).reshape(B, -1), mask[:, FULL * P:]], 1))
    a["mask"] = mask
    a["mask_tail"] = np.ascontiguousarray(mask[:, FULL * P:].T)
    return {**a, **constants()}


def kernel(**inputs):
    import concourse.bacc as bacc
    from concourse.bass_utils import run_bass_kernel_spmd

    nc = bacc.Bacc("TRN2", target_bir_lowering=False, num_devices=1)
    arrays = layout(inputs)
    io = {name: nc.dram_tensor(f"in_{name}", a.shape, mybir.dt.from_np(a.dtype), kind="ExternalInput").ap()
          for name, a in arrays.items()}
    io["out"] = nc.dram_tensor("out", (B, S, D), F32, kind="ExternalOutput").ap()
    program(nc, io)
    result = run_bass_kernel_spmd(nc, [{f"in_{name}": a for name, a in arrays.items()}], core_ids=[0])
    return result.results[0]["out"]
```

```python
from contextlib import ExitStack

import numpy as np

import concourse.bass as bass
from concourse import mybir

F32 = mybir.dt.float32
F32R = mybir.dt.float32r
BF16 = mybir.dt.bfloat16
U8 = mybir.dt.uint8
ALU = mybir.AluOpType
ACT = mybir.ActivationFunctionType
X = mybir.AxisListType.X

P = 128
B, S, D = 32, 64, 128
N_CTX = 1601
NT = B * S // P
NCH = (N_CTX + P - 1) // P
FULL = NCH - 1
TAIL = N_CTX - FULL * P
H, HD = 16, 8
LN_EPS = 1e-5
RMS_EPS = 1e-5
CAUSAL_FILL = -1e30
ROWS = [P] * FULL + [TAIL]
GROUPS = [list(range(i, min(i + 4, NCH))) for i in range(0, NCH, 4)]


class Tally:

    def __init__(self, sem):
        self.sem, self.base, self.n, self.it, self.per = sem, 0, 0, None, 0

    def next(self, k=1):
        self.n += k
        return self.value()

    def value(self):
        return self.base + self.n if self.it is None else self.it * self.per + (self.base + self.n)

    def enter(self, it, per):
        self.base, self.n, self.it, self.per = self.base + self.n, 0, it, per

    def leave(self, times):
        assert self.n == self.per, (self.n, self.per)
        self.base, self.n, self.it = self.base + self.per * times, 0, None


def wait_apart(eng, constant, waits):
    waits = [(sem, value if isinstance(value, int) else eng.to_reg(value)) for sem, value in waits]
    eng.wait_ge(*constant)
    for sem, value in waits:
        eng.wait_ge(sem, value)


class Memory:

    def __init__(self, nc, stack, prefix):
        self.nc, self.stack, self.prefix = nc, stack, prefix

    def sb(self, name, shape, dt=F32):
        return self.stack.enter_context(self.nc.sbuf_tensor(f"{self.prefix}_{name}", shape, dt))

    def psum(self, name, shape, dt=F32):
        return self.stack.enter_context(self.nc.psum_tensor(f"{self.prefix}_{name}", shape, dt))

    def sem(self, name):
        return self.stack.enter_context(self.nc.semaphore(f"{self.prefix}_{name}"))


def over(ap, n):
    return ap.unsqueeze(2).broadcast_to([ap.shape[0], ap.shape[1], n])


def under(ap, n):
    return ap.unsqueeze(1).broadcast_to([ap.shape[0], n, ap.shape[1]])


class Norm:

    def __init__(self, m, name="ln"):
        self.xn = m.sb(name + "_xn", [P, NT, D])
        self.sq = m.sb(name + "_sq", [P, NT, D])
        self.mean = m.sb(name + "_mean", [P, NT])
        self.var = m.sb(name + "_var", [P, NT])
        self.std = m.sb(name + "_std", [P, NT])
        self.rstd = m.sb(name + "_rstd", [P, NT])
        self.var_ready = m.sem(name + "_var_ready")
        self.std_ready = m.sem(name + "_std_ready")
        self.ready = m.sem(name + "_ready")


def norm_vector(dve, nm, x, chain):
    def step(ins):
        ins.then_inc(chain.sem, 1)
        dve.wait_ge(chain.sem, chain.next())

    step(dve.tensor_reduce(nm.mean[:, :], x[:, :, :], X, ALU.add))
    step(dve.tensor_scalar(nm.mean[:, :], nm.mean[:, :], 1.0 / D, None, ALU.mult))
    step(dve.tensor_tensor(nm.xn[:, :, :], x[:, :, :], over(nm.mean[:, :], D), ALU.subtract))
    step(dve.tensor_tensor(nm.sq[:, :, :], nm.xn[:, :, :], nm.xn[:, :, :], ALU.mult))
    step(dve.tensor_reduce(nm.var[:, :], nm.sq[:, :, :], X, ALU.add))
    dve.tensor_scalar(nm.var[:, :], nm.var[:, :], 1.0 / D, LN_EPS, ALU.mult, ALU.add).then_inc(nm.var_ready, 1)
    dve.wait_ge(nm.std_ready, 1)
    step(dve.reciprocal(nm.rstd[:, :], nm.std[:, :]))
    dve.tensor_tensor(nm.xn[:, :, :], nm.xn[:, :, :], over(nm.rstd[:, :], D), ALU.mult).then_inc(nm.ready, 1)


def norm_scalar(act, nm):
    act.wait_ge(nm.var_ready, 1)
    act.activation(nm.std[:, :], nm.var[:, :], ACT.Sqrt).then_inc(nm.std_ready, 1)


def load_ctx(eng, dst, src, sem):
    eng.dma_start(dst[:, 0:FULL, :], src[0:FULL * P, :].rearrange("(p j) c -> p j c", j=FULL)).then_inc(sem, 16)
    eng.dma_start(dst[0:TAIL, FULL, :], src[FULL * P:N_CTX, :]).then_inc(sem, 16)


def cross_attention_0(nc, io, x_tok, ident):
    NG = NT // 4
    NBUF = 4
    with ExitStack() as stack:
        m = Memory(nc, stack, "xa0")
        wq, wk, wv, wo = (m.sb(n, [P, D]) for n in ("wqT", "wk", "wvT", "woT"))
        bq, bk, bv = (m.sb(n, [P, 1]) for n in ("bq", "bk", "bv"))
        bo = m.sb("bo", [P, D])
        nm = Norm(m)
        xnT = m.sb("xnT", [P, NT * P])
        qT = m.sb("qT", [P, NT * P])
        fT = m.sb("fT", [P, NT * P])
        q_bk = m.sb("q_bk", [P, NT])
        ctx = [m.sb(f"ctx{u}", [P, 2, NCH, D]) for u in range(NBUF)]
        ctxT = m.sb("ctxT", [P, 2, N_CTX])
        fold = [m.sb(f"fold{u}", [P, P]) for u in range(2)]
        prob = m.sb("prob", [P, N_CTX])
        probT = m.sb("probT", [P, NCH, P])
        top = m.sb("top", [P, 1])
        shifted = m.sb("shifted", [P, 1])
        shift = m.sb("shift", [P, 1])
        total = m.sb("total", [P, 2])
        inv = m.sb("inv", [P, 1])
        att = m.sb("att", [P, NT, D])

        ps_s = m.psum("ps_s", [P, 4, 512])
        ps_t = m.psum("ps_t", [P, 2, 512])
        ps_o = m.psum("ps_o", [P, 512])
        ps_b = m.psum("ps_b", [P, 512])

        weights = m.sem("weights")
        ctx_loaded = [m.sem(f"ctx_loaded{u}") for u in range(NBUF)]
        chain = m.sem("vector_chain")
        turn_full = [m.sem(f"turn_full{i}") for i in range(2)]
        turn_free = [m.sem(f"turn_free{i}") for i in range(2)]
        q_bk_full = m.sem("q_bk_full")
        q_bk_ready = m.sem("q_bk_ready")
        fold_ready = m.sem("fold_ready")
        scores_full = m.sem("scores_full")
        shift_ready = m.sem("shift_ready")
        prob_ready = m.sem("prob_ready")
        attended = m.sem("attended")
        att_ready = m.sem("att_ready")
        bias_added = m.sem("bias_added")
        block = stack.enter_context(nc.Block())
        PAIR_TURNS = 3 * len(GROUPS)

        @block.sync
        def _(sp):
            for dst, src in ((wq, "L0_xattn_WqT"), (wk, "L0_xattn_Wk"), (wv, "L0_xattn_WvT"), (wo, "L0_xattn_WoT")):
                sp.dma_start(dst[:, :], io[src]).then_inc(weights, 16)
            for dst, src in ((bq, "L0_xattn_bq"), (bk, "L0_xattn_bk"), (bv, "L0_xattn_bv")):
                sp.dma_start(dst[:, :], io[src].rearrange("(p a) -> p a", a=1)).then_inc(weights, 16)
            sp.dma_start(bo[:, :], io["L0_xattn_bo"].rearrange("(a n) -> a n", a=1).broadcast_to([P, D])).then_inc(weights, 16)
            for u in range(NBUF):
                for b in range(2):
                    load_ctx(sp, ctx[u][:, b], io["ctx_1024"][2 * u + b], ctx_loaded[u])
            with sp.Fori(0, NT // NBUF - 1) as it:
                for u in range(NBUF):
                    sp.wait_ge(attended, it * NBUF + (u + 1))
                    for b in range(2):
                        load_ctx(sp, ctx[u][:, b], io["ctx_1024"][bass.ds(it * (2 * NBUF) + (2 * (NBUF + u) + b), 1)]
                                 .rearrange("a t c -> (a t) c"), ctx_loaded[u])

        def pairs(eng, enter, body, leave):
            with eng.Fori(0, NT // NBUF - 1) as it:
                enter(it)
                for u in range(NBUF):
                    body(it * NBUF + u, u, False)
                leave(NT // NBUF - 1)
            for u in range(NBUF):
                body(NT - NBUF + u, u, u == NBUF - 1)

        @block.gpsimd
        def _(pool):
            pool.wait_ge(turn_free[0], 6)
            pool.wait_ge(turn_free[1], 6)
            for u in range(2):
                pool.tensor_copy(fold[u][:, :], fT[:, u * P:(u + 1) * P]).then_inc(fold_ready, 1)
            with pool.Fori(0, NT // 2 - 1) as it:
                for u in range(2):
                    pool.wait_ge(scores_full, it * 2 + (u + 1))
                    pool.tensor_copy(fold[u][:, :], fT[:, bass.ds(it * (2 * P) + (2 + u) * P, P)]).then_inc(fold_ready, 1)
            pool.wait_ge(nm.ready, 1)
            pool.wait_ge(weights, 16 * 8)
            pool.tensor_tensor(x_tok[:, :, :], x_tok[:, :, :], under(bo[:, :], NT), ALU.add).then_inc(bias_added, 1)

        class Turns:

            def __init__(self):
                self.k = 0
                self.free = [Tally(s) for s in turn_free]

            def enter(self, it, per):
                for t in self.free:
                    t.enter(it, per // 2)

            def leave(self, times):
                for t in self.free:
                    t.leave(times)

        @block.tensor
        def _(pe):
            t = Turns()

            def turn(fill):
                i = t.k % 2
                if t.k >= 2:
                    pe.wait_ge(turn_free[i], t.free[i].value())
                t.free[i].next()
                fill(ps_t[:, i, :]).then_inc(turn_full[i], 1)
                t.k += 1

            def transposes(src):
                def fill(bank):
                    for c in range(4):
                        last = pe.transpose(bank[:, c * P:(c + 1) * P], src(c), ident[:, :])
                    return last
                return fill

            def project(w, src):
                return lambda bank: pe.matmul(bank, w[:, :], src, start=True, stop=True)

            pe.wait_ge(nm.ready, 1)
            for g in range(NG):
                turn(transposes(lambda c: nm.xn[:, 4 * g + c, :]))
            pe.wait_ge(weights, 16 * 8)
            for g in range(NG):
                pe.wait_ge(turn_free[g % 2], g // 2 + 1)
                turn(project(wq, xnT[:, g * 512:(g + 1) * 512]))
            for g in range(NG):
                pe.wait_ge(turn_free[g % 2], 2 + g // 2 + 1)
                turn(project(wk, qT[:, g * 512:(g + 1) * 512]))
            for n in range(NT):
                last = pe.matmul(ps_b[:, n:n + 1], qT[:, n * P:(n + 1) * P], bk[:, :], start=True, stop=True)
            last.then_inc(q_bk_full, 1)

            loaded = [Tally(s) for s in ctx_loaded]
            folded = Tally(fold_ready)
            done_p = Tally(prob_ready)

            def turn_ctx(u):
                pe.wait_ge(ctx_loaded[u], loaded[u].next(64))
                for b in range(2):
                    for chunks in GROUPS:
                        def fill(bank):
                            for j in chunks:
                                r = ROWS[j]
                                last = pe.transpose(bank[:, (j % 4) * P:(j % 4) * P + r],
                                                    ctx[u][0:r, b, j, :], ident[0:r, 0:r])
                            return last
                        turn(fill)

            def turn_probs():
                pe.wait_ge(prob_ready, done_p.next())
                for chunks in GROUPS:
                    def fill(bank):
                        for j in chunks:
                            r = ROWS[j]
                            c0 = chunks[0] * P + (j % 4) * P
                            last = pe.transpose(bank[0:r, (j % 4) * P:(j % 4 + 1) * P], prob[:, c0:c0 + r], ident[:, :])
                        return last
                    turn(fill)

            def scores(u):
                pe.wait_ge(fold_ready, folded.next())
                for c in range(0, N_CTX, 512):
                    w = min(512, N_CTX - c)
                    for b in range(2):
                        last = pe.matmul(ps_s[64 * b:64 * b + 64, c // 512, 0:w], fold[u % 2][:, 64 * b:64 * b + 64],
                                         ctxT[:, b, c:c + w], start=True, stop=True)
                last.then_inc(scores_full, 1)

            def wait_turned():
                for i in range(2):
                    pe.wait_ge(turn_free[i], t.free[i].value())

            def attend(n, u, last_pair):
                if not last_pair:
                    turn_ctx((u + 1) % NBUF)
                turn_probs()
                wait_turned()
                if not last_pair:
                    scores((u + 1) % NBUF)
                for j in range(NCH):
                    r = ROWS[j]
                    for b in range(2):
                        last = pe.matmul(ps_o[64 * b:64 * b + 64, 0:D], probT[0:r, j, 64 * b:64 * b + 64],
                                         ctx[u][0:r, b, j, :], start=(j == 0), stop=(j == NCH - 1))
                last.then_inc(attended, 1)

            def enter(it):
                t.enter(it, NBUF * PAIR_TURNS)
                for tally, per in ((folded, NBUF), (done_p, NBUF), *[(x, 64) for x in loaded]):
                    tally.enter(it, per)

            def leave(times):
                for tally in (t, folded, done_p, *loaded):
                    tally.leave(times)

            turn_ctx(0)
            wait_turned()
            scores(0)
            pairs(pe, enter, attend, leave)

            pe.wait_ge(att_ready, NT)
            base = [t.free[i].value() for i in range(2)]
            for g in range(NG):
                turn(transposes(lambda c: att[:, 4 * g + c, :]))
            for g in range(NG):
                pe.wait_ge(turn_free[g % 2], base[g % 2] + g // 2 + 1)
                cols = slice(g * 512, (g + 1) * 512)

                def fill(bank):
                    pe.matmul(bank, wv[:, :], fT[:, cols], start=True, stop=False)
                    return pe.matmul(bank, ident[:, :], xnT[:, cols], start=False, stop=True)
                turn(fill)
            pe.wait_ge(bias_added, 1)
            for g in range(NG):
                pe.wait_ge(turn_free[g % 2], base[g % 2] + 2 + g // 2 + 1)

                def fill(bank):
                    pe.matmul(bank, ident[:, :], x_tok[:, 4 * g:4 * g + 4, :].rearrange("p n d -> p (n d)"),
                              start=True, stop=False, skip_group_check=True)
                    for c in range(4):
                        n = 4 * g + c
                        last = pe.matmul(bank[:, c * P:(c + 1) * P], qT[:, n * P:(n + 1) * P], wo[:, :],
                                         start=False, stop=(c == 3), skip_group_check=True)
                    return last
                turn(fill)

        def empty(eng, t, i, out_of):
            eng.wait_ge(turn_full[i], t.next())
            out_of(ps_t[:, i, :]).then_inc(turn_free[i], 1)

        def common(eng, i, copy, add, mid_q, softmax, finish, enter, leave):
            full = Tally(turn_full[i])
            for g in range(i, NG, 2):
                empty(eng, full, i, lambda bank: copy(xnT[:, g * 512:(g + 1) * 512], bank))
            eng.wait_ge(weights, 16 * 8)
            for g in range(i, NG, 2):
                empty(eng, full, i, lambda bank: add(qT[:, g * 512:(g + 1) * 512], bank, bq))
            for g in range(i, NG, 2):
                empty(eng, full, i, lambda bank: copy(fT[:, g * 512:(g + 1) * 512], bank))
            mid_q()

            def take_ctx():
                k = 0
                for b in range(2):
                    for chunks in GROUPS:
                        c0 = chunks[0] * P
                        w = sum(ROWS[j] for j in chunks)
                        if k % 2 == i:
                            empty(eng, full, i, lambda bank: copy(ctxT[:, b, c0:c0 + w], bank[:, 0:w]))
                        k += 1

            def take_probs():
                for k, chunks in enumerate(GROUPS):
                    r = ROWS[chunks[0]]
                    w = len(chunks)
                    if k % 2 == i:
                        empty(eng, full, i, lambda bank: copy(probT[0:r, chunks[0]:chunks[0] + w, :],
                                                              bank[0:r, 0:w * P].rearrange("p (j q) -> p j q", j=w)))

            def body(n, u, last):
                if not last:
                    take_ctx()
                take_probs()
                if not last:
                    softmax(n + 1, (u + 1) % 2)
                finish(n, u % 2)

            take_ctx()
            softmax(0, 0)
            pairs(eng, lambda it: enter(full, it), body, lambda times: leave(full, times))
            for g in range(i, NG, 2):
                empty(eng, full, i, lambda bank: copy(fT[:, g * 512:(g + 1) * 512], bank))
            for g in range(i, NG, 2):
                empty(eng, full, i, lambda bank: add(qT[:, g * 512:(g + 1) * 512], bank, bv))
            for g in range(i, NG, 2):
                empty(eng, full, i, lambda bank: copy(x_tok[:, 4 * g:4 * g + 4, :].rearrange("p n d -> p (n d)"), bank))

        @block.scalar
        def _(act):
            norm_scalar(act, nm)

            def copy(dst, src):
                return act.activation(dst, src, ACT.Copy)

            def add(dst, src, bias):
                return act.activation(dst, src, ACT.Identity, bias=bias[:, 0:1])

            def softmax(n, u):
                act.wait_ge(shift_ready, n + 1)
                act.activation(prob[:, :], ps_s[:, :, :].rearrange("p a b -> p (a b)")[:, 0:N_CTX], ACT.Exp,
                               bias=shift[:, 0:1], scale=float(D) ** -0.5,
                               accum_out=total[:, u:u + 1]).then_inc(prob_ready, 1)

            common(act, 1, copy, add, lambda: None, softmax, lambda n, u: None,
                   lambda full, it: full.enter(it, NBUF * PAIR_TURNS // 2), lambda full, times: full.leave(times))

        @block.vector
        def _(dve):
            link = Tally(chain)

            def step(ins):
                ins.then_inc(chain, 1)
                dve.wait_ge(chain, link.next())

            norm_vector(dve, nm, x_tok, link)

            def copy(dst, src):
                return dve.tensor_copy(dst, src)

            def add(dst, src, bias):
                return dve.tensor_scalar(dst, src, bias[:, 0:1], None, ALU.add)

            def mid_q():
                dve.wait_ge(q_bk_full, 1)
                dve.tensor_copy(q_bk[:, :], ps_b[:, 0:NT]).then_inc(q_bk_ready, 1)
                dve.wait_ge(q_bk_ready, 1)

            def softmax(n, u):
                dve.wait_ge(scores_full, n + 1)
                step(dve.tensor_reduce(top[:, :], ps_s[:, :, :].rearrange("p a b -> p (a b)")[:, 0:N_CTX], X, ALU.max))
                step(dve.tensor_tensor(shifted[:, :], top[:, :], q_bk[:, bass.ds(n, 1)], ALU.add))
                step(dve.tensor_tensor(shift[:, :], q_bk[:, bass.ds(n, 1)], shifted[:, :], ALU.subtract))
                dve.tensor_scalar(shift[:, :], shift[:, :], float(D) ** -0.5, None, ALU.mult).then_inc(shift_ready, 1)

            def finish(n, u):
                dve.wait_ge(attended, n + 1)
                step(dve.reciprocal(inv[:, :], total[:, u:u + 1]))
                dve.tensor_scalar(att[:, bass.ds(n, 1), :].rearrange("p a d -> p (a d)"), ps_o[:, 0:D], inv[:, 0:1], None,
                                  ALU.mult).then_inc(att_ready, 1)

            def enter(full, it):
                full.enter(it, NBUF * PAIR_TURNS // 2)
                link.enter(it, 4 * NBUF)

            def leave(full, times):
                full.leave(times)
                link.leave(times)

            common(dve, 0, copy, add, mid_q, softmax, finish, enter, leave)


NG = 4
GT = NT // NG
GB = 2 * GT
GC = GT * P


def flat(ap):
    return ap.rearrange("p a b -> p (a b)")


class Lane:

    def __init__(self, m, name, banks=2):
        self.banks = banks
        self.ps = m.psum(name, [P, banks, 512])
        self.full = m.sem(name + "_full")
        self.free = m.sem(name + "_free")


class Fill:

    def __init__(self, pe, lane):
        self.pe, self.lane, self.k, self.t = pe, lane, 0, Tally(lane.free)

    def __call__(self, matmuls):
        self.pe.wait_ge(self.lane.free, self.t.next())
        matmuls(self.lane.ps[:, self.k % self.lane.banks, :]).then_inc(self.lane.full, 1)
        self.k += 1

    def wait_emptied(self):
        self.pe.wait_ge(self.lane.free, self.t.value() + self.lane.banks)

    def enter(self, it, per):
        assert per % self.lane.banks == 0
        self.t.enter(it, per)

    def leave(self, times):
        self.t.leave(times)


class Take:

    def __init__(self, eng, lane):
        self.eng, self.lane, self.k, self.t = eng, lane, 0, Tally(lane.full)

    def __call__(self, out_of):
        self.eng.wait_ge(self.lane.full, self.t.next())
        out_of(self.lane.ps[:, self.k % self.lane.banks, :]).then_inc(self.lane.free, 1)
        self.k += 1

    def wait_taken(self):
        self.eng.wait_ge(self.lane.free, self.t.value() + self.lane.banks)

    def enter(self, it, per):
        self.t.enter(it, per)

    def leave(self, times):
        self.t.leave(times)


class Chain:

    def __init__(self, eng, sem):
        self.eng, self.sem, self.t = eng, sem, Tally(sem)

    def __call__(self, ins):
        ins.then_inc(self.sem, 1)
        self.eng.wait_ge(self.sem, self.t.next())

    def enter(self, it, per):
        self.t.enter(it, per)

    def leave(self, times):
        self.t.leave(times)


class GroupNorm:

    def __init__(self, m):
        self.xn = m.sb("xn", [P, GT, D])
        self.sq = m.sb("xn_sq", [P, GT, D])
        self.mean, self.var, self.std, self.rstd = (m.sb("ln_" + n, [P, GT]) for n in ("mean", "var", "std", "rstd"))
        self.var_ready, self.std_ready, self.ready = (m.sem("ln_" + n) for n in ("var_ready", "std_ready", "ready"))

    STEPS = 6

    def vector(self, dve, x, step, it):
        step(dve.tensor_reduce(self.mean[:, :], x, X, ALU.add))
        step(dve.tensor_scalar(self.mean[:, :], self.mean[:, :], 1.0 / D, None, ALU.mult))
        step(dve.tensor_tensor(self.xn[:, :, :], x, over(self.mean[:, :], D), ALU.subtract))
        step(dve.tensor_tensor(self.sq[:, :, :], self.xn[:, :, :], self.xn[:, :, :], ALU.mult))
        step(dve.tensor_reduce(self.var[:, :], self.sq[:, :, :], X, ALU.add))
        dve.tensor_scalar(self.var[:, :], self.var[:, :], 1.0 / D, LN_EPS, ALU.mult, ALU.add).then_inc(self.var_ready, 1)
        dve.wait_ge(self.std_ready, it + 1)
        step(dve.reciprocal(self.rstd[:, :], self.std[:, :]))
        dve.tensor_tensor(self.xn[:, :, :], self.xn[:, :, :], over(self.rstd[:, :], D), ALU.mult).then_inc(self.ready, 1)

    def scalar(self, act, it):
        act.wait_ge(self.var_ready, it + 1)
        act.activation(self.std[:, :], self.var[:, :], ACT.Sqrt).then_inc(self.std_ready, 1)


class AheadNorm:

    def __init__(self, m):
        self.xn = m.sb("xn", [P, GT, D])
        self.copy, self.sq = m.sb("ln_copy", [P, GT, D]), m.sb("ln_sq", [P, GT, D])
        self.total, self.shift, self.var, self.std, self.rstd = (m.sb("ln_" + n, [P, GT]) for n in
                                                                 ("total", "shift", "var", "std", "rstd"))
        self.total_ready, self.shift_ready, self.sq_ready, self.var_ready, self.std_ready, self.ready = (
            m.sem("ln_" + n) for n in ("total_ready", "shift_ready", "sq_ready", "var_ready", "std_ready", "ready"))

    STEPS = 1

    def vector(self, dve, x, step, it):
        dve.wait_ge(self.total_ready, it * GT + GT)
        dve.tensor_scalar(self.shift[:, :], self.total[:, :], -1.0 / D, None, ALU.mult).then_inc(self.shift_ready, 1)
        dve.wait_ge(self.sq_ready, it * GT + GT)
        dve.tensor_scalar(self.var[:, :], self.var[:, :], 1.0 / D, LN_EPS, ALU.mult, ALU.add).then_inc(self.var_ready, 1)
        dve.wait_ge(self.std_ready, it + 1)
        step(dve.reciprocal(self.rstd[:, :], self.std[:, :]))
        for c in range(GT):
            dve.tensor_scalar(self.xn[:, c, :], x[:, c, :], self.shift[:, c:c + 1], self.rstd[:, c:c + 1], ALU.add,
                              ALU.mult).then_inc(self.ready, 1)

    def scalar(self, act, x, it):
        for c in range(GT):
            act.activation(self.copy[:, c, :], x[:, c, :], ACT.Copy, accum_out=self.total[:, c:c + 1]).then_inc(self.total_ready, 1)
        act.wait_ge(self.shift_ready, it + 1)
        for c in range(GT):
            act.activation(self.sq[:, c, :], self.copy[:, c, :], ACT.Square, bias=self.shift[:, c:c + 1],
                           accum_out=self.var[:, c:c + 1]).then_inc(self.sq_ready, 1)
        act.wait_ge(self.var_ready, it + 1)
        act.activation(self.std[:, :], self.var[:, :], ACT.Sqrt).then_inc(self.std_ready, 1)


def groups(eng, enter, body, leave):
    with eng.Fori(0, NG - 1) as it:
        enter(it)
        body(it, False)
        leave(NG - 1)
    body(NG - 1, True)


def load_row(eng, dst, src, sem):
    eng.dma_start(dst, src.rearrange("(a n) -> a n", a=1).broadcast_to([P, src.shape[0]])).then_inc(sem, 16)


def linear_attention_0(nc, io, x_tok, ident):
    with ExitStack() as stack:
        m = Memory(nc, stack, "la0")
        wqkv = m.sb("wqkv", [P, 3, D])
        bqkv = m.sb("bqkv", [P, 3, D])
        wo = m.sb("wo", [P, D])
        bo = m.sb("bo", [P, D])
        rope = m.sb("rope", [P, 2, HD])
        own = m.sb("own", [P, D])
        nm = GroupNorm(m)
        xb = m.sb("xb", [P, GT, D])
        xnT = m.sb("xnT", [P, GC])
        qkv = m.sb("qkv", [P, GT, 3 * D])
        cross = m.sb("cross", [P, GT, 2 * D])
        rot = m.sb("rot", [P, GT, 2 * D])
        qT = m.sb("qT", [P, GC])
        kv = m.sb("kv", [P, 2, GT, D])
        ctxT = m.sb("ctxT", [P, GC])
        scratch = m.sb("scratch", [P, 2])
        vl = Lane(m, "vector_lane")
        sl = Lane(m, "scalar_lane")
        consts = m.sem("consts")
        chain = m.sem("vector_chain")
        xb_ready = m.sem("xb_ready")
        rotated = m.sem("rotated")
        block = stack.enter_context(nc.Block())
        N_CONSTS = 10

        def group(it):
            return x_tok[:, bass.ds(it * GT, GT), :]

        @block.sync
        def _(sp):
            for i, n in enumerate("qkv"):
                sp.dma_start(wqkv[:, i, :], io["L0_attn_W" + n]).then_inc(consts, 16)
                load_row(sp, bqkv[:, i, :], io["L0_attn_b" + n], consts)
            sp.dma_start(wo[:, :], io["L0_attn_Wo"]).then_inc(consts, 16)
            load_row(sp, bo[:, :], io["L0_attn_bo"], consts)
            sp.dma_start(rope[:, :, :], io["rope"]).then_inc(consts, 16)
            sp.dma_start(own[:, :], io["own_head_scaled"]).then_inc(consts, 16)

        @block.gpsimd
        def _(pool):
            pool.wait_ge(consts, 16 * N_CONSTS)
            pool.tensor_tensor(xb[:, :, :], x_tok[:, 0:GT, :], under(bo[:, :], GT), ALU.add).then_inc(xb_ready, 1)
            with pool.Fori(0, NG - 1) as it:
                pool.wait_ge(sl.free, it * 4 + (4 + sl.banks))
                pool.tensor_tensor(xb[:, :, :], group(it + 1), under(bo[:, :], GT), ALU.add).then_inc(xb_ready, 1)

        @block.tensor
        def _(pe):
            v, s = Fill(pe, vl), Fill(pe, sl)
            pe.wait_ge(consts, 16 * N_CONSTS)
            with pe.Fori(0, NG) as it:
                v.enter(it, GT + 2)
                s.enter(it, 4)
                pe.wait_ge(nm.ready, it + 1)

                def turn(src):
                    def fill(bank):
                        for c in range(GT):
                            last = pe.transpose(bank[:, c * P:(c + 1) * P], src(c), ident[:, :])
                        return last
                    return fill

                s(turn(lambda c: nm.xn[:, c, :]))
                s.wait_emptied()
                for c in range(GT):
                    v(lambda bank: pe.matmul(bank[:, 0:3 * D], xnT[:, c * P:(c + 1) * P], flat(wqkv[:, :, :]),
                                             start=True, stop=True))
                pe.wait_ge(rotated, it + 1)
                s(turn(lambda c: rot[:, c, 0:D]))
                for u in range(2):
                    def fill(bank):
                        for c in range(GT):
                            rows = slice(64 * u, 64 * u + 64)
                            last = pe.matmul(bank[:, c * D:(c + 1) * D], rot[rows, c, D:2 * D], qkv[rows, c, 2 * D:3 * D],
                                             start=True, stop=True)
                        return last
                    v(fill)
                s.wait_emptied()
                v.wait_emptied()

                def fill(bank):
                    for c in range(GT):
                        for u in range(2):
                            t0 = c * P + 64 * u
                            last = pe.matmul(bank[:, t0:t0 + 64], kv[:, u, c, :], qT[:, t0:t0 + 64], start=True, stop=True)
                    return last
                s(fill)
                s.wait_emptied()
                pe.wait_ge(xb_ready, it + 1)

                def fill(bank):
                    pe.matmul(bank, ident[:, :], flat(xb[:, :, :]), start=True, stop=False, skip_group_check=True)
                    for c in range(GT):
                        last = pe.matmul(bank[:, c * D:(c + 1) * D], ctxT[:, c * P:(c + 1) * P], wo[:, :],
                                         start=False, stop=(c == GT - 1), skip_group_check=True)
                    return last
                s(fill)
                v.leave(NG)
                s.leave(NG)

        @block.scalar
        def _(act):
            take = Take(act, sl)
            act.wait_ge(consts, 16 * N_CONSTS)
            for _ in range(sl.banks):
                act.activation(scratch[:, 0:1], ident[:, 0:1], ACT.Copy).then_inc(sl.free, 1)
                act.wait_ge(sl.free, _ + 1)
            with act.Fori(0, NG) as it:
                take.enter(it, 4)
                nm.scalar(act, it)
                take(lambda bank: act.activation(xnT[:, :], bank, ACT.Copy))
                take(lambda bank: act.activation(qT[:, :], bank, ACT.Copy))
                take(lambda bank: act.activation(ctxT[:, :], bank, ACT.Copy))
                take(lambda bank: act.activation(group(it), bank.rearrange("p (c d) -> p c d", c=GT), ACT.Copy))
                take.leave(NG)

        @block.vector
        def _(dve):
            take, step = Take(dve, vl), Chain(dve, chain)
            for _ in range(vl.banks):
                dve.memset(scratch[:, 1:2], 0.0).then_inc(vl.free, 1)
                dve.wait_ge(vl.free, _ + 1)
            dve.wait_ge(consts, 16 * N_CONSTS)
            with dve.Fori(0, NG) as it:
                step.enter(it, nm.STEPS + 3)
                take.enter(it, GT + 2)
                nm.vector(dve, group(it), step, it)
                for c in range(GT):
                    take(lambda bank: dve.tensor_tensor(qkv[:, c, :], bank[:, 0:3 * D], flat(bqkv[:, :, :]), ALU.add))
                take.wait_taken()
                qk = qkv[:, :, 0:2 * D].rearrange("p c (m i two) -> p c m i two", i=HD // 2, two=2)
                cr = cross[:, :, :].rearrange("p c (m i two) -> p c m i two", i=HD // 2, two=2)
                sin = rope[:, 1, :].rearrange("p (i two) -> p i two", two=2)
                dims = [P, GT, 2 * H, HD // 2]
                for part in range(2):
                    last = dve.tensor_tensor(cr[:, :, :, :, part], qk[:, :, :, :, 1 - part],
                                             sin[:, :, part].unsqueeze(1).unsqueeze(1).broadcast_to(dims), ALU.mult)
                    if part == 0:
                        last.then_inc(chain, 1)
                        step.t.next()
                    else:
                        step(last)
                step(dve.tensor_tensor(rot[:, :, :].rearrange("p c (m e) -> p c m e", e=HD),
                                       qkv[:, :, 0:2 * D].rearrange("p c (m e) -> p c m e", e=HD),
                                       rope[:, 0, :].unsqueeze(1).unsqueeze(1).broadcast_to([P, GT, 2 * H, HD]), ALU.mult))
                dve.tensor_tensor(rot[:, :, :], rot[:, :, :], cross[:, :, :], ALU.add).then_inc(rotated, 1)
                for u in range(2):
                    take(lambda bank: dve.tensor_tensor(kv[:, u, :, :], bank.rearrange("p (c d) -> p c d", c=GT),
                                                        under(own[:, :], GT), ALU.mult))
                take.leave(NG)
                step.leave(NG)


def linear_attention_1(nc, io, x_tok, ident):
    with ExitStack() as stack:
        m = Memory(nc, stack, "la1")
        wqkv = m.sb("wqkv", [P, 3 * D])
        wo = m.sb("wo", [P, D])
        bo = m.sb("bo", [P, D])
        gain = m.sb("gain", [P, H])
        offset = m.sb("offset", [P, H])
        own = m.sb("own", [P, D])
        ones = m.sb("ones", [P, 64])
        nm = GroupNorm(m)
        xb = m.sb("xb", [P, GT, D])
        xnT = m.sb("xnT", [P, GC])
        qkv = m.sb("qkv", [P, GT, 3 * D])
        qT = m.sb("qT", [P, GC])
        gram = m.sb("gram", [P, 2, GT, 2 * D])
        y = m.sb("y", [P, GT, 3 * D])
        prod = m.sb("prod", [P, GT, D])
        square, length, ratio = (m.sb(n, [P, GT * H]) for n in ("square", "length", "ratio"))
        att = m.sb("att", [P, GT, D])
        attT = m.sb("attT", [P, GC])
        scratch = m.sb("scratch", [P, 2])
        vl = Lane(m, "vector_lane")
        sl = Lane(m, "scalar_lane")
        consts = m.sem("consts")
        chain = m.sem("vector_chain")
        xb_ready = m.sem("xb_ready")
        square_ready = m.sem("square_ready")
        length_ready = m.sem("length_ready")
        att_ready = m.sem("att_ready")
        block = stack.enter_context(nc.Block())
        N_CONSTS = 6
        VT, ST = 3 * GT, 4

        def group(it):
            return x_tok[:, bass.ds(it * GT, GT), :]

        @block.sync
        def _(sp):
            sp.dma_start(wqkv[:, :], io["L1_attn_w_qkvT"]).then_inc(consts, 16)
            sp.dma_start(wo[:, :], io["L1_attn_w_outT"]).then_inc(consts, 16)
            load_row(sp, bo[:, :], io["L1_attn_b_out"], consts)
            load_row(sp, gain[:, :], io["L1_attn_norm_g"].rearrange("a h b c -> (a h b c)"), consts)
            load_row(sp, offset[:, :], io["L1_attn_norm_b"].rearrange("a h b c -> (a h b c)"), consts)
            sp.dma_start(own[:, :], io["own_head"]).then_inc(consts, 16)

        @block.gpsimd
        def _(pool):
            pool.wait_ge(consts, 16 * N_CONSTS)
            pool.tensor_tensor(xb[:, :, :], x_tok[:, 0:GT, :], under(bo[:, :], GT), ALU.add).then_inc(xb_ready, 1)
            with pool.Fori(0, NG - 1) as it:
                pool.wait_ge(sl.free, it * ST + (ST + sl.banks))
                pool.tensor_tensor(xb[:, :, :], group(it + 1), under(bo[:, :], GT), ALU.add).then_inc(xb_ready, 1)

        @block.tensor
        def _(pe):
            v, s = Fill(pe, vl), Fill(pe, sl)
            pe.wait_ge(consts, 16 * N_CONSTS)
            with pe.Fori(0, NG) as it:
                v.enter(it, VT)
                s.enter(it, ST)
                pe.wait_ge(nm.ready, it + 1)

                def turn(src):
                    def fill(bank):
                        for c in range(GT):
                            last = pe.transpose(bank[:, c * P:(c + 1) * P], src(c), ident[:, :])
                        return last
                    return fill

                s(turn(lambda c: nm.xn[:, c, :]))
                s.wait_emptied()
                for c in range(GT):
                    v(lambda bank: pe.matmul(bank[:, 0:3 * D], xnT[:, c * P:(c + 1) * P], wqkv[:, :], start=True, stop=True))
                v.wait_emptied()
                s(turn(lambda c: qkv[:, c, 0:D]))
                for u in range(2):
                    for half in range(2):
                        def fill(bank):
                            rows = slice(64 * u, 64 * u + 64)
                            for i in range(GT // 2):
                                c = half * (GT // 2) + i
                                last = pe.matmul(bank[:, i * 2 * D:(i + 1) * 2 * D], qkv[rows, c, D:2 * D],
                                                 qkv[rows, c, D:3 * D], start=True, stop=True)
                            return last
                        v(fill)
                s.wait_emptied()
                v.wait_emptied()
                for c in range(GT):
                    def fill(bank):
                        for u in range(2):
                            rows = slice(64 * u, 64 * u + 64)
                            pe.matmul(bank[rows, 0:2 * D], qT[:, c * P + 64 * u:c * P + 64 * u + 64], gram[:, u, c, :],
                                      start=True, stop=True)
                        for u in range(2):
                            rows = slice(64 * u, 64 * u + 64)
                            last = pe.matmul(bank[rows, 2 * D:3 * D], ones[rows, :], qkv[rows, c, 2 * D:3 * D],
                                             start=True, stop=True)
                        return last
                    v(fill)
                pe.wait_ge(att_ready, it + 1)
                s(turn(lambda c: att[:, c, :]))
                s.wait_emptied()
                pe.wait_ge(xb_ready, it + 1)

                def fill(bank):
                    pe.matmul(bank, ident[:, :], flat(xb[:, :, :]), start=True, stop=False, skip_group_check=True)
                    for c in range(GT):
                        last = pe.matmul(bank[:, c * D:(c + 1) * D], attT[:, c * P:(c + 1) * P], wo[:, :],
                                         start=False, stop=(c == GT - 1), skip_group_check=True)
                    return last
                s(fill)
                v.leave(NG)
                s.leave(NG)

        @block.scalar
        def _(act):
            take = Take(act, sl)
            for _ in range(sl.banks):
                act.activation(scratch[:, 0:1], ident[:, 0:1], ACT.Copy).then_inc(sl.free, 1)
                act.wait_ge(sl.free, _ + 1)
            with act.Fori(0, NG) as it:
                take.enter(it, ST)
                nm.scalar(act, it)
                take(lambda bank: act.activation(xnT[:, :], bank, ACT.Copy))
                take(lambda bank: act.activation(qT[:, :], bank, ACT.Copy))
                act.wait_ge(square_ready, it + 1)
                act.activation(length[:, :], square[:, :], ACT.Sqrt).then_inc(length_ready, 1)
                take(lambda bank: act.activation(attT[:, :], bank, ACT.Copy))
                take(lambda bank: act.activation(group(it), bank.rearrange("p (c d) -> p c d", c=GT), ACT.Copy))
                take.leave(NG)

        @block.vector
        def _(dve):
            take, step = Take(dve, vl), Chain(dve, chain)
            for _ in range(vl.banks):
                dve.memset(ones[:, :], 1.0).then_inc(vl.free, 1)
                dve.wait_ge(vl.free, _ + 1)
            dve.wait_ge(consts, 16 * N_CONSTS)
            with dve.Fori(0, NG) as it:
                step.enter(it, nm.STEPS + 7)
                take.enter(it, VT)
                nm.vector(dve, group(it), step, it)
                for c in range(GT):
                    take(lambda bank: dve.tensor_copy(qkv[:, c, :], bank[:, 0:3 * D]))
                for u in range(2):
                    for half in range(2):
                        c0 = half * (GT // 2)
                        take(lambda bank: dve.tensor_tensor(
                            gram[:, u, c0:c0 + GT // 2, :].rearrange("p c (k d) -> p (c k) d", k=2),
                            bank.rearrange("p (c d) -> p c d", c=4), under(own[:, :], 4), ALU.mult))
                for c in range(GT):
                    take(lambda bank: dve.tensor_copy(y[:, c, :], bank[:, 0:3 * D]))
                take.wait_taken()

                def heads(ap):
                    return ap.rearrange("p c (h d) -> p c h d", d=HD)

                step(dve.tensor_tensor(prod[:, :, :], qkv[:, :, 0:D], y[:, :, 0:D], ALU.mult))
                step(dve.tensor_reduce(square[:, :], heads(prod[:, :, :]), X, ALU.add))
                dve.tensor_scalar(square[:, :], square[:, :], 0.0, None, ALU.max).then_inc(square_ready, 1)
                dve.wait_ge(length_ready, it + 1)
                step(dve.tensor_scalar(length[:, :], length[:, :], 1e-12, None, ALU.max))
                step(dve.reciprocal(ratio[:, :], length[:, :]))
                step(dve.tensor_tensor(ratio[:, :].rearrange("p (c h) -> p c h", h=H),
                                       ratio[:, :].rearrange("p (c h) -> p c h", h=H), under(gain[:, :], GT), ALU.mult))
                step(dve.tensor_tensor(heads(prod[:, :, :]), heads(y[:, :, D:2 * D]),
                                       ratio[:, :].rearrange("p (c h) -> p c h", h=H).unsqueeze(3)
                                       .broadcast_to([P, GT, H, HD]), ALU.mult))
                step(dve.tensor_tensor(heads(att[:, :, :]), heads(y[:, :, 2 * D:3 * D]),
                                       offset[:, :].unsqueeze(1).unsqueeze(3).broadcast_to([P, GT, H, HD]), ALU.mult))
                dve.tensor_tensor(att[:, :, :], att[:, :, :], prod[:, :, :], ALU.add).then_inc(att_ready, 1)
                take.leave(NG)
                step.leave(NG)


E = 8
FF = 512


def first_of_largest(dve, step, score, rank, top, hit, order):
    sh = [P, GT, E]
    step(dve.tensor_reduce(top[:, :], score, X, ALU.max))
    step(dve.tensor_tensor(hit, score, top[:, :].unsqueeze(2).broadcast_to(sh), ALU.is_equal))
    step(dve.tensor_tensor(hit, hit, under(rank[:, :], GT), ALU.mult))
    step(dve.tensor_reduce(order[:, :], hit, X, ALU.max))
    step(dve.tensor_tensor(hit, hit, order[:, :].unsqueeze(2).broadcast_to(sh), ALU.is_equal))


def moe_top1(nc, io, x_tok, ident):
    NF = FF // P
    with ExitStack() as stack:
        m = Memory(nc, stack, "moe1")
        gate = m.sb("gate", [P, E])
        w1 = m.sb("w1", [P, E, FF])
        b1 = m.sb("b1", [P, E * NF])
        w2 = m.sb("w2", [P, E * NF, D])
        b2 = m.sb("b2", [E, D])
        rank = m.sb("rank", [P, E])
        nm = AheadNorm(m)
        xnT = m.sb("xnT", [P, GC])
        logits = m.sb("logits", [P, GT, E])
        probs = m.sb("probs", [P, GT, E])
        hit = m.sb("hit", [P, GT, E])
        top, total, order = (m.sb(n, [P, GT]) for n in ("top", "total", "order"))
        share = m.sb("share", [P, GT, E])
        shareT = m.sb("shareT", [E, GC])
        hidden = m.sb("hidden", [P, 2, NF, GC])
        acc = m.sb("acc", [P, 2, GT, D])
        scratch = m.sb("scratch", [P, 2])
        vl = Lane(m, "vector_lane")
        sl = Lane(m, "scalar_lane")
        consts = m.sem("consts")
        w_loaded = m.sem("w_loaded")
        chain = m.sem("vector_chain")
        logits_ready = m.sem("logits_ready")
        probs_ready = m.sem("probs_ready")
        share_ready = m.sem("share_ready")
        block = stack.enter_context(nc.Block())
        N_CONSTS = 3
        V_ORDER = ["first"] + [f"down{e}" for e in range(E - 1)] + ["logits", f"down{E - 1}"]
        VT, ST = len(V_ORDER), 2 + E * NF

        def group(it):
            return x_tok[:, GT * it:GT * (it + 1), :] if isinstance(it, int) else x_tok[:, bass.ds(it * GT, GT), :]

        @block.sync
        def _(sp):
            sp.dma_start(gate[:, :], io["L1_ffn_gate_wT"]).then_inc(consts, 16)
            sp.dma_start(rank[:, :], io["rank"]).then_inc(consts, 16)
            sp.dma_start(b2[:, :], io["L1_ffn_b2"]).then_inc(consts, 16)
            sp.dma_start(b1[:, :], io["L1_ffn_b1T"]).then_inc(w_loaded, 16)
            sp.dma_start(w1[:, :, :], io["L1_ffn_w1"].rearrange("e c f -> c e f")).then_inc(w_loaded, 16)
            sp.dma_start(w2[:, :, :], io["L1_ffn_w2"].rearrange("e (f p) d -> p (e f) d", p=P)).then_inc(w_loaded, 16)

        @block.tensor
        def _(pe):
            v, s = Fill(pe, vl), Fill(pe, sl)
            pe.wait_ge(consts, 16 * N_CONSTS)
            pe.wait_ge(w_loaded, 48)

            def turn(src, rows=P):
                def fill(bank):
                    for c in range(GT):
                        last = pe.transpose(bank[0:rows, c * P:(c + 1) * P], src(c), ident[:, :])
                    return last
                return fill

            def turn_xn(it):
                pe.wait_ge(nm.ready, it * GT + GT)
                s(turn(lambda c: nm.xn[:, c, :]))

            def take_logits():
                s.wait_emptied()

                def fill(bank):
                    for c in range(GT):
                        last = pe.matmul(bank[:, c * E:(c + 1) * E], xnT[:, c * P:(c + 1) * P], gate[:, :],
                                         start=True, stop=True)
                    return last
                v(fill)

            def up(e):
                for f in range(NF):
                    s(lambda bank: pe.matmul(bank, w1[:, e, f * P:(f + 1) * P], xnT[:, :], start=True, stop=True))
                return s.t.value() + sl.banks

            def down(e, hidden_ready):
                pe.wait_ge(sl.free, hidden_ready)

                def fill(bank):
                    for c in range(GT):
                        for f in range(NF):
                            last = pe.matmul(bank[:, c * D:(c + 1) * D], hidden[:, e % 2, f, c * P:(c + 1) * P],
                                             w2[:, e * NF + f, :], start=(f == 0), stop=(f == NF - 1))
                    return last
                v(fill)

            def group_products(it, is_last):
                hidden_ready = [up(0), up(1)]
                pe.wait_ge(share_ready, it + 1)
                s(turn(lambda c: share[:, c, :], E))
                s.wait_emptied()

                def fill(bank):
                    pe.matmul(bank, ident[:, :], group(it).rearrange("p c d -> p (c d)"),
                              start=True, stop=False, skip_group_check=True)
                    for c in range(GT):
                        last = pe.matmul(bank[:, c * D:(c + 1) * D], shareT[:, c * P:(c + 1) * P], b2[:, :],
                                         start=False, stop=(c == GT - 1), skip_group_check=True)
                    return last
                v(fill)
                for e in range(E - 2):
                    down(e, hidden_ready[e])
                    hidden_ready.append(up(e + 2))
                if is_last:
                    down(E - 2, hidden_ready[E - 2])
                else:
                    turn_xn(it + 1)
                    down(E - 2, hidden_ready[E - 2])
                    take_logits()
                down(E - 1, hidden_ready[E - 1])

            turn_xn(0)
            take_logits()

            def enter(it):
                v.enter(it, VT)
                s.enter(it, ST)

            def leave(n):
                v.leave(n)
                s.leave(n)

            groups(pe, enter, group_products, leave)

        @block.scalar
        def _(act):
            take = Take(act, sl)
            for _ in range(sl.banks):
                act.activation(scratch[:, 0:1], ident[:, 0:1], ACT.Copy).then_inc(sl.free, 1)
                act.wait_ge(sl.free, _ + 1)
            act.wait_ge(w_loaded, 48)

            def up(it, e, after_2=lambda: None):
                for f in range(NF):
                    if f == 0 and e >= 2:
                        act.wait_ge(vl.full, it * VT + (1 + V_ORDER.index(f"down{e - 2}") + 1))
                    take(lambda bank: act.activation(hidden[:, e % 2, f, :], bank, ACT.Relu,
                                                     bias=b1[:, e * NF + f:e * NF + f + 1]))
                    if f == 1:
                        after_2()

            def take_xn():
                take(lambda bank: act.activation(xnT[:, :], bank, ACT.Copy))

            def group_steps(it, is_last):
                def exps():
                    act.wait_ge(logits_ready, it + 1)
                    act.activation(probs[:, :, :], logits[:, :, :], ACT.Exp).then_inc(probs_ready, 1)

                up(it, 0, exps)
                up(it, 1)
                take(lambda bank: act.activation(shareT[:, :], bank[0:E, :], ACT.Copy))
                for e in range(2, E):
                    up(it, e)
                    if e == 4 and not is_last:
                        nm.scalar(act, group(it + 1), it + 1)
                if not is_last:
                    take_xn()

            nm.scalar(act, group(0), 0)
            take_xn()
            groups(act, lambda it: take.enter(it, ST), group_steps, take.leave)

        @block.vector
        def _(dve):
            take, step = Take(dve, vl), Chain(dve, chain)
            for _ in range(vl.banks):
                dve.memset(scratch[:, 1:2], 0.0).then_inc(vl.free, 1)
                dve.wait_ge(vl.free, _ + 1)
            dve.wait_ge(consts, 16 * N_CONSTS)

            def take_logits():
                take(lambda bank: dve.tensor_copy(logits[:, :, :], bank[:, 0:GT * E].rearrange("p (c e) -> p c e", e=E)))

            def group_steps(it, is_last):
                take.wait_taken()
                step(dve.tensor_reduce(top[:, :], logits[:, :, :], X, ALU.max))
                dve.tensor_tensor(logits[:, :, :], logits[:, :, :], over(top[:, :], E), ALU.subtract).then_inc(logits_ready, 1)
                dve.wait_ge(probs_ready, it + 1)
                step(dve.tensor_reduce(total[:, :], probs[:, :, :], X, ALU.add))
                step(dve.reciprocal(total[:, :], total[:, :]))
                step(dve.tensor_tensor(probs[:, :, :], probs[:, :, :], over(total[:, :], E), ALU.mult))
                first_of_largest(dve, step, probs[:, :, :], rank, top, hit[:, :, :], order)
                dve.tensor_tensor(share[:, :, :], hit[:, :, :], probs[:, :, :], ALU.mult).then_inc(share_ready, 1)
                dve.wait_ge(share_ready, it + 1)
                take(lambda bank: dve.tensor_copy(acc[:, 1, :, :], bank.rearrange("p (c d) -> p c d", c=GT)))
                for e in range(E):
                    if e == E - 1 and not is_last:
                        take_logits()
                    take.wait_taken()

                    def out_of(bank):
                        for c in range(GT):
                            dst = acc[:, e % 2, c, :] if e < E - 1 else group(it)[:, c, :]
                            last = dve.scalar_tensor_tensor(out=dst, in0=bank[:, c * D:(c + 1) * D],
                                                            scalar=share[:, c, e:e + 1], in1=acc[:, (e + 1) % 2, c, :],
                                                            op0=ALU.mult, op1=ALU.add)
                        return last
                    take(out_of)
                    if e == 3 and not is_last:
                        nm.vector(dve, group(it + 1), step, it + 1)

            nm.vector(dve, group(0), step, 0)
            take_logits()

            def enter(it):
                step.enter(it, nm.STEPS + 9)
                take.enter(it, VT)

            def leave(n):
                step.leave(n)
                take.leave(n)

            groups(dve, enter, group_steps, leave)


class GroupRms:

    def __init__(self, m, name):
        self.sq = m.sb(name + "_sq", [P, GT, D])
        self.var, self.std, self.rstd = (m.sb(name + "_" + n, [P, GT]) for n in ("var", "std", "rstd"))
        self.sq_ready, self.var_ready, self.std_ready, self.ready = (
            m.sem(name + "_" + n) for n in ("sq_ready", "var_ready", "std_ready", "ready"))

    STEPS = 1

    def vector(self, dve, src, gain, step, it):
        dve.wait_ge(self.sq_ready, it * GT + GT)
        dve.tensor_scalar(self.var[:, :], self.var[:, :], 1.0 / D, RMS_EPS, ALU.mult, ALU.add).then_inc(self.var_ready, 1)
        dve.wait_ge(self.std_ready, it + 1)
        step(dve.reciprocal(self.rstd[:, :], self.std[:, :]))
        for c in range(GT):
            dve.scalar_tensor_tensor(out=src[:, c, :], in0=src[:, c, :], scalar=self.rstd[:, c:c + 1], in1=gain,
                                     op0=ALU.mult, op1=ALU.mult).then_inc(self.ready, 1)

    def scalar(self, act, src, it):
        for c in range(GT):
            act.activation(self.sq[:, c, :], src[:, c, :], ACT.Square, accum_out=self.var[:, c:c + 1]).then_inc(self.sq_ready, 1)
        act.wait_ge(self.var_ready, it + 1)
        act.activation(self.std[:, :], self.var[:, :], ACT.Sqrt).then_inc(self.std_ready, 1)


def ffn_0(nc, io, x_tok, ident):
    with ExitStack() as stack:
        y = Memory(nc, stack, "ffn0").sb("y", [P, NT, D])
        moe_top2(nc, io, x_tok, ident, y)
        dense_path(nc, io, x_tok, ident, y)


def moe_top2(nc, io, x_tok, ident, y):
    with ExitStack() as stack:
        m = Memory(nc, stack, "moe0")
        router = m.sb("router", [P, E])
        w1, w3, w2 = (m.sb(n, [P, E, P]) for n in ("w1", "w3", "w2"))
        gain = m.sb("gain", [P, D])
        rank = m.sb("rank", [P, E])
        nm, rms = AheadNorm(m), GroupRms(m, "rms")
        xnT = m.sb("xnT", [P, GC])
        logits, probs, hit, hit2, rest, share = (m.sb(n, [P, GT, E]) for n in ("logits", "probs", "hit", "hit2", "rest", "share"))
        top, total, order = (m.sb(n, [P, GT]) for n in ("top", "total", "order"))
        gate = m.sb("gate", [P, 2, GC])
        hidden = m.sb("hidden", [P, 2, GC])
        acc = m.sb("acc", [P, 2, GT, D])
        out = acc[:, (E - 1) % 2, :, :]
        zeros = m.sb("zeros", [P, D])
        scratch = m.sb("scratch", [P, 2])
        vl = Lane(m, "vector_lane")
        sl = Lane(m, "scalar_lane")
        consts = m.sem("consts")
        w_loaded = m.sem("w_loaded")
        y_ready = m.sem("y_ready")
        chain = m.sem("vector_chain")
        logits_ready = m.sem("logits_ready")
        probs_ready = m.sem("probs_ready")
        block = stack.enter_context(nc.Block())
        N_CONSTS = 3
        V_ORDER = [("up", 0)] + [x for e in range(1, E) for x in (("up", e), ("down", e - 1))] + [("down", E - 1)]
        VT, ST = len(V_ORDER), 2 + E

        def v_at(what):
            return V_ORDER.index(what) + 1

        def group(it, of=x_tok):
            return of[:, GT * it:GT * (it + 1), :] if isinstance(it, int) else of[:, bass.ds(it * GT, GT), :]

        @block.sync
        def _(sp):
            sp.dma_start(router[:, :], io["L0_ffn_router_w"]).then_inc(consts, 16)
            sp.dma_start(rank[:, :], io["rank"]).then_inc(consts, 16)
            load_row(sp, gain[:, :], io["L0_ffn_moe_norm_w"], consts)
            sp.dma_start(w1[:, :, :], io["L0_ffn_ew1"].rearrange("e c f -> c e f")).then_inc(w_loaded, 16)
            sp.dma_start(w3[:, :, :], io["L0_ffn_ew3"].rearrange("e c f -> c e f")).then_inc(w_loaded, 16)
            sp.dma_start(w2[:, :, :], io["L0_ffn_ew2"].rearrange("e f d -> f e d")).then_inc(w_loaded, 16)

        @block.tensor
        def _(pe):
            v, s = Fill(pe, vl), Fill(pe, sl)
            pe.wait_ge(consts, 16 * N_CONSTS)
            pe.wait_ge(w_loaded, 48)

            def turn_xn(it):
                pe.wait_ge(nm.ready, it * GT + GT)

                def fill(bank):
                    for c in range(GT):
                        last = pe.transpose(bank[:, c * P:(c + 1) * P], nm.xn[:, c, :], ident[:, :])
                    return last
                s(fill)

            def take_logits():
                s.wait_emptied()

                def fill(bank):
                    for c in range(GT):
                        last = pe.matmul(bank[:, c * E:(c + 1) * E], xnT[:, c * P:(c + 1) * P], router[:, :],
                                         start=True, stop=True)
                    return last
                s(fill)

            def up(e):
                s(lambda bank: pe.matmul(bank, w1[:, e, :], xnT[:, :], start=True, stop=True))
                v(lambda bank: pe.matmul(bank, w3[:, e, :], xnT[:, :], start=True, stop=True))
                return v.t.value() + vl.banks

            def down(e, hidden_ready):
                pe.wait_ge(vl.free, hidden_ready)

                def fill(bank):
                    for c in range(GT):
                        last = pe.matmul(bank[:, c * D:(c + 1) * D], hidden[:, e % 2, c * P:(c + 1) * P],
                                         w2[:, e, :], start=True, stop=True)
                    return last
                v(fill)

            def group_products(it, is_last):
                ready = up(0)
                for e in range(1, E):
                    next_ready = up(e)
                    if e == E - 1 and not is_last:
                        turn_xn(it + 1)
                    down(e - 1, ready)
                    ready = next_ready
                if not is_last:
                    take_logits()
                down(E - 1, ready)

            turn_xn(0)
            take_logits()

            def enter(it):
                v.enter(it, VT)
                s.enter(it, ST)

            def leave(n):
                v.leave(n)
                s.leave(n)

            groups(pe, enter, group_products, leave)

        @block.scalar
        def _(act):
            take = Take(act, sl)
            for _ in range(sl.banks):
                act.activation(scratch[:, 0:1], ident[:, 0:1], ACT.Copy).then_inc(sl.free, 1)
                act.wait_ge(sl.free, _ + 1)

            def take_xn():
                take(lambda bank: act.activation(xnT[:, :], bank, ACT.Copy))
                take(lambda bank: act.activation(logits[:, :, :], bank[:, 0:GT * E].rearrange("p (c e) -> p c e", e=E), ACT.Copy))

            def group_steps(it, is_last):
                act.wait_ge(logits_ready, it + 1)
                act.activation(probs[:, :, :], logits[:, :, :], ACT.Exp).then_inc(probs_ready, 1)
                for e in range(E):
                    if e >= 2:
                        act.wait_ge(vl.free, it * VT + (v_at(("up", e - 2)) + vl.banks))
                    take(lambda bank: act.activation(gate[:, e % 2, :], bank, ACT.Silu))
                    if e == 4 and not is_last:
                        nm.scalar(act, group(it + 1), it + 1)
                if not is_last:
                    take_xn()
                act.wait_ge(vl.free, it * VT + (VT + vl.banks))
                rms.scalar(act, out, it)

            nm.scalar(act, group(0), 0)
            take_xn()
            groups(act, lambda it: take.enter(it, ST), group_steps, take.leave)

        @block.gpsimd
        def _(pool):
            pool.wait_ge(consts, 16 * N_CONSTS)
            pool.memset(scratch[:, 1:2], 0.0).then_inc(y_ready, 1)

            def group_steps(it, is_last):
                pool.wait_ge(rms.ready, it * GT + GT)
                pool.tensor_tensor(group(it, y), out, group(it), ALU.add).then_inc(y_ready, 1)

            groups(pool, lambda it: None, group_steps, lambda n: None)

        @block.vector
        def _(dve):
            take, step = Take(dve, vl), Chain(dve, chain)
            for _ in range(vl.banks):
                dve.memset(zeros[:, :], 0.0).then_inc(vl.free, 1)
                dve.wait_ge(vl.free, _ + 1)
            dve.wait_ge(consts, 16 * N_CONSTS)

            def group_steps(it, is_last):
                dve.wait_ge(sl.free, it * ST + (2 + sl.banks))
                step(dve.tensor_reduce(top[:, :], logits[:, :, :], X, ALU.max))
                dve.tensor_tensor(logits[:, :, :], logits[:, :, :], over(top[:, :], E), ALU.subtract).then_inc(logits_ready, 1)

                def choose():
                    dve.wait_ge(probs_ready, it + 1)
                    step(dve.tensor_reduce(total[:, :], probs[:, :, :], X, ALU.add))
                    step(dve.reciprocal(total[:, :], total[:, :]))
                    step(dve.tensor_tensor(probs[:, :, :], probs[:, :, :], over(total[:, :], E), ALU.mult))
                    first_of_largest(dve, step, probs[:, :, :], rank, top, hit[:, :, :], order)
                    step(dve.scalar_tensor_tensor(out=rest[:, :, :], in0=hit[:, :, :], scalar=-2.0, in1=probs[:, :, :],
                                                  op0=ALU.mult, op1=ALU.add))
                    first_of_largest(dve, step, rest[:, :, :], rank, top, hit2[:, :, :], order)
                    step(dve.tensor_tensor(hit[:, :, :], hit[:, :, :], hit2[:, :, :], ALU.add))
                    step(dve.tensor_tensor(share[:, :, :], hit[:, :, :], probs[:, :, :], ALU.mult))

                for what, e in V_ORDER:
                    if what == "up":
                        dve.wait_ge(sl.free, it * ST + (2 + e + 1 + sl.banks))
                        take(lambda bank: dve.tensor_tensor(hidden[:, e % 2, :], gate[:, e % 2, :], bank, ALU.mult))
                        if e == 1:
                            choose()
                        continue
                    if e > 0:
                        take.wait_taken()
                    if e == 1:
                        dve.wait_ge(y_ready, it + 1)

                    def out_of(bank):
                        for c in range(GT):
                            last = dve.scalar_tensor_tensor(out=acc[:, e % 2, c, :], in0=bank[:, c * D:(c + 1) * D],
                                                            scalar=share[:, c, e:e + 1],
                                                            in1=acc[:, (e + 1) % 2, c, :] if e else zeros[:, :],
                                                            op0=ALU.mult, op1=ALU.add)
                        return last
                    take(out_of)
                    if e == 3 and not is_last:
                        nm.vector(dve, group(it + 1), step, it + 1)
                take.wait_taken()
                rms.vector(dve, out, gain[:, :], step, it)

            nm.vector(dve, group(0), step, 0)

            def enter(it):
                step.enter(it, nm.STEPS + 17 + rms.STEPS)
                take.enter(it, VT)

            def leave(n):
                step.leave(n)
                take.leave(n)

            groups(dve, enter, group_steps, leave)


def dense_path(nc, io, x_tok, ident, y):
    NF = FF // P
    HV = HD + 1
    with ExitStack() as stack:
        m = Memory(nc, stack, "dense")
        wq, wk, wv, wo = (m.sb(n, [P, D]) for n in ("wq", "wk", "wv", "wo"))
        w1, w3 = m.sb("w1", [P, FF]), m.sb("w3", [P, FF])
        w2 = m.sb("w2", [P, NF, D])
        attn_gain, ff_gain = m.sb("attn_gain", [P, D]), m.sb("ff_gain", [P, D])
        own = m.sb("own", [P, D])
        parity = m.sb("parity", [P, H])
        causal = m.sb("causal", [P, S])
        nm, rms1, rms2 = GroupNorm(m), GroupRms(m, "rms1"), GroupRms(m, "rms2")
        xnT = m.sb("xnT", [P, GC])
        qT = m.sb("qT", [P, GC])
        kT = m.sb("kT", [P, GC])
        keys = m.sb("keys", [P, 2 * GT, H, S])
        vals = m.sb("vals", [P, 2 * GT, H, HV])
        sc = m.sb("scores", [P, 2, H, S])
        mx = m.sb("max", [P, 2, H])
        ex = m.sb("exps", [P, 2, H, S])
        exT = m.sb("expsT", [P, 2, H // 2, P])
        denom = m.sb("denom", [P, GT, H])
        o = m.sb("o", [P, GT, D])
        oT = m.sb("oT", [P, GC])
        proj = m.sb("proj", [P, GT, D])
        h = m.sb("h", [P, GT, D])
        hT = m.sb("hT", [P, GC])
        gate = m.sb("gate", [P, NF, GC])
        hidden = m.sb("hidden", [P, NF, GC])
        ffn = m.sb("ffn", [P, GT, D])
        scratch = m.sb("scratch", [P, 2])
        vl = Lane(m, "vector_lane", 3)
        sl = Lane(m, "scalar_lane", 4)
        consts = m.sem("consts")
        ffn_loaded = m.sem("ffn_loaded")
        chain = m.sem("vector_chain")
        keys_even = m.sem("keys_of_even_tiles")
        keys_odd = m.sem("keys_of_odd_tiles")
        scores_ready = m.sem("scores_ready")
        shifted = m.sem("shifted")
        exps_ready = m.sem("exps_ready")
        vals_preset = m.sem("vals_preset")
        h_ready = m.sem("h_ready")
        block = stack.enter_context(nc.Block())
        N_CONSTS = 7
        V_ORDER = ["k", "v0", "v1", "s0", "s0", "s1", "s1", "s2", "s2", "o0", "s3", "s3", "o1", "o2", "o3",
                   "wo"] + ["w3"] * NF + ["w2"]
        S_ORDER = ["xn", "q"] + [f"e{c}" for c in range(GT) for _ in range(2)] + ["o", "h"] + ["w1"] * NF
        VT, ST = len(V_ORDER), len(S_ORDER)

        def v_at(what):
            return V_ORDER.index(what) + V_ORDER.count(what)

        def s_at(what):
            return S_ORDER.index(what) + S_ORDER.count(what)

        def group(it):
            return x_tok[:, bass.ds(it * GT, GT), :]

        def write_keys(eng, c):
            src = kT[:, c * P:(c + 1) * P].rearrange("p (b k) -> p b k", b=2).unsqueeze(2).broadcast_to([P, 2, H, S])
            of_head = own[:, :].rearrange("p (h d) -> p h d", d=HD)[:, :, 0].unsqueeze(1).unsqueeze(3)
            return eng.tensor_tensor(keys[:, 2 * c:2 * c + 2, :, :], src, of_head.broadcast_to([P, 2, H, S]), ALU.mult)

        @block.sync
        def _(sp):
            sp.dma_start(wq[:, :], io["L0_ffn_wq"]).then_inc(consts, 16)
            sp.dma_start(wk[:, :], io["L0_ffn_wk"]).then_inc(consts, 16)
            sp.dma_start(wv[:, :], io["L0_ffn_wv"]).then_inc(consts, 16)
            sp.dma_start(own[:, :], io["own_head"]).then_inc(consts, 16)
            sp.dma_start(parity[:, :], io["head_parity"]).then_inc(consts, 16)
            sp.dma_start(causal[:, :], io["causal"]).then_inc(consts, 16)
            sp.dma_start(wo[:, :], io["L0_ffn_wo"]).then_inc(consts, 16)
            load_row(sp, attn_gain[:, :], io["L0_ffn_attn_norm_w"], ffn_loaded)
            load_row(sp, ff_gain[:, :], io["L0_ffn_ff_norm_w"], ffn_loaded)
            sp.dma_start(w1[:, :], io["L0_ffn_w1"]).then_inc(ffn_loaded, 16)
            sp.dma_start(w3[:, :], io["L0_ffn_w3"]).then_inc(ffn_loaded, 16)
            sp.dma_start(w2[:, :, :], io["L0_ffn_w2"].rearrange("(f p) d -> p f d", p=P)).then_inc(ffn_loaded, 16)

        @block.gpsimd
        def _(pool):
            pool.wait_ge(consts, 16 * N_CONSTS)
            with pool.Fori(0, NG) as it:
                def shift(c):
                    pool.wait_ge(scores_ready, it * GT + (c + 1))
                    pool.tensor_tensor(sc[:, c % 2, :, :], sc[:, c % 2, :, :], over(mx[:, c % 2, :], S),
                                       ALU.subtract).then_inc(shifted, 1)

                pool.wait_ge(vl.free, it * VT + (v_at("k") + vl.banks))
                write_keys(pool, 1).then_inc(keys_odd, 1)
                shift(0)
                write_keys(pool, 3).then_inc(keys_odd, 1)
                for c in range(1, GT):
                    shift(c)

        @block.tensor
        def _(pe):
            v, s = Fill(pe, vl), Fill(pe, sl)
            pe.wait_ge(consts, 16 * N_CONSTS)
            pe.wait_ge(ffn_loaded, 16 * 5)
            with pe.Fori(0, NG) as it:
                v.enter(it, VT)
                s.enter(it, ST)

                def turn(src):
                    def fill(bank):
                        for c in range(GT):
                            last = pe.transpose(bank[:, c * P:(c + 1) * P], src[:, c, :], ident[:, :])
                        return last
                    return fill

                def values(i):
                    def fill(bank):
                        for j in range(4):
                            b = 4 * i + j
                            for half in range(2):
                                last = pe.matmul(bank[64 * half:64 * half + 64, j * D:(j + 1) * D],
                                                 xnT[:, b * S:(b + 1) * S], wv[:, :], start=True, stop=True)
                        return last
                    v(fill)

                def scores(c):
                    if c % 2 == 0:
                        pe.wait_ge(keys_even, it * 2 + (c // 2 + 1))
                    else:
                        pe.wait_ge(keys_odd, it * 2 + (c // 2 + 1))
                    for half in range(2):
                        def fill(bank):
                            for u in range(2):
                                last = pe.matmul(bank[64 * u:64 * u + 64, :], qT[:, c * P + 64 * u:c * P + 64 * u + 64],
                                                 flat(keys[:, 2 * c + u, half * 8:half * 8 + 8, :]), start=True, stop=True)
                            return last
                        v(fill)

                def turn_exps(c):
                    pe.wait_ge(exps_ready, it * GT + (c + 1))
                    pairs = ex[:, c % 2, :, :].rearrange("p (j t) k -> p j (t k)", t=2)
                    for half in range(2):
                        def fill(bank):
                            for i in range(4):
                                last = pe.transpose(bank[:, i * P:(i + 1) * P], pairs[:, half * 4 + i, :], ident[:, :])
                            return last
                        s(fill)

                def attend(c):
                    s.wait_emptied()

                    def fill(bank):
                        for j in range(H // 2):
                            for u in range(2):
                                last = pe.matmul(bank[64 * u:64 * u + 64, j * 2 * HV:(j + 1) * 2 * HV],
                                                 exT[:, c % 2, j, 64 * u:64 * u + 64],
                                                 flat(vals[:, 2 * c + u, 2 * j:2 * j + 2, :]), start=True, stop=True)
                        return last
                    v(fill)

                pe.wait_ge(nm.ready, it + 1)
                s(turn(nm.xn))
                s.wait_emptied()
                v(lambda bank: pe.matmul(bank, wk[:, :], xnT[:, :], start=True, stop=True))
                s(lambda bank: pe.matmul(bank, wq[:, :], xnT[:, :], start=True, stop=True))
                values(0)
                values(1)
                s.wait_emptied()
                scores(0)
                scores(1)
                turn_exps(0)
                scores(2)
                attend(0)
                turn_exps(1)
                scores(3)
                attend(1)
                for c in (2, 3):
                    turn_exps(c)
                    attend(c)
                v.wait_emptied()
                s(turn(o))
                s.wait_emptied()

                def fill(bank):
                    for c in range(GT):
                        last = pe.matmul(bank[:, c * D:(c + 1) * D], oT[:, c * P:(c + 1) * P], wo[:, :], start=True, stop=True)
                    return last
                v(fill)
                pe.wait_ge(h_ready, it + 1)
                s(turn(h))
                s.wait_emptied()
                for f in range(NF):
                    s(lambda bank: pe.matmul(bank, w1[:, f * P:(f + 1) * P], hT[:, :], start=True, stop=True))
                    v(lambda bank: pe.matmul(bank, w3[:, f * P:(f + 1) * P], hT[:, :], start=True, stop=True))
                v.wait_emptied()

                def fill(bank):
                    for c in range(GT):
                        for f in range(NF):
                            last = pe.matmul(bank[:, c * D:(c + 1) * D], hidden[:, f, c * P:(c + 1) * P], w2[:, f, :],
                                             start=(f == 0), stop=(f == NF - 1))
                    return last
                v(fill)
                v.leave(NG)
                s.leave(NG)

        @block.scalar
        def _(act):
            take = Take(act, sl)
            for _ in range(sl.banks):
                act.activation(scratch[:, 0:1], ident[:, 0:1], ACT.Copy).then_inc(sl.free, 1)
                act.wait_ge(sl.free, _ + 1)
            with act.Fori(0, NG) as it:
                take.enter(it, ST)

                def exps(c):
                    act.wait_ge(shifted, it * GT + (c + 1))
                    act.activation(ex[:, c % 2, :, :], sc[:, c % 2, :, :], ACT.Exp,
                                   scale=float(1 / np.sqrt(np.float32(HD)))).then_inc(exps_ready, 1)

                def take_exps(c):
                    if c >= 2:
                        act.wait_ge(vl.full, it * VT + v_at(f"o{c - 2}"))
                    for half in range(2):
                        take(lambda bank: act.activation(exT[:, c % 2, half * 4:half * 4 + 4, :],
                                                         bank.rearrange("p (j q) -> p j q", j=4), ACT.Copy))

                nm.scalar(act, it)
                take(lambda bank: act.activation(xnT[:, :], bank, ACT.Copy))
                take(lambda bank: act.activation(qT[:, :], bank, ACT.Copy))
                exps(0)
                for c in range(GT):
                    if c + 1 < GT:
                        exps(c + 1)
                    take_exps(c)
                take(lambda bank: act.activation(oT[:, :], bank, ACT.Copy))
                act.wait_ge(vl.free, it * VT + (v_at("wo") + vl.banks))
                rms1.scalar(act, proj, it)
                take(lambda bank: act.activation(hT[:, :], bank, ACT.Copy))
                for f in range(NF):
                    take(lambda bank: act.activation(gate[:, f, :], bank, ACT.Silu))
                act.wait_ge(vl.free, it * VT + (v_at("w2") + vl.banks))
                rms2.scalar(act, ffn, it)
                take.leave(NG)

        @block.vector
        def _(dve):
            take, step = Take(dve, vl), Chain(dve, chain)
            for _ in range(vl.banks):
                dve.memset(scratch[:, 1:2], 0.0).then_inc(vl.free, 1)
                dve.wait_ge(vl.free, _ + 1)
            dve.wait_ge(consts, 16 * N_CONSTS)
            dve.wait_ge(ffn_loaded, 16 * 5)
            dve.tensor_copy(vals[:, :, :, HD], under(parity[:, :], 2 * GT)).then_inc(vals_preset, 1)
            dve.wait_ge(vals_preset, 1)
            with dve.Fori(0, NG) as it:
                step.enter(it, nm.STEPS + rms1.STEPS + rms2.STEPS + GT + 2)
                take.enter(it, VT)

                def take_scores(c):
                    if c >= 2:
                        dve.wait_ge(exps_ready, it * GT + (c - 1))
                    for half in range(2):
                        take(lambda bank: dve.tensor_tensor(sc[:, c % 2, half * 8:half * 8 + 8, :],
                                                            bank.rearrange("p (h k) -> p h k", h=8),
                                                            under(causal[:, :], 8), ALU.add))
                    take.wait_taken()
                    dve.tensor_reduce(mx[:, c % 2, :], sc[:, c % 2, :, :], X, ALU.max).then_inc(scores_ready, 1)

                def take_o(c):
                    def out_of(bank):
                        got = bank[:, 0:H * HV].rearrange("p (h d) -> p h d", d=HV)
                        step(dve.reciprocal(denom[:, c, :], got[:, :, HD]))
                        return dve.tensor_tensor(o[:, c, :].rearrange("p (h d) -> p h d", d=HD), got[:, :, 0:HD],
                                                 over(denom[:, c, :], HD), ALU.mult)
                    take(out_of)

                nm.vector(dve, group(it), step, it)
                take(lambda bank: dve.tensor_copy(kT[:, :], bank))
                take.wait_taken()
                write_keys(dve, 0).then_inc(keys_even, 1)
                for i in range(2):
                    take(lambda bank: dve.tensor_tensor(
                        vals[:, 4 * i:4 * i + 4, :, 0:HD], bank.rearrange("p (b h d) -> p b h d", b=4, d=HD),
                        parity[:, :].unsqueeze(1).unsqueeze(3).broadcast_to([P, 4, H, HD]), ALU.mult))
                write_keys(dve, 2).then_inc(keys_even, 1)
                take_scores(0)
                take_scores(1)
                take_scores(2)
                take_o(0)
                take_scores(3)
                take_o(1)
                take_o(2)
                take_o(3)
                take(lambda bank: dve.tensor_copy(proj[:, :, :], bank.rearrange("p (c d) -> p c d", c=GT)))
                take.wait_taken()
                rms1.vector(dve, proj, attn_gain[:, :], step, it)
                dve.wait_ge(rms1.ready, it * GT + GT)
                dve.tensor_tensor(h[:, :, :], nm.xn[:, :, :], proj[:, :, :], ALU.add).then_inc(h_ready, 1)
                for f in range(NF):
                    dve.wait_ge(sl.free, it * ST + (s_at("h") + f + 1 + sl.banks))
                    take(lambda bank: dve.tensor_tensor(hidden[:, f, :], gate[:, f, :], bank, ALU.mult))
                take(lambda bank: dve.tensor_copy(ffn[:, :, :], bank.rearrange("p (c d) -> p c d", c=GT)))
                take.wait_taken()
                rms2.vector(dve, ffn, ff_gain[:, :], step, it)
                dve.wait_ge(rms2.ready, it * GT + GT)
                dve.wait_ge(h_ready, it + 1)
                step(dve.tensor_tensor(ffn[:, :, :], ffn[:, :, :], h[:, :, :], ALU.add))
                step(dve.tensor_tensor(group(it), ffn[:, :, :], y[:, bass.ds(it * GT, GT), :], ALU.add))
                take.leave(NG)
                step.leave(NG)


PIECES = [(c, min(512, N_CTX - c)) for c in range(0, N_CTX, 512)]
NK = N_CTX + N_CTX % 2
MASK_FILL = -float(2 ** 27)
HALF = H // 2
HC = HALF * S


def cross_attention_1(nc, io, x_tok, ident):
    NU = 2 * len(GROUPS) + (1 + HALF) * len(PIECES) + 1
    TURNS = 1
    A_HEADS = 12
    DEN = 24
    SCALE = float(np.float32(1.0) / np.sqrt(np.float32(HD)))
    with ExitStack() as stack:
        m = Memory(nc, stack, "xa1")
        wq, bq = m.sb("wq_twice", [P, 2, P]), m.sb("bq_twice", [P, 2])
        bk = m.sb("bk", [P, 1])
        wk, wv, wo = m.sb("wkT", [P, D]), m.sb("wvT", [P, D]), m.sb("woT", [P, D])
        bv, bo = m.sb("bv", [P, D]), m.sb("bo", [P, D])
        half_head = m.sb("half_head", [P, HALF])
        pair_row = m.sb("pair_row", [P, 2, 4])
        nm = Norm(m)
        att = nm.xn
        xnT = m.sb("xnT", [P, NT * P])
        qf = m.sb("qf", [P, 512])
        q_hi = [m.sb(f"q_hi{g}", [P, NT * P], F32R) for g in range(2)]
        q_lo = [m.sb(f"q_lo{g}", [P, NT * P], F32R) for g in range(2)]
        ctx = [m.sb(f"ctx{u}", [P, NCH, D]) for u in range(2)]
        mask_row = [m.sb(f"mask_row{u}", [P, N_CTX], U8) for u in range(2)]
        mask_col = m.sb("mask_col", [P, B, FULL], U8)
        mask_tail = m.sb("mask_tail", [P, B], U8)
        key_fill = m.sb("key_fill", [P, B, NCH])
        bias = [m.sb(f"bias{u}", [P, NCH]) for u in range(2)]
        fill_row = m.sb("fill_row", [P, N_CTX])
        ctxT = m.sb("ctxT", [P, N_CTX])
        kf = m.sb("kf", [P, N_CTX])
        k_lo = m.sb("k_lo", [P, N_CTX], F32R)
        keys = [[m.sb(f"keys{u}{g}", [P, NK], F32R) for g in range(2)] for u in range(2)]
        vals = [m.sb(f"vals{u}", [P, NCH, 8, 32]) for u in range(2)]
        qb_hi = [[m.sb(f"qb_hi{u}{g}", [P, HC], F32R) for g in range(2)] for u in range(2)]
        qb_lo = [[m.sb(f"qb_lo{u}{g}", [P, HC], F32R) for g in range(2)] for u in range(2)]
        shift = [[m.sb(f"shift{u}{g}", [P, HC], BF16) for g in range(2)] for u in range(2)]
        prob = [m.sb(f"prob{i}", [P, 2 * HC]) for i in range(2)]
        junk = m.sb("junk", [P, 2, 512])
        tops = m.sb("tops", [P, 2 * HALF // 2, len(PIECES)])
        top = m.sb("top", [P, HALF])
        top_hi, top_lo = m.sb("top_hi", [P, HALF], BF16), m.sb("top_lo", [P, HALF], BF16)
        top_parts = m.sb("top_parts", [P, P])
        topT = m.sb("topT", [P, P], BF16)
        ones = m.sb("ones", [P, 32])
        sums = m.sb("sums", [P, 4, S])
        ones_b = m.sb("ones_b", [P, P], BF16)
        recip = m.sb("recip", [P, 4, 4])
        scratch = m.sb("scratch", [P, 2])
        sl = Lane(m, "setup_lane", 4)
        el = Lane(m, "exp_lane", 2)
        ps_o = m.psum("ps_o", [P, 4 * S])
        consts = m.sem("consts")
        chain = m.sem("vector_chain")
        pool_chain = m.sem("pool_chain")
        ctx_loaded = [m.sem(f"ctx_loaded{u}") for u in range(2)]
        q_ready = m.sem("q_ready")
        key_fill_ready = m.sem("key_fill_ready")
        fill_ready = m.sem("fill_ready")
        k_hi_ready = m.sem("k_hi_ready")
        k_lo_ready = m.sem("k_lo_ready")
        keys_moved = [m.sem(f"keys_moved{g}") for g in range(2)]
        blocks_ready = m.sem("blocks_ready")
        top_ready = m.sem("top_ready")
        shift_ready = m.sem("shift_ready")
        prob_used = m.sem("prob_used")
        sums_ready = m.sem("sums_ready")
        att_ready = m.sem("att_ready")
        bias_added = m.sem("bias_added")
        mask_tail_cleared = m.sem("mask_tail_cleared")
        block = stack.enter_context(nc.Block())
        N_CONSTS = 12
        LOADS = 48

        def half_rows(g):
            return slice(64 * g, 64 * g + 64)

        def cols(b):
            return bass.ds(b * S, S)

        def batches(eng, enter, body, leave):
            body(0, 0, None, True, False)
            with eng.Fori(0, B // 2 - 1) as it:
                enter(it)
                body(it * 2 + 1, 1, it, False, False)
                body(it * 2 + 2, 0, it, False, False)
                leave(B // 2 - 1)
            body(B - 1, 1, NT - 1, False, True)

        @block.sync
        def _(sp):
            for dst, src in ((wq[:, :, :], "L1_xattn_WqT2"), (wk[:, :], "L1_xattn_WkT"), (bq[:, :], "L1_xattn_bq2"),
                             (bk[:, :], "L1_xattn_bkT"), (wv[:, :], "L1_xattn_WvT"), (wo[:, :], "L1_xattn_WoT"),
                             (half_head[:, :], "half_head"), (pair_row[:, :, :], "pair_row")):
                sp.dma_start(dst, io[src]).then_inc(consts, 16)
            load_row(sp, bv[:, :], io["L1_xattn_bv"], consts)
            load_row(sp, bo[:, :], io["L1_xattn_bo"], consts)
            sp.dma_start(mask_col[:, :, :], io["mask"][:, 0:FULL * P].rearrange("b (p j) -> p b j", j=FULL)).then_inc(consts, 16)
            sp.wait_ge(mask_tail_cleared, 1)
            sp.dma_start(mask_tail[0:TAIL, :], io["mask_tail"]).then_inc(consts, 16)

            def load(b, u):
                src = io["ctx_1024"][b] if isinstance(b, int) else io["ctx_1024"][bass.ds(b, 1)].rearrange("a t c -> (a t) c")
                row = io["mask_row"][b:b + 1, :] if isinstance(b, int) else io["mask_row"][bass.ds(b, 1), :]
                load_ctx(sp, ctx[u][:, :, :], src, ctx_loaded[u])
                sp.dma_start(mask_row[u][:, :], row.broadcast_to([P, N_CTX])).then_inc(ctx_loaded[u], 16)

            low = Tally(k_lo_ready)

            def move_keys(u):
                for g in range(2):
                    sp.wait_ge(k_lo_ready, low.next())
                    src, dst = half_rows(g), half_rows(1 - g)
                    sp.dma_start(keys[u][g][dst, 0:N_CTX].bitcast(F32), k_lo[src, :].bitcast(F32)).then_inc(keys_moved[g], 16)

            load(0, 0)
            load(1, 1)
            move_keys(0)
            with sp.Fori(0, B // 2 - 1) as it:
                low.enter(it, 4)
                for u in range(2):
                    sp.wait_ge(top_ready, it * 2 + (u + 1))
                    load(it * 2 + (2 + u), u)
                    move_keys(1 - u)
                low.leave(B // 2 - 1)
            move_keys(1)

        @block.gpsimd
        def _(pool):
            pool.memset(mask_tail[:, :], 0).then_inc(mask_tail_cleared, 1)
            loaded = [Tally(s) for s in ctx_loaded]
            step_t, tops_t, free = Tally(pool_chain), Tally(top_ready), Tally(sl.free)

            def setup(b, u, first=False, turns=TURNS):
                wait_apart(pool, (consts, 16 * N_CONSTS), [(ctx_loaded[u], loaded[u].next(LOADS))]
                           + ([] if first else [(top_ready, tops_t.next())]))
                pool.tensor_scalar(fill_row[:, :], mask_row[u][:, :], -1.0, -MASK_FILL, ALU.add, ALU.mult).then_inc(fill_ready, 1)
                wait_apart(pool, (consts, 16 * N_CONSTS), [(sl.free, free.value() + (1 + sl.banks))])
                for h in range(2):
                    for dst, src in ((qb_hi, q_hi), (qb_lo, q_lo)):
                        pool.tensor_tensor(
                            dst[u][h][:, :].rearrange("p (a q) -> p a q", q=S),
                            src[h][:, cols(b)].unsqueeze(1).broadcast_to([P, HALF, S]),
                            over(half_head[:, :], S), ALU.mult).then_inc(blocks_ready, 1)
                pool.tensor_copy(bias[u][:, :], key_fill[:, bass.ds(b, 1), :].rearrange("p a j -> p (a j)")).then_inc(blocks_ready, 1)
                pool.wait_ge(sl.free, free.value() + (NU - len(GROUPS) + turns + sl.banks))
                free.next(NU + turns)
                for g in range(2):
                    pool.tensor_tensor(shift[u][g][:, :].rearrange("p (a q) -> p a q", q=P), under(topT[:, :], 4),
                                       over(pair_row[:, g, :], P), ALU.mult).then_inc(shift_ready, 1)

            pool.memset(ones[:, :], 1.0).then_inc(q_ready, 1)
            pool.memset(ones_b[:, :], 1.0).then_inc(q_ready, 1)
            pool.memset(top_parts[:, :], 0.0).then_inc(q_ready, 1)
            for u in range(2):
                pool.memset(vals[u][:, :, :, :], 0.0).then_inc(pool_chain, 1)
                pool.wait_ge(pool_chain, step_t.next())
                pool.memset(vals[u][:, :, :, DEN:DEN + 1], 1.0).then_inc(q_ready, 1)
            for u in range(2):
                for g in range(2):
                    pool.memset(keys[u][g][:, N_CTX:NK].bitcast(F32), 0.0).then_inc(pool_chain, 1)
                    pool.wait_ge(pool_chain, step_t.next())
            pool.wait_ge(consts, 16 * N_CONSTS)
            pool.wait_ge(key_fill_ready, 10)
            free.next(12)
            setup(0, 0, first=True, turns=0)

            tallies = (tops_t, free)

            def enter(it):
                for t, per in zip(tallies, (2, 2 * (NU + TURNS))):
                    t.enter(it, per)
                for t in loaded:
                    t.enter(it, LOADS)

            def leave(n):
                for t in (*tallies, *loaded):
                    t.leave(n)

            batches(pool, enter, lambda b, u, n, first, last: None if last else setup(b + 1, 1 - u, turns=0 if first else TURNS),
                    leave)
            pool.tensor_tensor(x_tok[:, :, :], x_tok[:, :, :], under(bo[:, :], NT), ALU.add).then_inc(bias_added, 1)

        @block.tensor
        def _(pe):
            s, e = Fill(pe, sl), Fill(pe, el)
            loaded = [Tally(t) for t in ctx_loaded]
            moved = [Tally(t) for t in keys_moved]
            blocks_t, top_t, shift_t, taken_t = (Tally(t) for t in (blocks_ready, top_ready, shift_ready, sums_ready))
            pe.wait_ge(nm.ready, 1)
            for g in range(NG):
                def fill(bank):
                    for c in range(GT):
                        last = pe.transpose(bank[:, c * P:(c + 1) * P], nm.xn[:, GT * g + c, :], ident[:, :])
                    return last
                s(fill)
            s.wait_emptied()
            pe.wait_ge(consts, 16 * N_CONSTS)
            for h in range(2):
                for g in range(NG):
                    s(lambda bank: pe.matmul(bank, wq[:, h, :], xnT[:, g * GC:(g + 1) * GC], start=True, stop=True))
            pe.wait_ge(q_ready, 5)
            for _ in range(2):
                pe.matmul(ps_o[0:32, 0:32], ones[:, :], ones[:, :], start=True, stop=True).then_inc(prob_used, 1)

            def setup_parts(u):
                def turn_ctx():
                    pe.wait_ge(ctx_loaded[u], loaded[u].next(LOADS))
                    for chunks in GROUPS:
                        def fill(bank):
                            for j in chunks:
                                r = ROWS[j]
                                last = pe.transpose(bank[:, (j % 4) * P:(j % 4) * P + r], ctx[u][0:r, j, :], ident[0:r, 0:r])
                            return last
                        s(fill)

                def project_keys():
                    s.wait_emptied()
                    for c, w in PIECES:
                        s(lambda bank: pe.matmul(bank[:, 0:w], wk[:, :], ctxT[:, c:c + w], start=True, stop=True))

                def project_values():
                    for chunks in GROUPS:
                        def fill(bank):
                            for j in chunks:
                                r = ROWS[j]
                                last = pe.matmul(bank[0:r, (j % 4) * D:(j % 4 + 1) * D], ctxT[:, j * P:j * P + r], wv[:, :],
                                                 start=True, stop=True)
                            return last
                        s(fill)

                def pair_scores(pair):
                    g, a = divmod(pair, HALF // 2)
                    if pair == 0:
                        pe.wait_ge(blocks_ready, blocks_t.next(5))
                    if a == 0:
                        pe.wait_ge(keys_moved[g], moved[g].next(16))
                    for c, w in PIECES:
                        w += w % 2
                        s(lambda bank: pe.matmul(bank[:, 0:w], qb_hi[u][g][:, a * P:(a + 1) * P], keys[u][g][:, c:c + w],
                                                 start=True, stop=True))

                def turn_top():
                    pe.wait_ge(top_ready, top_t.next())
                    s(lambda bank: pe.transpose(bank[:, 0:P], top_parts[:, :], ident[:, :]))

                return turn_ctx, [project_keys, None, None, None, *[lambda pair=pair: pair_scores(pair) for pair in range(HALF)],
                                  lambda: (turn_top(), project_values())]

            turn_ctx, parts = setup_parts(0)
            turn_ctx()
            for part in parts:
                if part:
                    part()

            def turn_sums(u):
                rows = slice(64 * u, 64 * u + 64)

                def fill(bank):
                    for i in range(4):
                        last = pe.matmul(bank[rows, i * P:(i + 1) * P], sums[:, i, :], ident[:, :], start=True, stop=True)
                    return last
                s(fill)

            def weigh(u, c, j):
                r = ROWS[j]
                pe.wait_ge(el.free, e.t.value() + el.banks - (2 if j < NCH - 1 else 0))
                p = prob[c % 2]
                for k in range(4):
                    pe.matmul(ps_o[32 * k:32 * k + 32, 0:3 * S], vals[u][0:r, j, k, :], p[0:r, 3 * S * k:3 * S * (k + 1)],
                              start=(j == 0), stop=(j == NCH - 1), skip_group_check=True)
                for k in range(4):
                    last = pe.matmul(ps_o[32 * k:32 * k + 32, 3 * S:4 * S], vals[u][0:r, j, 4 + k, :],
                                     p[0:r, (A_HEADS + k) * S:(A_HEADS + k + 1) * S],
                                     start=False, stop=(j == NCH - 1), skip_group_check=True)
                last.then_inc(prob_used, 1)

            def attend(b, u, n, first, last):
                turn_ctx, parts = (None, [None] * NCH) if last else setup_parts(1 - u)
                if not last:
                    turn_ctx()
                pe.wait_ge(shift_ready, shift_t.next(2))
                for j in range(NCH):
                    r = ROWS[j]
                    for g in range(2):
                        def fill(bank):
                            k = keys[u][g][:, j * P:j * P + r]
                            pe.matmul(bank[0:r, :], k, qb_hi[u][g][:, :], start=True, stop=False)
                            pe.matmul(bank[0:r, :], k, qb_lo[u][g][:, :], start=False, stop=False)
                            return pe.matmul(bank[0:r, :], ones_b[:, 0:r], shift[u][g][:, :], start=False, stop=True)
                        e(fill)
                    if j == 1:
                        pe.wait_ge(sums_ready, taken_t.next())
                    if j > 0:
                        weigh(u, u * NCH + j - 1, j - 1)
                    if parts[j]:
                        parts[j]()
                    if j == 1 and not first:
                        turn_sums(1 - u)
                weigh(u, u * NCH + NCH - 1, NCH - 1)

            tallies = (blocks_t, top_t, shift_t, taken_t)

            def enter(it):
                s.enter(it, 2 * (NU + TURNS))
                e.enter(it, 4 * NCH)
                for t, per in zip(tallies, (10, 2, 4, 2)):
                    t.enter(it, per)
                for t in moved:
                    t.enter(it, 32)
                for t in loaded:
                    t.enter(it, LOADS)

            def leave(n):
                for t in (s, e, *tallies, *loaded, *moved):
                    t.leave(n)

            batches(pe, enter, attend, leave)
            pe.wait_ge(sums_ready, B + 1)
            turn_sums(1)
            pe.wait_ge(att_ready, 1)
            for g in range(NG):
                def fill(bank):
                    for c in range(GT):
                        last = pe.transpose(bank[:, c * P:(c + 1) * P], att[:, GT * g + c, :], ident[:, :])
                    return last
                s(fill)
            s.wait_emptied()
            pe.wait_ge(bias_added, 1)
            for g in range(NG):
                def fill(bank):
                    pe.matmul(bank, ident[:, :], x_tok[:, GT * g:GT * (g + 1), :].rearrange("p c d -> p (c d)"),
                              start=True, stop=False, skip_group_check=True)
                    for c in range(GT):
                        n = GT * g + c
                        last = pe.matmul(bank[:, c * D:(c + 1) * D], xnT[:, n * P:(n + 1) * P], wo[:, :],
                                         start=False, stop=(c == GT - 1), skip_group_check=True)
                    return last
                s(fill)

        @block.scalar
        def _(act):
            take = Take(act, el)
            norm_scalar(act, nm)
            for _ in range(el.banks):
                act.activation(scratch[:, 0:1], ident[:, 0:1], ACT.Copy).then_inc(el.free, 1)
                act.wait_ge(el.free, _ + 1)
            blocks_t, used, free = Tally(blocks_ready), Tally(prob_used), Tally(sl.free)

            def split_keys(u, g):
                rows = half_rows(g)
                act.wait_ge(sl.free, free.value() + (len(GROUPS) + len(PIECES) + sl.banks))
                act.activation(keys[u][g][rows, 0:N_CTX], kf[rows, :], ACT.Copy).then_inc(k_hi_ready, 1)

            free.next(12)
            for g in range(2):
                split_keys(0, g)
            free.next(NU)

            def attend(b, u, n, first, last):
                act.wait_ge(blocks_ready, blocks_t.next(5))
                for j in range(NCH):
                    r = ROWS[j]
                    i = (u * NCH + j) % 2
                    act.wait_ge(prob_used, used.next())
                    for g in range(2):
                        take(lambda bank: act.activation(prob[i][0:r, g * HC:(g + 1) * HC], bank[0:r, :], ACT.Exp,
                                                         bias=bias[u][0:r, j:j + 1], scale=SCALE))
                    if j in (1, 2) and not last:
                        split_keys(1 - u, j - 1)
                free.next((0 if last else NU) + (0 if first else TURNS))

            def enter(it):
                take.enter(it, 4 * NCH)
                blocks_t.enter(it, 10)
                used.enter(it, 2 * NCH)
                free.enter(it, 2 * (NU + TURNS))

            def leave(n):
                for t in (take, blocks_t, used, free):
                    t.leave(n)

            batches(act, enter, attend, leave)

        @block.vector
        def _(dve):
            take, step = Take(dve, sl), Chain(dve, chain)
            loaded = [Tally(t) for t in ctx_loaded]
            fill_t, o_t, hi_t = Tally(fill_ready), Tally(prob_used), Tally(k_hi_ready)
            o_t.next(2)
            for _ in range(sl.banks):
                dve.memset(scratch[:, 1:2], 0.0).then_inc(sl.free, 1)
                dve.wait_ge(sl.free, _ + 1)
            dve.memset(scratch[:, 1:2], 0.0).then_inc(sums_ready, 1)
            norm_vector(dve, nm, x_tok, step.t)
            for g in range(NG):
                take(lambda bank: dve.tensor_copy(xnT[:, g * GC:(g + 1) * GC], bank))
            dve.wait_ge(consts, 16 * N_CONSTS)
            dve.tensor_scalar(key_fill[:, :, 0:FULL], mask_col[:, :, :], -1.0, -MASK_FILL * SCALE, ALU.add,
                              ALU.mult).then_inc(key_fill_ready, 1)
            dve.tensor_scalar(key_fill[:, :, FULL], mask_tail[:, :], -1.0, -MASK_FILL * SCALE, ALU.add,
                              ALU.mult).then_inc(key_fill_ready, 1)
            for h in range(2):
                for g in range(NG):
                    part = slice(g * GC, (g + 1) * GC)
                    take(lambda bank: dve.tensor_scalar(qf[:, :], bank, bq[:, h:h + 1], None, ALU.add))
                    take.wait_taken()
                    step(dve.tensor_copy(q_hi[h][:, part], qf[:, :]))
                    dve.tensor_tensor(q_lo[h][:, part], qf[:, :], q_hi[h][:, part], ALU.subtract).then_inc(key_fill_ready, 1)
                    dve.wait_ge(key_fill_ready, 2 + h * NG + g + 1)

            def take_turned(n, u):
                rows = slice(64 * u, 64 * u + 64)
                dst = att[rows, n, :] if isinstance(n, int) else att[rows, bass.ds(n, 1), :].rearrange("p a d -> p (a d)")
                dst3 = dst[:, 0:A_HEADS * HD].rearrange("p (k i d) -> p i k d", k=4, d=HD)
                dst1 = dst[:, A_HEADS * HD:D].rearrange("p (k d) -> p k d", d=HD)

                def out_of(bank):
                    b = bank[rows, :]
                    step(dve.reciprocal(recip[rows, :, :], b.rearrange("p (i k c) -> p i k c", i=4, k=4)[:, :, :, DEN]))
                    src3 = b[:, 0:3 * (P + HD)].rearrange("p (i x) -> p i x", i=3)[:, :, 0:P]
                    step(dve.tensor_tensor(dst3, src3.rearrange("p i (k c) -> p i k c", k=4)[:, :, :, 0:HD],
                                           recip[rows, 0:3, :].unsqueeze(3).broadcast_to([64, 3, 4, HD]), ALU.mult))
                    return dve.tensor_tensor(dst1, b[:, 3 * P:4 * P].rearrange("p (k c) -> p k c", k=4)[:, :, 0:HD],
                                             over(recip[rows, 3, :], HD), ALU.mult)
                take(out_of)

            def setup(u, before):
                for chunks in GROUPS:
                    c0, w = chunks[0] * P, sum(ROWS[j] for j in chunks)
                    take(lambda bank: dve.tensor_copy(ctxT[:, c0:c0 + w], bank[:, 0:w]))
                dve.wait_ge(ctx_loaded[u], loaded[u].next(LOADS))
                for c, w in PIECES:
                    take(lambda bank: dve.scalar_tensor_tensor(out=kf[:, c:c + w], in0=bank[:, 0:w], scalar=bk[:, 0:1],
                                                               in1=mask_row[u][:, c:c + w], op0=ALU.add, op1=ALU.mult))
                if before is not None:
                    take_turned(*before)
                for g in range(2):
                    rows = half_rows(g)
                    dve.wait_ge(k_hi_ready, hi_t.next())
                    dve.tensor_tensor(k_lo[rows, :], kf[rows, :], keys[u][g][rows, 0:N_CTX], ALU.subtract).then_inc(k_lo_ready, 1)
                dve.wait_ge(fill_ready, fill_t.next())
                for pair in range(HALF):
                    for i, (c, w) in enumerate(PIECES):
                        wait_apart(dve, (consts, 16 * N_CONSTS), [(sl.full, take.t.next()), (sl.free, take.t.value() + (sl.banks - 2))])
                        dve.tensor_tensor_reduce(junk[:, take.k % 2, 0:w], sl.ps[:, take.k % sl.banks, 0:w], fill_row[:, c:c + w], 1.0,
                                                 -3.0e38, ALU.add, ALU.max, tops[:, pair, i:i + 1]).then_inc(sl.free, 1)
                        take.k += 1
                take.wait_taken()
                step(dve.tensor_reduce(top[:, :], tops[:, :, :], X, ALU.max))
                step(dve.tensor_scalar(top_hi[:, :], top[:, :], -1.0, None, ALU.mult))
                step(dve.scalar_tensor_tensor(out=top_lo[:, :], in0=top[:, :], scalar=-1.0, in1=top_hi[:, :],
                                              op0=ALU.mult, op1=ALU.subtract))
                slots = top_parts[:, :].rearrange("p (g i) -> p g i", g=2)[:, :, 0:8].rearrange("p g (a part) -> p g a part", part=2)
                step(dve.tensor_copy(slots[:, :, :, 0], top_hi[:, :].rearrange("p (g a) -> p g a", g=2)))
                dve.tensor_copy(slots[:, :, :, 1], top_lo[:, :].rearrange("p (g a) -> p g a", g=2)).then_inc(top_ready, 1)
                take(lambda bank: dve.tensor_copy(topT[:, :], bank[:, 0:P]))
                for chunks in GROUPS:
                    r, w, j = ROWS[chunks[0]], len(chunks), chunks[0]

                    def out_of(bank):
                        src, dst, cut = bank[0:r, 0:w * D].rearrange("p (j d) -> p j d", j=w), vals[u][0:r, j:j + w, :, :], A_HEADS * HD
                        dve.tensor_copy(dst[:, :, 0:4, 0:3 * HD], src[:, :, 0:cut].rearrange("p j (k d) -> p j k d", k=4))
                        return dve.tensor_copy(dst[:, :, 4:8, 0:HD], src[:, :, cut:D].rearrange("p j (k d) -> p j k d", k=4))
                    take(out_of)

            dve.wait_ge(q_ready, 5)
            setup(0, None)

            def attend(b, u, n, first, last):
                if last:
                    take_turned(n, 1 - u)
                else:
                    setup(1 - u, None if first else (n, 1 - u))
                dve.wait_ge(prob_used, o_t.next(NCH))
                dve.tensor_copy(flat(sums[:, :, :]), ps_o[:, :]).then_inc(sums_ready, 1)

            tallies = (take, step, *loaded, fill_t, o_t, hi_t)

            def enter(it):
                for t, per in zip(tallies, (2 * (NU + TURNS), 12, LOADS, LOADS, 2, 2 * NCH, 4)):
                    t.enter(it, per)

            def leave(n):
                for t in tallies:
                    t.leave(n)

            batches(dve, enter, attend, leave)
            take_turned(NT - 1, 1)
            take.wait_taken()
            dve.tensor_tensor(att[:, :, :], att[:, :, :], under(bv[:, :], NT), ALU.add).then_inc(att_ready, 1)
            for g in range(NG):
                take(lambda bank: dve.tensor_copy(xnT[:, g * GC:(g + 1) * GC], bank))
            for g in range(NG):
                take(lambda bank: dve.tensor_copy(x_tok[:, GT * g:GT * (g + 1), :], bank.rearrange("p (c d) -> p c d", c=GT)))


def program(nc, io):
    with ExitStack() as stack:
        m = Memory(nc, stack, "all")
        ident = m.sb("ident", [P, P])
        x_tok = m.sb("x_tok", [P, NT, D])
        loaded = m.sem("loaded")
        stored = m.sem("stored")
        x_dram = io["x"].rearrange("b s d -> (b s) d").rearrange("(n p) d -> p n d", p=P)
        with nc.Block() as block:
            @block.sync
            def _(sp):
                sp.dma_start(ident[:, :], io["ident"]).then_inc(loaded, 16)
                sp.dma_start(x_tok[:, :, :], x_dram).then_inc(loaded, 16)
                sp.wait_ge(loaded, 32)
        for part in PARTS:
            part(nc, io, x_tok, ident)
        with nc.Block() as block:
            @block.sync
            def _(sp):
                sp.dma_start(io["out"].rearrange("b s d -> (b s) d").rearrange("(n p) d -> p n d", p=P), x_tok[:, :, :]).then_inc(stored, 16)
                sp.wait_ge(stored, 16)


PARTS = (cross_attention_0, linear_attention_0, ffn_0, cross_attention_1, linear_attention_1, moe_top1)


def constants():
    pos = np.arange(P)[:, None] % S
    freq = (1.0 / np.float32(10000.0) ** np.arange(0, HD, 2, dtype=np.float32)).astype(np.float32)
    angle = (pos.astype(np.float32) * freq[None, :]).astype(np.float32)
    rope = np.zeros((P, 2, HD), np.float32)
    rope[:, 0, 0::2] = rope[:, 0, 1::2] = np.cos(angle)
    rope[:, 1, 0::2], rope[:, 1, 1::2] = -np.sin(angle), np.sin(angle)
    head = np.arange(D) // HD
    own = (head[:, None] == head[None, :]).astype(np.float32)
    row = np.arange(P)
    half_head = (row[:, None] % 64 // HD == np.arange(H // 2)[None, :]).astype(np.float32)
    pair_row = np.zeros((P, 2, 4), np.float32)
    for g in range(2):
        for a in range(4):
            pair_row[64 * g + 2 * a:64 * g + 2 * a + 2, g, a] = 1
    causal = np.where(np.arange(S)[None, :] <= row[:, None] % S, 0.0, CAUSAL_FILL).astype(np.float32)
    parity = (np.arange(H)[None, :] % 2 == row[:, None] // 64).astype(np.float32)
    return {"causal": causal, "head_parity": parity, "half_head": half_head, "pair_row": pair_row,
            "ident": np.eye(P, dtype=np.float32), "rope": rope, "own_head": own,
            "rank": np.tile(np.arange(E, 0, -1, dtype=np.float32), (P, 1)),
            "own_head_scaled": (own / np.sqrt(np.float32(HD))).astype(np.float32)}


def layout(inputs):
    a = {k: np.asarray(v) for k, v in inputs.items()}
    for name in ("L0_xattn_Wq", "L0_xattn_Wv", "L0_xattn_Wo", "L1_attn_w_qkv", "L1_attn_w_out", "L1_ffn_gate_w", "L1_xattn_Wk",
                 "L1_xattn_Wv", "L1_xattn_Wo"):
        a[name + "T"] = np.ascontiguousarray(a.pop(name).T)
    a["L1_ffn_b1T"] = np.ascontiguousarray(a.pop("L1_ffn_b1").reshape(E, FF // P, P).transpose(2, 0, 1).reshape(P, -1))
    wt = a.pop("L1_xattn_Wq").T.reshape(D, 2, 1, D // 2)
    a["L1_xattn_WqT2"] = np.ascontiguousarray(np.repeat(wt, 2, axis=2).reshape(D, 2, D))
    bt = a.pop("L1_xattn_bq").reshape(2, 1, D // 2)
    a["L1_xattn_bq2"] = np.ascontiguousarray(np.repeat(bt, 2, axis=1).reshape(2, D).T)
    a["L1_xattn_bkT"] = a.pop("L1_xattn_bk").reshape(D, 1)
    mask = a.pop("mask_BxS2_bf1").view(np.uint8)
    full = mask[:, :FULL * P].reshape(B, P, FULL)
    a["mask_row"] = np.ascontiguousarray(np.concatenate([full.transpose(0, 2, 1).reshape(B, -1), mask[:, FULL * P:]], 1))
    a["mask"] = mask
    a["mask_tail"] = np.ascontiguousarray(mask[:, FULL * P:].T)
    return {**a, **constants()}


def kernel(**inputs):
    import concourse.bacc as bacc
    from concourse.bass_utils import run_bass_kernel_spmd

    nc = bacc.Bacc("TRN2", target_bir_lowering=False, num_devices=1)
    arrays = layout(inputs)
    io = {name: nc.dram_tensor(f"in_{name}", a.shape, mybir.dt.from_np(a.dtype), kind="ExternalInput").ap()
          for name, a in arrays.items()}
    io["out"] = nc.dram_tensor("out", (B, S, D), F32, kind="ExternalOutput").ap()
    program(nc, io)
    result = run_bass_kernel_spmd(nc, [{f"in_{name}": a for name, a in arrays.items()}], core_ids=[0])
    return result.results[0]["out"]
```

```python
from contextlib import ExitStack

import numpy as np

import concourse.bass as bass
from concourse import mybir

F32 = mybir.dt.float32
F32R = mybir.dt.float32r
BF16 = mybir.dt.bfloat16
U8 = mybir.dt.uint8
ALU = mybir.AluOpType
ACT = mybir.ActivationFunctionType
X = mybir.AxisListType.X

P = 128
B, S, D = 32, 64, 128
N_CTX = 1601
NT = B * S // P
NCH = (N_CTX + P - 1) // P
FULL = NCH - 1
TAIL = N_CTX - FULL * P
H, HD = 16, 8
NG = 4
GT = NT // NG
GC = GT * P
LN_EPS = 1e-5
RMS_EPS = 1e-5
CAUSAL_FILL = -1e30
ROWS = [P] * FULL + [TAIL]
GROUPS = [list(range(i, min(i + 4, NCH))) for i in range(0, NCH, 4)]


class Tally:

    def __init__(self, sem):
        self.sem, self.base, self.n, self.it, self.per = sem, 0, 0, None, 0

    def next(self, k=1):
        self.n += k
        return self.value()

    def value(self):
        return self.base + self.n if self.it is None else self.it * self.per + (self.base + self.n)

    def enter(self, it, per):
        self.base, self.n, self.it, self.per = self.base + self.n, 0, it, per

    def leave(self, times):
        assert self.n == self.per, (self.n, self.per)
        self.base, self.n, self.it = self.base + self.per * times, 0, None


def wait_apart(eng, constant, waits):
    waits = [(sem, value if isinstance(value, int) else eng.to_reg(value)) for sem, value in waits]
    eng.wait_ge(*constant)
    for sem, value in waits:
        eng.wait_ge(sem, value)


class Memory:

    def __init__(self, nc, stack, prefix):
        self.nc, self.stack, self.prefix = nc, stack, prefix

    def sb(self, name, shape, dt=F32):
        return self.stack.enter_context(self.nc.sbuf_tensor(f"{self.prefix}_{name}", shape, dt))

    def psum(self, name, shape, dt=F32):
        return self.stack.enter_context(self.nc.psum_tensor(f"{self.prefix}_{name}", shape, dt))

    def sem(self, name):
        return self.stack.enter_context(self.nc.semaphore(f"{self.prefix}_{name}"))


def over(ap, n):
    return ap.unsqueeze(2).broadcast_to([ap.shape[0], ap.shape[1], n])


def under(ap, n):
    return ap.unsqueeze(1).broadcast_to([ap.shape[0], n, ap.shape[1]])


class Norm:

    def __init__(self, m):
        self.xn = m.sb("xn", [P, NT, D])
        self.parts = m.sb("ln_parts", [P, NT, 6])
        self.stats = m.sb("ln_stats", [P, NT, 2])
        self.var, self.std, self.rstd = (m.sb("ln_" + s, [P, NT]) for s in ("var", "std", "rstd"))
        self.var_ready, self.std_ready, self.ready = (m.sem("ln_" + s) for s in ("var_ready", "std_ready", "ready"))

    def begin(self, dve, x_tok, step, g):
        s = GT * g
        for out_of in (lambda c: dve.bn_stats(self.parts[:, s + c, :], x_tok[:, s + c, :]),
                       lambda c: dve.bn_aggr(self.stats[:, s + c, :], self.parts[:, s + c, :])):
            for c in range(GT):
                out_of(c).then_inc(step.sem, 1)
            dve.wait_ge(step.sem, step.t.next(GT))
        dve.tensor_scalar(self.var[:, s:s + GT], self.stats[:, s:s + GT, 1], LN_EPS, None, ALU.add).then_inc(self.var_ready, 1)

    def finish(self, dve, x_tok, step, g):
        s = GT * g
        dve.wait_ge(self.std_ready, g + 1)
        step(dve.reciprocal(self.rstd[:, s:s + GT], self.std[:, s:s + GT]))
        for c in range(GT):
            dve.tensor_scalar(self.xn[:, s + c, :], x_tok[:, s + c, :], self.stats[:, s + c, 0:1], self.rstd[:, s + c:s + c + 1],
                              ALU.subtract, ALU.mult).then_inc(self.ready, 1)

    def vector(self, dve, x_tok, step):
        for g in range(NG + 1):
            if g < NG:
                self.begin(dve, x_tok, step, g)
            if g > 0:
                self.finish(dve, x_tok, step, g - 1)

    def scalar(self, act):
        for s in range(0, NT, GT):
            act.wait_ge(self.var_ready, s // GT + 1)
            act.activation(self.std[:, s:s + GT], self.var[:, s:s + GT], ACT.Sqrt).then_inc(self.std_ready, 1)


def load_ctx(eng, dst, src, sem):
    eng.dma_start(dst[:, 0:FULL, :], src[0:FULL * P, :].rearrange("(p j) c -> p j c", j=FULL)).then_inc(sem, 16)
    eng.dma_start(dst[0:TAIL, FULL, :], src[FULL * P:N_CTX, :]).then_inc(sem, 16)


def cross_attention_0(nc, io, x_tok, ident):
    NBUF = 4
    with ExitStack() as stack:
        m = Memory(nc, stack, "xa0")
        wq, wk, wv, wo = (m.sb(n, [P, D]) for n in ("wqT", "wk", "wvT", "woT"))
        bq, bk, bv = (m.sb(n, [P, 1]) for n in ("bq", "bk", "bv"))
        bo = m.sb("bo", [P, D])
        nm = Norm(m)
        xnT = m.sb("xnT", [P, NT * P])
        qT = m.sb("qT", [P, NT * P])
        fT = m.sb("fT", [P, NT * P])
        q_bk = m.sb("q_bk", [P, NT])
        ctx = [m.sb(f"ctx{u}", [P, 2, NCH, D]) for u in range(NBUF)]
        ctxT = m.sb("ctxT", [P, 2, N_CTX])
        fold = [m.sb(f"fold{u}", [P, P]) for u in range(2)]
        prob = m.sb("prob", [P, N_CTX])
        probT = m.sb("probT", [P, NCH, P])
        top = m.sb("top", [P, 1])
        shifted = m.sb("shifted", [P, 1])
        shift = m.sb("shift", [P, 1])
        total = m.sb("total", [P, 2])
        inv = m.sb("inv", [P, 1])
        att = m.sb("att", [P, NT, D])

        ps_s = m.psum("ps_s", [P, 4, 512])
        ps_t = m.psum("ps_t", [P, 3, 512])
        ps_o = m.psum("ps_o", [P, 512])
        ps_b = ps_o[:, 512 - NT:512]

        weights = m.sem("weights")
        ctx_loaded = [m.sem(f"ctx_loaded{u}") for u in range(NBUF)]
        chain = m.sem("vector_chain")
        turn_full = [m.sem(f"turn_full{i}") for i in range(2)]
        turn_free = [m.sem(f"turn_free{i}") for i in range(2)]
        q_bk_full = m.sem("q_bk_full")
        q_bk_ready = m.sem("q_bk_ready")
        fold_ready = m.sem("fold_ready")
        scores_full = m.sem("scores_full")
        shift_ready = m.sem("shift_ready")
        prob_ready = m.sem("prob_ready")
        attended = m.sem("attended")
        att_ready = m.sem("att_ready")
        bias_added = m.sem("bias_added")
        block = stack.enter_context(nc.Block())
        PAIR_TURNS = 3 * len(GROUPS)

        @block.sync
        def _(sp):
            for dst, src in ((wq, "L0_xattn_WqT"), (wk, "L0_xattn_Wk"), (wv, "L0_xattn_WvT"), (wo, "L0_xattn_WoT")):
                sp.dma_start(dst[:, :], io[src]).then_inc(weights, 16)
            for dst, src in ((bq, "L0_xattn_bq"), (bk, "L0_xattn_bk"), (bv, "L0_xattn_bv")):
                sp.dma_start(dst[:, :], io[src].rearrange("(p a) -> p a", a=1)).then_inc(weights, 16)
            sp.dma_start(bo[:, :], io["L0_xattn_bo"].rearrange("(a n) -> a n", a=1).broadcast_to([P, D])).then_inc(weights, 16)
            for u in range(NBUF):
                for b in range(2):
                    load_ctx(sp, ctx[u][:, b], io["ctx_1024"][2 * u + b], ctx_loaded[u])
            with sp.Fori(0, NT // NBUF - 1) as it:
                for u in range(NBUF):
                    sp.wait_ge(attended, it * NBUF + (u + 1))
                    for b in range(2):
                        load_ctx(sp, ctx[u][:, b], io["ctx_1024"][bass.ds(it * (2 * NBUF) + (2 * (NBUF + u) + b), 1)]
                                 .rearrange("a t c -> (a t) c"), ctx_loaded[u])

        def pairs(eng, enter, body, leave):
            with eng.Fori(0, NT // NBUF - 1) as it:
                enter(it)
                for u in range(NBUF):
                    body(it * NBUF + u, u, False)
                leave(NT // NBUF - 1)
            for u in range(NBUF):
                body(NT - NBUF + u, u, u == NBUF - 1)

        @block.gpsimd
        def _(pool):
            pool.wait_ge(turn_free[0], 6)
            pool.wait_ge(turn_free[1], 6)
            for u in range(2):
                pool.tensor_copy(fold[u][:, :], fT[:, u * P:(u + 1) * P]).then_inc(fold_ready, 1)
            with pool.Fori(0, NT // 2 - 1) as it:
                for u in range(2):
                    pool.wait_ge(scores_full, it * 2 + (u + 1))
                    pool.tensor_copy(fold[u][:, :], fT[:, bass.ds(it * (2 * P) + (2 + u) * P, P)]).then_inc(fold_ready, 1)
            pool.wait_ge(nm.ready, NT)
            pool.wait_ge(weights, 16 * 8)
            pool.tensor_tensor(x_tok[:, :, :], x_tok[:, :, :], under(bo[:, :], NT), ALU.add).then_inc(bias_added, 1)

        class Turns:

            def __init__(self):
                self.k = 0
                self.free = [Tally(s) for s in turn_free]

            def enter(self, it, per):
                for t in self.free:
                    t.enter(it, per // 2)

            def leave(self, times):
                for t in self.free:
                    t.leave(times)

        @block.tensor
        def _(pe):
            t = Turns()

            def turn(fill):
                i = t.k % 2
                if t.k >= 3:
                    pe.wait_ge(turn_free[1 - i], t.free[1 - i].value() - 1)
                t.free[i].next()
                fill(ps_t[:, t.k % 3, :]).then_inc(turn_full[i], 1)
                t.k += 1

            def transposes(src):
                def fill(bank):
                    for c in range(4):
                        last = pe.transpose(bank[:, c * P:(c + 1) * P], src(c), ident[:, :])
                    return last
                return fill

            def project(w, src):
                return lambda bank: pe.matmul(bank, w[:, :], src, start=True, stop=True)

            for g in range(NG):
                pe.wait_ge(nm.ready, GT * (g + 1))
                turn(transposes(lambda c: nm.xn[:, 4 * g + c, :]))
            pe.wait_ge(weights, 16 * 8)
            for g in range(NG):
                pe.wait_ge(turn_free[g % 2], g // 2 + 1)
                turn(project(wq, xnT[:, g * 512:(g + 1) * 512]))
            for g in range(NG):
                pe.wait_ge(turn_free[g % 2], 2 + g // 2 + 1)
                turn(project(wk, qT[:, g * 512:(g + 1) * 512]))
            for n in range(NT):
                last = pe.matmul(ps_b[:, n:n + 1], qT[:, n * P:(n + 1) * P], bk[:, :], start=True, stop=True)
            last.then_inc(q_bk_full, 1)

            loaded = [Tally(s) for s in ctx_loaded]
            folded = Tally(fold_ready)
            done_p = Tally(prob_ready)

            def turn_ctx(u):
                pe.wait_ge(ctx_loaded[u], loaded[u].next(64))
                for b in range(2):
                    for chunks in GROUPS:
                        def fill(bank):
                            for j in chunks:
                                r = ROWS[j]
                                last = pe.transpose(bank[:, (j % 4) * P:(j % 4) * P + r],
                                                    ctx[u][0:r, b, j, :], ident[0:r, 0:r])
                            return last
                        turn(fill)

            def turn_probs():
                pe.wait_ge(prob_ready, done_p.next())
                for chunks in GROUPS:
                    def fill(bank):
                        for j in chunks:
                            r = ROWS[j]
                            c0 = chunks[0] * P + (j % 4) * P
                            last = pe.transpose(bank[0:r, (j % 4) * P:(j % 4 + 1) * P], prob[:, c0:c0 + r], ident[:, :])
                        return last
                    turn(fill)

            def scores(u):
                pe.wait_ge(fold_ready, folded.next())
                for c in range(0, N_CTX, 512):
                    w = min(512, N_CTX - c)
                    for b in range(2):
                        last = pe.matmul(ps_s[64 * b:64 * b + 64, c // 512, 0:w], fold[u % 2][:, 64 * b:64 * b + 64],
                                         ctxT[:, b, c:c + w], start=True, stop=True)
                last.then_inc(scores_full, 1)

            def wait_turned():
                for i in range(2):
                    pe.wait_ge(turn_free[i], t.free[i].value())

            def attend(n, u, last_pair):
                if not last_pair:
                    turn_ctx((u + 1) % NBUF)
                turn_probs()
                wait_turned()
                if not last_pair:
                    scores((u + 1) % NBUF)
                for j in range(NCH):
                    r = ROWS[j]
                    for b in range(2):
                        last = pe.matmul(ps_o[64 * b:64 * b + 64, 0:D], probT[0:r, j, 64 * b:64 * b + 64],
                                         ctx[u][0:r, b, j, :], start=(j == 0), stop=(j == NCH - 1))
                last.then_inc(attended, 1)

            def enter(it):
                t.enter(it, NBUF * PAIR_TURNS)
                for tally, per in ((folded, NBUF), (done_p, NBUF), *[(x, 64) for x in loaded]):
                    tally.enter(it, per)

            def leave(times):
                for tally in (t, folded, done_p, *loaded):
                    tally.leave(times)

            turn_ctx(0)
            wait_turned()
            scores(0)
            pairs(pe, enter, attend, leave)

            pe.wait_ge(att_ready, NT)
            base = [t.free[i].value() for i in range(2)]
            for g in range(NG):
                turn(transposes(lambda c: att[:, 4 * g + c, :]))
            for g in range(NG):
                pe.wait_ge(turn_free[g % 2], base[g % 2] + g // 2 + 1)
                cols = slice(g * 512, (g + 1) * 512)

                def fill(bank):
                    pe.matmul(bank, wv[:, :], fT[:, cols], start=True, stop=False)
                    return pe.matmul(bank, ident[:, :], xnT[:, cols], start=False, stop=True)
                turn(fill)
            pe.wait_ge(bias_added, 1)
            for g in range(NG):
                pe.wait_ge(turn_free[g % 2], base[g % 2] + 2 + g // 2 + 1)

                def fill(bank):
                    pe.matmul(bank, ident[:, :], x_tok[:, 4 * g:4 * g + 4, :].rearrange("p n d -> p (n d)"),
                              start=True, stop=False, skip_group_check=True)
                    for c in range(4):
                        n = 4 * g + c
                        last = pe.matmul(bank[:, c * P:(c + 1) * P], qT[:, n * P:(n + 1) * P], wo[:, :],
                                         start=False, stop=(c == 3), skip_group_check=True)
                    return last
                turn(fill)

        def empty(eng, full, i, out_of):
            eng.wait_ge(turn_full[i], full.next())
            out_of(ps_t[:, (2 * taken[i] + i) % 3, :]).then_inc(turn_free[i], 1)
            taken[i] += 1

        taken = [0, 0]

        def common(eng, i, copy, add, mid_q, softmax, finish, enter, leave):
            full = Tally(turn_full[i])
            for g in range(i, NG, 2):
                empty(eng, full, i, lambda bank: copy(xnT[:, g * 512:(g + 1) * 512], bank))
            eng.wait_ge(weights, 16 * 8)
            for g in range(i, NG, 2):
                empty(eng, full, i, lambda bank: add(qT[:, g * 512:(g + 1) * 512], bank, bq))
            for g in range(i, NG, 2):
                empty(eng, full, i, lambda bank: copy(fT[:, g * 512:(g + 1) * 512], bank))
            mid_q()

            def take_ctx():
                k = 0
                for b in range(2):
                    for chunks in GROUPS:
                        c0 = chunks[0] * P
                        w = sum(ROWS[j] for j in chunks)
                        if k % 2 == i:
                            empty(eng, full, i, lambda bank: copy(ctxT[:, b, c0:c0 + w], bank[:, 0:w]))
                        k += 1

            def take_probs():
                for k, chunks in enumerate(GROUPS):
                    r = ROWS[chunks[0]]
                    w = len(chunks)
                    if k % 2 == i:
                        empty(eng, full, i, lambda bank: copy(probT[0:r, chunks[0]:chunks[0] + w, :],
                                                              bank[0:r, 0:w * P].rearrange("p (j q) -> p j q", j=w)))

            def body(n, u, last):
                if not last:
                    take_ctx()
                take_probs()
                if not last:
                    softmax(n + 1, (u + 1) % 2)
                finish(n, u % 2)

            take_ctx()
            softmax(0, 0)
            pairs(eng, lambda it: enter(full, it), body, lambda times: leave(full, times))
            for g in range(i, NG, 2):
                empty(eng, full, i, lambda bank: copy(fT[:, g * 512:(g + 1) * 512], bank))
            for g in range(i, NG, 2):
                empty(eng, full, i, lambda bank: add(qT[:, g * 512:(g + 1) * 512], bank, bv))
            for g in range(i, NG, 2):
                empty(eng, full, i, lambda bank: copy(x_tok[:, 4 * g:4 * g + 4, :].rearrange("p n d -> p (n d)"), bank))

        @block.scalar
        def _(act):
            nm.scalar(act)

            def copy(dst, src):
                return act.activation(dst, src, ACT.Copy)

            def add(dst, src, bias):
                return act.activation(dst, src, ACT.Identity, bias=bias[:, 0:1])

            def softmax(n, u):
                act.wait_ge(shift_ready, n + 1)
                act.activation(prob[:, :], ps_s[:, :, :].rearrange("p a b -> p (a b)")[:, 0:N_CTX], ACT.Exp,
                               bias=shift[:, 0:1], scale=float(D) ** -0.5,
                               accum_out=total[:, u:u + 1]).then_inc(prob_ready, 1)

            common(act, 1, copy, add, lambda: None, softmax, lambda n, u: None,
                   lambda full, it: full.enter(it, NBUF * PAIR_TURNS // 2), lambda full, times: full.leave(times))

        @block.vector
        def _(dve):
            step = Chain(dve, chain)
            nm.vector(dve, x_tok, step)

            def copy(dst, src):
                return dve.tensor_copy(dst, src)

            def add(dst, src, bias):
                return dve.tensor_scalar(dst, src, bias[:, 0:1], None, ALU.add)

            def mid_q():
                dve.wait_ge(q_bk_full, 1)
                dve.tensor_copy(q_bk[:, :], ps_b).then_inc(q_bk_ready, 1)
                dve.wait_ge(q_bk_ready, 1)

            def softmax(n, u):
                dve.wait_ge(scores_full, n + 1)
                step(dve.tensor_reduce(top[:, :], ps_s[:, :, :].rearrange("p a b -> p (a b)")[:, 0:N_CTX], X, ALU.max))
                step(dve.tensor_tensor(shifted[:, :], top[:, :], q_bk[:, bass.ds(n, 1)], ALU.add))
                step(dve.tensor_tensor(shift[:, :], q_bk[:, bass.ds(n, 1)], shifted[:, :], ALU.subtract))
                dve.tensor_scalar(shift[:, :], shift[:, :], float(D) ** -0.5, None, ALU.mult).then_inc(shift_ready, 1)

            def finish(n, u):
                dve.wait_ge(attended, n + 1)
                step(dve.reciprocal(inv[:, :], total[:, u:u + 1]))
                dve.tensor_scalar(att[:, bass.ds(n, 1), :].rearrange("p a d -> p (a d)"), ps_o[:, 0:D], inv[:, 0:1], None,
                                  ALU.mult).then_inc(att_ready, 1)

            def enter(full, it):
                full.enter(it, NBUF * PAIR_TURNS // 2)
                step.enter(it, 4 * NBUF)

            def leave(full, times):
                full.leave(times)
                step.leave(times)

            common(dve, 0, copy, add, mid_q, softmax, finish, enter, leave)


def flat(ap):
    return ap.rearrange("p a b -> p (a b)")


class Lane:

    def __init__(self, m, name, banks=2):
        self.banks = banks
        self.ps = m.psum(name, [P, banks, 512])
        self.full = m.sem(name + "_full")
        self.free = m.sem(name + "_free")


class Fill:

    def __init__(self, pe, lane):
        self.pe, self.lane, self.k, self.t = pe, lane, 0, Tally(lane.free)

    def __call__(self, matmuls):
        self.pe.wait_ge(self.lane.free, self.t.next())
        matmuls(self.lane.ps[:, self.k % self.lane.banks, :]).then_inc(self.lane.full, 1)
        self.k += 1

    def wait_emptied(self):
        self.pe.wait_ge(self.lane.free, self.t.value() + self.lane.banks)

    def enter(self, it, per):
        assert per % self.lane.banks == 0
        self.t.enter(it, per)

    def leave(self, times):
        self.t.leave(times)


class Take:

    def __init__(self, eng, lane):
        self.eng, self.lane, self.k, self.t = eng, lane, 0, Tally(lane.full)

    def __call__(self, out_of):
        self.eng.wait_ge(self.lane.full, self.t.next())
        out_of(self.lane.ps[:, self.k % self.lane.banks, :]).then_inc(self.lane.free, 1)
        self.k += 1

    def wait_taken(self):
        self.eng.wait_ge(self.lane.free, self.t.value() + self.lane.banks)

    def enter(self, it, per):
        self.t.enter(it, per)

    def leave(self, times):
        self.t.leave(times)


def prime(eng, lane, put):
    for k in range(lane.banks):
        put().then_inc(lane.free, 1)
        eng.wait_ge(lane.free, k + 1)


class Chain:

    def __init__(self, eng, sem):
        self.eng, self.sem, self.t = eng, sem, Tally(sem)

    def __call__(self, ins):
        ins.then_inc(self.sem, 1)
        self.eng.wait_ge(self.sem, self.t.next())

    def enter(self, it, per):
        self.t.enter(it, per)

    def leave(self, times):
        self.t.leave(times)


def groups(eng, enter, body, leave):
    with eng.Fori(0, NG - 1) as it:
        enter(it)
        body(it, False)
        leave(NG - 1)
    body(NG - 1, True)


def load_row(eng, dst, src, sem):
    eng.dma_start(dst, src.rearrange("(a n) -> a n", a=1).broadcast_to([P, src.shape[0]])).then_inc(sem, 16)


def linear_attention_0(nc, io, x_tok, ident):
    with ExitStack() as stack:
        m = Memory(nc, stack, "la0")
        wqkv = m.sb("wqkv", [P, 3, D])
        bqkv = m.sb("bqkv", [P, 3, D])
        wo = m.sb("wo", [P, D])
        bo = m.sb("bo", [P, D])
        rope = m.sb("rope", [P, 2, HD])
        own = m.sb("own", [P, D])
        nm = Norm(m)
        xb = m.sb("xb", [P, NT, D])
        xnT = m.sb("xnT", [P, NT * P])
        qkv = m.sb("qkv", [P, NT, 3 * D])
        cross = m.sb("cross", [P, NT, 2 * D])
        rot = m.sb("rot", [P, NT, 2 * D])
        qT = m.sb("qT", [P, NT * P])
        kv = m.sb("kv", [P, 2, NT, D])
        ctxT = m.sb("ctxT", [P, NT * P])
        scratch = m.sb("scratch", [P, 2])
        vl = Lane(m, "vector_lane")
        sl = Lane(m, "scalar_lane")
        consts = m.sem("consts")
        chain = m.sem("vector_chain")
        xb_ready = m.sem("xb_ready")
        rotated = m.sem("rotated")
        block = stack.enter_context(nc.Block())
        N_CONSTS = 10

        def tiles(g):
            return slice(GT * g, GT * (g + 1))

        def tokens(g):
            return slice(GC * g, GC * (g + 1))

        def skewed(project, outer_products, output):
            for g in range(NG + 2):
                if g < NG:
                    project(g)
                if 1 <= g <= NG:
                    outer_products(g - 1)
                if g >= 2:
                    output(g - 2)

        @block.sync
        def _(sp):
            for i, n in enumerate("qkv"):
                sp.dma_start(wqkv[:, i, :], io["L0_attn_W" + n]).then_inc(consts, 16)
                load_row(sp, bqkv[:, i, :], io["L0_attn_b" + n], consts)
            sp.dma_start(wo[:, :], io["L0_attn_Wo"]).then_inc(consts, 16)
            load_row(sp, bo[:, :], io["L0_attn_bo"], consts)
            sp.dma_start(rope[:, :, :], io["rope"]).then_inc(consts, 16)
            sp.dma_start(own[:, :], io["own_head_scaled"]).then_inc(consts, 16)

        @block.gpsimd
        def _(pool):
            pool.wait_ge(consts, 16 * N_CONSTS)
            pool.tensor_tensor(xb[:, :, :], x_tok[:, :, :], under(bo[:, :], NT), ALU.add).then_inc(xb_ready, 1)

        @block.tensor
        def _(pe):
            v, s = Fill(pe, vl), Fill(pe, sl)
            pe.wait_ge(consts, 16 * N_CONSTS)
            products_ready = {}

            def turn(src):
                def fill(bank):
                    for c in range(GT):
                        last = pe.transpose(bank[:, c * P:(c + 1) * P], src(c), ident[:, :])
                    return last
                s(fill)

            def project(g):
                pe.wait_ge(nm.ready, GT * (g + 1))
                turn(lambda c: nm.xn[:, GT * g + c, :])
                s.wait_emptied()
                for n in range(GT * g, GT * (g + 1)):
                    v(lambda bank: pe.matmul(bank[:, 0:3 * D], xnT[:, n * P:(n + 1) * P], flat(wqkv[:, :, :]),
                                             start=True, stop=True))

            def outer_products(g):
                pe.wait_ge(rotated, g + 1)
                turn(lambda c: rot[:, GT * g + c, 0:D])
                for u in range(2):
                    def fill(bank):
                        for c in range(GT):
                            rows, n = slice(64 * u, 64 * u + 64), GT * g + c
                            last = pe.matmul(bank[:, c * D:(c + 1) * D], rot[rows, n, D:2 * D], qkv[rows, n, 2 * D:3 * D],
                                             start=True, stop=True)
                        return last
                    v(fill)
                products_ready[g] = s.t.value() + sl.banks, v.t.value() + vl.banks

            def output(g):
                for lane, value in zip((sl, vl), products_ready[g]):
                    pe.wait_ge(lane.free, value)

                def fill(bank):
                    for c in range(GT):
                        for u in range(2):
                            t0 = c * P + 64 * u
                            last = pe.matmul(bank[:, t0:t0 + 64], kv[:, u, GT * g + c, :], qT[:, GC * g + t0:GC * g + t0 + 64],
                                             start=True, stop=True)
                    return last
                s(fill)
                s.wait_emptied()
                if g == 0:
                    pe.wait_ge(xb_ready, 1)

                def fill(bank):
                    pe.matmul(bank, ident[:, :], flat(xb[:, tiles(g), :]), start=True, stop=False, skip_group_check=True)
                    for c in range(GT):
                        n = GT * g + c
                        last = pe.matmul(bank[:, c * D:(c + 1) * D], ctxT[:, n * P:(n + 1) * P], wo[:, :],
                                         start=False, stop=(c == GT - 1), skip_group_check=True)
                    return last
                s(fill)

            skewed(project, outer_products, output)

        @block.scalar
        def _(act):
            take = Take(act, sl)
            act.wait_ge(consts, 16 * N_CONSTS)
            for _ in range(sl.banks):
                act.activation(scratch[:, 0:1], ident[:, 0:1], ACT.Copy).then_inc(sl.free, 1)
                act.wait_ge(sl.free, _ + 1)
            nm.scalar(act)

            def output(g):
                take(lambda bank: act.activation(ctxT[:, tokens(g)], bank, ACT.Copy))
                if g == 0:
                    act.wait_ge(xb_ready, 1)
                take(lambda bank: act.activation(x_tok[:, tiles(g), :], bank.rearrange("p (c d) -> p c d", c=GT), ACT.Copy))

            skewed(lambda g: take(lambda bank: act.activation(xnT[:, tokens(g)], bank, ACT.Copy)),
                   lambda g: take(lambda bank: act.activation(qT[:, tokens(g)], bank, ACT.Copy)), output)

        @block.vector
        def _(dve):
            take, step = Take(dve, vl), Chain(dve, chain)
            for _ in range(vl.banks):
                dve.memset(scratch[:, 1:2], 0.0).then_inc(vl.free, 1)
                dve.wait_ge(vl.free, _ + 1)
            dve.wait_ge(consts, 16 * N_CONSTS)
            nm.vector(dve, x_tok, step)
            sin = rope[:, 1, :].rearrange("p (i two) -> p i two", two=2)
            dims = [P, GT, 2 * H, HD // 2]

            def project(g):
                for n in range(GT * g, GT * (g + 1)):
                    take(lambda bank: dve.tensor_tensor(qkv[:, n, :], bank[:, 0:3 * D], flat(bqkv[:, :, :]), ALU.add))
                take.wait_taken()
                qk = qkv[:, tiles(g), 0:2 * D].rearrange("p c (m i two) -> p c m i two", i=HD // 2, two=2)
                cr = cross[:, tiles(g), :].rearrange("p c (m i two) -> p c m i two", i=HD // 2, two=2)
                for part in range(2):
                    last = dve.tensor_tensor(cr[:, :, :, :, part], qk[:, :, :, :, 1 - part],
                                             sin[:, :, part].unsqueeze(1).unsqueeze(1).broadcast_to(dims), ALU.mult)
                    if part == 0:
                        last.then_inc(chain, 1)
                        step.t.next()
                    else:
                        step(last)
                step(dve.tensor_tensor(rot[:, tiles(g), :].rearrange("p c (m e) -> p c m e", e=HD),
                                       qkv[:, tiles(g), 0:2 * D].rearrange("p c (m e) -> p c m e", e=HD),
                                       rope[:, 0, :].unsqueeze(1).unsqueeze(1).broadcast_to([P, GT, 2 * H, HD]), ALU.mult))
                dve.tensor_tensor(rot[:, tiles(g), :], rot[:, tiles(g), :], cross[:, tiles(g), :], ALU.add).then_inc(rotated, 1)

            def outer_products(g):
                for u in range(2):
                    take(lambda bank: dve.tensor_tensor(kv[:, u, tiles(g), :], bank.rearrange("p (c d) -> p c d", c=GT),
                                                        under(own[:, :], GT), ALU.mult))

            skewed(project, outer_products, lambda g: None)


def linear_attention_1(nc, io, x_tok, ident, experts):
    with ExitStack() as stack:
        m = Memory(nc, stack, "la1")
        wqkv = m.sb("wqkv", [P, 3 * D])
        wo = m.sb("wo", [P, D])
        bo = m.sb("bo", [P, D])
        gain = m.sb("gain", [P, H])
        offset = m.sb("offset", [P, H])
        own = m.sb("own", [P, D])
        ones = m.sb("ones", [P, 64])
        nm = Norm(m)
        xb = m.sb("xb", [P, NT, D])
        xnT = m.sb("xnT", [P, NT * P])
        qkv = m.sb("qkv", [P, NT, 3 * D])
        qT = m.sb("qT", [P, 2, GC])
        gram = m.sb("gram", [P, 2, 2, GT, 2 * D])
        y = m.sb("y", [P, GT, 3 * D])
        prod = m.sb("prod", [P, GT, D])
        square, length, ratio = (m.sb(n, [P, GT * H]) for n in ("square", "length", "ratio"))
        att = m.sb("att", [P, NT, D])
        attT = m.sb("attT", [P, GC])
        scratch = m.sb("scratch", [P, 2])
        vl = Lane(m, "vector_lane")
        sl = Lane(m, "scalar_lane")
        consts = m.sem("consts")
        chain = m.sem("vector_chain")
        xb_ready = m.sem("xb_ready")
        square_ready = m.sem("square_ready")
        length_ready = m.sem("length_ready")
        att_ready = m.sem("att_ready")
        block = stack.enter_context(nc.Block())
        N_CONSTS = 6

        def tiles(g):
            return slice(GT * g, GT * (g + 1))

        def tokens(g):
            return slice(GC * g, GC * (g + 1))

        def skewed(project, grams, products, output):
            for g in range(NG + 3):
                for step, work in enumerate((project, grams, products, output)):
                    if 0 <= g - step < NG:
                        work(g - step)

        @block.sync
        def _(sp):
            sp.dma_start(wqkv[:, :], io["L1_attn_w_qkvT"]).then_inc(consts, 16)
            sp.dma_start(wo[:, :], io["L1_attn_w_outT"]).then_inc(consts, 16)
            load_row(sp, bo[:, :], io["L1_attn_b_out"], consts)
            load_row(sp, gain[:, :], io["L1_attn_norm_g"].rearrange("a h b c -> (a h b c)"), consts)
            load_row(sp, offset[:, :], io["L1_attn_norm_b"].rearrange("a h b c -> (a h b c)"), consts)
            sp.dma_start(own[:, :], io["own_head"]).then_inc(consts, 16)
            experts.load(sp, io)

        @block.gpsimd
        def _(pool):
            pool.wait_ge(consts, 16 * N_CONSTS)
            pool.tensor_tensor(xb[:, :, :], x_tok[:, :, :], under(bo[:, :], NT), ALU.add).then_inc(xb_ready, 1)

        @block.tensor
        def _(pe):
            v, s = Fill(pe, vl), Fill(pe, sl)
            pe.wait_ge(consts, 16 * N_CONSTS)
            grams_ready = {}

            def turn(src):
                def fill(bank):
                    for c in range(GT):
                        last = pe.transpose(bank[:, c * P:(c + 1) * P], src(c), ident[:, :])
                    return last
                s(fill)

            def project(g):
                pe.wait_ge(nm.ready, GT * (g + 1))
                turn(lambda c: nm.xn[:, GT * g + c, :])
                s.wait_emptied()
                for n in range(GT * g, GT * (g + 1)):
                    v(lambda bank: pe.matmul(bank[:, 0:3 * D], xnT[:, n * P:(n + 1) * P], wqkv[:, :], start=True, stop=True))
                grams_ready[g] = None, v.t.value() + vl.banks

            def grams(g):
                pe.wait_ge(vl.free, grams_ready[g][1])
                turn(lambda c: qkv[:, GT * g + c, 0:D])
                for u in range(2):
                    for half in range(2):
                        def fill(bank):
                            rows = slice(64 * u, 64 * u + 64)
                            for i in range(GT // 2):
                                n = GT * g + half * (GT // 2) + i
                                last = pe.matmul(bank[:, i * 2 * D:(i + 1) * 2 * D], qkv[rows, n, D:2 * D],
                                                 qkv[rows, n, D:3 * D], start=True, stop=True)
                            return last
                        v(fill)
                grams_ready[g] = s.t.value() + sl.banks, v.t.value() + vl.banks

            def products(g):
                for lane, value in zip((sl, vl), grams_ready[g]):
                    pe.wait_ge(lane.free, value)
                for c in range(GT):
                    def fill(bank):
                        for u in range(2):
                            rows = slice(64 * u, 64 * u + 64)
                            pe.matmul(bank[rows, 0:2 * D], qT[:, g % 2, c * P + 64 * u:c * P + 64 * u + 64],
                                      gram[:, g % 2, u, c, :], start=True, stop=True)
                        for u in range(2):
                            rows = slice(64 * u, 64 * u + 64)
                            last = pe.matmul(bank[rows, 2 * D:3 * D], ones[rows, :], qkv[rows, GT * g + c, 2 * D:3 * D],
                                             start=True, stop=True)
                        return last
                    v(fill)

            def output(g):
                pe.wait_ge(att_ready, g + 1)
                turn(lambda c: att[:, GT * g + c, :])
                s.wait_emptied()
                if g == 0:
                    pe.wait_ge(xb_ready, 1)

                def fill(bank):
                    pe.matmul(bank, ident[:, :], flat(xb[:, tiles(g), :]), start=True, stop=False, skip_group_check=True)
                    for c in range(GT):
                        last = pe.matmul(bank[:, c * D:(c + 1) * D], attT[:, c * P:(c + 1) * P], wo[:, :],
                                         start=False, stop=(c == GT - 1), skip_group_check=True)
                    return last
                s(fill)

            skewed(project, grams, products, output)

        @block.scalar
        def _(act):
            take = Take(act, sl)
            for _ in range(sl.banks):
                act.activation(scratch[:, 0:1], ident[:, 0:1], ACT.Copy).then_inc(sl.free, 1)
                act.wait_ge(sl.free, _ + 1)
            nm.scalar(act)

            def products(g):
                act.wait_ge(square_ready, g + 1)
                act.activation(length[:, :], square[:, :], ACT.Sqrt).then_inc(length_ready, 1)

            def output(g):
                take(lambda bank: act.activation(attT[:, :], bank, ACT.Copy))
                if g == 0:
                    act.wait_ge(xb_ready, 1)
                take(lambda bank: act.activation(x_tok[:, tiles(g), :], bank.rearrange("p (c d) -> p c d", c=GT), ACT.Copy))

            skewed(lambda g: take(lambda bank: act.activation(xnT[:, tokens(g)], bank, ACT.Copy)),
                   lambda g: take(lambda bank: act.activation(qT[:, g % 2, :], bank, ACT.Copy)), products, output)

        @block.vector
        def _(dve):
            take, step = Take(dve, vl), Chain(dve, chain)
            for _ in range(vl.banks):
                dve.memset(ones[:, :], 1.0).then_inc(vl.free, 1)
                dve.wait_ge(vl.free, _ + 1)
            dve.wait_ge(consts, 16 * N_CONSTS)
            nm.vector(dve, x_tok, step)

            def heads(ap):
                return ap.rearrange("p c (h d) -> p c h d", d=HD)

            def project(g):
                for n in range(GT * g, GT * (g + 1)):
                    take(lambda bank: dve.tensor_copy(qkv[:, n, :], bank[:, 0:3 * D]))

            def grams(g):
                for u in range(2):
                    for half in range(2):
                        c0 = half * (GT // 2)
                        take(lambda bank: dve.tensor_tensor(
                            gram[:, g % 2, u, c0:c0 + GT // 2, :].rearrange("p c (k d) -> p (c k) d", k=2),
                            bank.rearrange("p (c d) -> p c d", c=4), under(own[:, :], 4), ALU.mult))

            def products(g):
                for c in range(GT):
                    take(lambda bank: dve.tensor_copy(y[:, c, :], bank[:, 0:3 * D]))
                take.wait_taken()
                step(dve.tensor_tensor(prod[:, :, :], qkv[:, tiles(g), 0:D], y[:, :, 0:D], ALU.mult))
                step(dve.tensor_reduce(square[:, :], heads(prod[:, :, :]), X, ALU.add))
                dve.tensor_scalar(square[:, :], square[:, :], 0.0, None, ALU.max).then_inc(square_ready, 1)
                dve.wait_ge(length_ready, g + 1)
                step(dve.tensor_scalar(length[:, :], length[:, :], 1e-12, None, ALU.max))
                step(dve.reciprocal(ratio[:, :], length[:, :]))
                step(dve.tensor_tensor(ratio[:, :].rearrange("p (c h) -> p c h", h=H),
                                       ratio[:, :].rearrange("p (c h) -> p c h", h=H), under(gain[:, :], GT), ALU.mult))
                step(dve.tensor_tensor(heads(prod[:, :, :]), heads(y[:, :, D:2 * D]),
                                       ratio[:, :].rearrange("p (c h) -> p c h", h=H).unsqueeze(3)
                                       .broadcast_to([P, GT, H, HD]), ALU.mult))
                out = att[:, tiles(g), :]
                step(dve.tensor_tensor(heads(out), heads(y[:, :, 2 * D:3 * D]),
                                       offset[:, :].unsqueeze(1).unsqueeze(3).broadcast_to([P, GT, H, HD]), ALU.mult))
                dve.tensor_tensor(out, out, prod[:, :, :], ALU.add).then_inc(att_ready, 1)
                dve.wait_ge(att_ready, g + 1)

            skewed(project, grams, products, lambda g: None)


E = 8
FF = 512


def first_of_largest(dve, step, score, rank, top, hit, order):
    sh = score.shape
    step(dve.tensor_reduce(top[:, :], score, X, ALU.max))
    step(dve.tensor_tensor(hit, score, top[:, :].unsqueeze(2).broadcast_to(sh), ALU.is_equal))
    step(dve.tensor_tensor(hit, hit, under(rank[:, :], sh[1]), ALU.mult))
    step(dve.tensor_reduce(order[:, :], hit, X, ALU.max))
    step(dve.tensor_tensor(hit, hit, order[:, :].unsqueeze(2).broadcast_to(sh), ALU.is_equal))


class Experts1:

    def __init__(self, m):
        self.w1 = m.sb("w1", [P, E, FF])
        self.b1 = m.sb("b1", [P, E * (FF // P)])
        self.w2 = m.sb("w2", [P, E * (FF // P), D])
        self.loaded = m.sem("loaded")

    def load(self, sp, io):
        sp.dma_start(self.b1[:, :], io["L1_ffn_b1T"]).then_inc(self.loaded, 16)
        sp.dma_start(self.w1[:, :, :], io["L1_ffn_w1"].rearrange("e c f -> c e f")).then_inc(self.loaded, 16)
        sp.dma_start(self.w2[:, :, :], io["L1_ffn_w2"].rearrange("e (f p) d -> p (e f) d", p=P)).then_inc(self.loaded, 16)


def layer_1_end(nc, io, x_tok, ident):
    with ExitStack() as stack:
        experts = Experts1(Memory(nc, stack, "experts1"))
        linear_attention_1(nc, io, x_tok, ident, experts)
        moe_top1(nc, io, x_tok, ident, experts)


def moe_top1(nc, io, x_tok, ident, experts):
    NF = FF // P
    with ExitStack() as stack:
        m = Memory(nc, stack, "moe1")
        gate = m.sb("gate", [P, E])
        b2 = m.sb("b2", [E, D])
        rank = m.sb("rank", [P, E])
        nm = Norm(m)
        xnT = m.sb("xnT", [P, NT * P])
        logits, probs, hit = (m.sb(n, [P, NT, E]) for n in ("logits", "probs", "hit"))
        top, total, order = (m.sb(n, [P, NT]) for n in ("top", "total", "order"))
        chosen = m.sb("chosen", [P, NT, E])
        share = m.sb("share", [P, GT, E])
        chosenT = m.sb("chosenT", [E, NT * P])
        base = m.sb("base", [P, NT, D])
        hidden = m.sb("hidden", [P, 2, NF, GC])
        acc = m.sb("acc", [P, 2, GT, D])
        scratch = m.sb("scratch", [P, 2])
        vl, sl = Lane(m, "vector_lane"), Lane(m, "scalar_lane")
        ps_l = m.psum("ps_l", [P, NT, E])
        consts = m.sem("consts")
        chain = m.sem("vector_chain")
        logits_full, logits_ready, probs_ready, chosen_ready = (
            m.sem(n) for n in ("logits_full", "logits_ready", "probs_ready", "chosen_ready"))
        block = stack.enter_context(nc.Block())
        N_CONSTS = 3
        PRE_S = 3 * NG
        VT, ST = E, E * NF

        def tiles(g):
            return slice(GT * g, GT * (g + 1))

        def tokens(g):
            return slice(GC * g, GC * (g + 1))

        @block.sync
        def _(sp):
            sp.dma_start(gate[:, :], io["L1_ffn_gate_wT"]).then_inc(consts, 16)
            sp.dma_start(rank[:, :], io["rank"]).then_inc(consts, 16)
            sp.dma_start(b2[:, :], io["L1_ffn_b2"]).then_inc(consts, 16)

        @block.tensor
        def _(pe):
            v, s = Fill(pe, vl), Fill(pe, sl)

            def turn(src, rows=P):
                def fill(bank):
                    for c in range(GT):
                        last = pe.transpose(bank[0:rows, c * P:(c + 1) * P], src(c), ident[:, :])
                    return last
                s(fill)

            for g in range(NG):
                pe.wait_ge(nm.ready, GT * (g + 1))
                turn(lambda c: nm.xn[:, GT * g + c, :])
            s.wait_emptied()
            pe.wait_ge(consts, 16 * N_CONSTS)
            for n in range(NT):
                last = pe.matmul(ps_l[:, n, :], xnT[:, n * P:(n + 1) * P], gate[:, :], start=True, stop=True)
            last.then_inc(logits_full, 1)
            pe.wait_ge(chosen_ready, 1)
            for g in range(NG):
                turn(lambda c: chosen[:, GT * g + c, :], E)
            s.wait_emptied()
            for g in range(NG):
                def fill(bank):
                    pe.matmul(bank, ident[:, :], flat(x_tok[:, tiles(g), :]), start=True, stop=False, skip_group_check=True)
                    for c in range(GT):
                        n = GT * g + c
                        last = pe.matmul(bank[:, c * D:(c + 1) * D], chosenT[:, n * P:(n + 1) * P], b2[:, :],
                                         start=False, stop=(c == GT - 1), skip_group_check=True)
                    return last
                s(fill)
            pe.wait_ge(experts.loaded, 48)
            with pe.Fori(0, NG) as it:
                v.enter(it, VT)
                s.enter(it, ST)

                def up(e):
                    for f in range(NF):
                        s(lambda bank: pe.matmul(bank, experts.w1[:, e, f * P:(f + 1) * P], xnT[:, bass.ds(it * GC, GC)],
                                                 start=True, stop=True))
                    return s.t.value() + sl.banks

                def down(e, hidden_ready):
                    pe.wait_ge(sl.free, hidden_ready)

                    def fill(bank):
                        for c in range(GT):
                            for f in range(NF):
                                last = pe.matmul(bank[:, c * D:(c + 1) * D], hidden[:, e % 2, f, c * P:(c + 1) * P],
                                                 experts.w2[:, e * NF + f, :], start=(f == 0), stop=(f == NF - 1))
                        return last
                    v(fill)

                ready = up(0)
                for e in range(E):
                    next_ready = up(e + 1) if e + 1 < E else None
                    down(e, ready)
                    ready = next_ready
                v.leave(NG)
                s.leave(NG)

        @block.scalar
        def _(act):
            take = Take(act, sl)
            prime(act, sl, lambda: act.activation(scratch[:, 0:1], ident[:, 0:1], ACT.Copy))
            nm.scalar(act)
            for g in range(NG):
                take(lambda bank: act.activation(xnT[:, tokens(g)], bank, ACT.Copy))
            act.wait_ge(logits_ready, 1)
            act.activation(probs[:, :, :], logits[:, :, :], ACT.Exp).then_inc(probs_ready, 1)
            for g in range(NG):
                take(lambda bank: act.activation(chosenT[:, tokens(g)], bank[0:E, :], ACT.Copy))
            for g in range(NG):
                take(lambda bank: act.activation(base[:, tiles(g), :], bank.rearrange("p (c d) -> p c d", c=GT), ACT.Copy))
            act.wait_ge(experts.loaded, 48)
            with act.Fori(0, NG) as it:
                take.enter(it, ST)
                for e in range(E):
                    for f in range(NF):
                        if f == 0 and e >= 2:
                            act.wait_ge(vl.full, it * VT + (e - 1))
                        take(lambda bank: act.activation(hidden[:, e % 2, f, :], bank, ACT.Relu,
                                                         bias=experts.b1[:, e * NF + f:e * NF + f + 1]))
                take.leave(NG)

        @block.vector
        def _(dve):
            take, step = Take(dve, vl), Chain(dve, chain)
            prime(dve, vl, lambda: dve.memset(scratch[:, 1:2], 0.0))
            nm.vector(dve, x_tok, step)
            dve.wait_ge(logits_full, 1)
            step(dve.tensor_reduce(top[:, :], ps_l[:, :, :], X, ALU.max))
            dve.tensor_tensor(logits[:, :, :], ps_l[:, :, :], over(top[:, :], E), ALU.subtract).then_inc(logits_ready, 1)
            dve.wait_ge(probs_ready, 1)
            dve.wait_ge(consts, 16 * N_CONSTS)
            step(dve.tensor_reduce(total[:, :], probs[:, :, :], X, ALU.add))
            step(dve.reciprocal(total[:, :], total[:, :]))
            step(dve.tensor_tensor(probs[:, :, :], probs[:, :, :], over(total[:, :], E), ALU.mult))
            first_of_largest(dve, step, probs[:, :, :], rank, top, hit[:, :, :], order)
            dve.tensor_tensor(chosen[:, :, :], hit[:, :, :], probs[:, :, :], ALU.mult).then_inc(chosen_ready, 1)
            dve.wait_ge(chosen_ready, 1)
            dve.wait_ge(sl.free, PRE_S + sl.banks)
            with dve.Fori(0, NG) as it:
                take.enter(it, VT)
                step.enter(it, 1)
                group = bass.ds(it * GT, GT)
                step(dve.tensor_copy(share[:, :, :], chosen[:, group, :]))
                for e in range(E):
                    if e > 0:
                        take.wait_taken()

                    def out_of(bank):
                        src = acc[:, (e + 1) % 2, :, :] if e > 0 else base[:, group, :]
                        dst = acc[:, e % 2, :, :] if e < E - 1 else x_tok[:, group, :]
                        for c in range(GT):
                            last = dve.scalar_tensor_tensor(out=dst[:, c, :], in0=bank[:, c * D:(c + 1) * D],
                                                            scalar=share[:, c, e:e + 1], in1=src[:, c, :],
                                                            op0=ALU.mult, op1=ALU.add)
                        return last
                    take(out_of)
                take.wait_taken()
                take.leave(NG)
                step.leave(NG)


class Rms:

    def __init__(self, m, name):
        self.sq = m.sb(name + "_sq", [P, NT, D])
        self.var, self.std, self.rstd = (m.sb(name + "_" + s, [P, NT]) for s in ("var", "std", "rstd"))
        self.sq_ready, self.var_ready, self.std_ready, self.ready = (
            m.sem(name + "_" + s) for s in ("sq_ready", "var_ready", "std_ready", "ready"))

    def vector(self, dve, src, gain, step, after=lambda g: None):
        for g in range(NG + 1):
            if g < NG:
                part = slice(GT * g, GT * (g + 1))
                dve.wait_ge(self.sq_ready, GT * (g + 1))
                dve.tensor_scalar(self.var[:, part], self.var[:, part], 1.0 / D, RMS_EPS, ALU.mult, ALU.add).then_inc(self.var_ready, 1)
            if g > 0:
                part = slice(GT * (g - 1), GT * g)
                dve.wait_ge(self.std_ready, g)
                step(dve.reciprocal(self.rstd[:, part], self.std[:, part]))
                for c in range(part.start, part.stop):
                    dve.scalar_tensor_tensor(out=src[:, c, :], in0=src[:, c, :], scalar=self.rstd[:, c:c + 1], in1=gain,
                                             op0=ALU.mult, op1=ALU.mult).then_inc(self.ready, 1)
                after(g - 1)

    def squares(self, act, src, g):
        for c in range(GT * g, GT * (g + 1)):
            act.activation(self.sq[:, c, :], src[:, c, :], ACT.Square, accum_out=self.var[:, c:c + 1]).then_inc(self.sq_ready, 1)

    def roots(self, act, g):
        part = slice(GT * g, GT * (g + 1))
        act.wait_ge(self.var_ready, g + 1)
        act.activation(self.std[:, part], self.var[:, part], ACT.Sqrt).then_inc(self.std_ready, 1)

    def scalar(self, act, src):
        for g in range(NG + 1):
            if g < NG:
                self.squares(act, src, g)
            if g > 0:
                self.roots(act, g - 1)


def ffn_0(nc, io, x_tok, ident):
    with ExitStack() as stack:
        m = Memory(nc, stack, "ffn0")
        t = Ffn0(m)
        route(nc, io, x_tok, ident, t)
        experts(nc, ident, t)
        causal_attention(nc, ident, t)
        feed_forward(nc, x_tok, ident, t)


class Ffn0:

    def __init__(self, m):
        self.nm = Norm(m)
        self.xn = self.nm.xn
        self.xnT = m.sb("xnT", [P, NT * P])
        self.share = m.sb("share", [P, NT, E])
        self.sparse = m.sb("sparse", [P, NT, D])
        self.rms_sparse = Rms(m, "rms_sparse")
        self.proj = m.sb("proj", [P, NT, D])
        self.ew1, self.ew3, self.ew2 = (m.sb(n, [P, E, P]) for n in ("ew1", "ew3", "ew2"))
        self.wq, self.wk, self.wv, self.wo = (m.sb(n, [P, D]) for n in ("wq", "wk", "wv", "wo"))
        self.own = m.sb("own", [P, D])
        self.parity = m.sb("parity", [P, H])
        self.causal = m.sb("causal", [P, S])
        self.w1, self.w3 = m.sb("w1", [P, FF]), m.sb("w3", [P, FF])
        self.w2 = m.sb("w2", [P, FF // P, D])
        self.attn_gain, self.ff_gain, self.moe_gain = (m.sb(n, [P, D]) for n in ("attn_gain", "ff_gain", "moe_gain"))
        self.experts_loaded, self.attention_loaded, self.ffn_loaded = (
            m.sem(n) for n in ("experts_loaded", "attention_loaded", "ffn_loaded"))

    EXPERTS, ATTENTION, FFN = 16 * 3, 16 * 7, 16 * 6


def route(nc, io, x_tok, ident, t):
    with ExitStack() as stack:
        m = Memory(nc, stack, "route")
        router = m.sb("router", [P, E])
        rank = m.sb("rank", [P, E])
        logits, probs, hit, hit2, rest = (m.sb(n, [P, NT, E]) for n in ("logits", "probs", "hit", "hit2", "rest"))
        top, total, order = (m.sb(n, [P, NT]) for n in ("top", "total", "order"))
        scratch = m.sb("scratch", [P, 1])
        sl = Lane(m, "scalar_lane")
        ps_l = m.psum("ps_l", [P, NT, E])
        consts, chain = m.sem("consts"), m.sem("vector_chain")
        logits_full, logits_ready, probs_ready = (m.sem(n) for n in ("logits_full", "logits_ready", "probs_ready"))
        block = stack.enter_context(nc.Block())

        @block.sync
        def _(sp):
            sp.dma_start(router[:, :], io["L0_ffn_router_w"]).then_inc(consts, 16)
            sp.dma_start(rank[:, :], io["rank"]).then_inc(consts, 16)
            for dst, src in ((t.ew1, "L0_ffn_ew1"), (t.ew3, "L0_ffn_ew3"), (t.ew2, "L0_ffn_ew2")):
                sp.dma_start(dst[:, :, :], io[src].rearrange("e c f -> c e f")).then_inc(t.experts_loaded, 16)
            for dst, src in ((t.wq, "L0_ffn_wq"), (t.wk, "L0_ffn_wk"), (t.wv, "L0_ffn_wv"), (t.wo, "L0_ffn_wo"),
                             (t.own, "own_head"), (t.parity, "head_parity"), (t.causal, "causal")):
                sp.dma_start(dst[:, :], io[src]).then_inc(t.attention_loaded, 16)
            for dst, src in ((t.attn_gain, "L0_ffn_attn_norm_w"), (t.ff_gain, "L0_ffn_ff_norm_w"), (t.moe_gain, "L0_ffn_moe_norm_w")):
                load_row(sp, dst[:, :], io[src], t.ffn_loaded)
            sp.dma_start(t.w1[:, :], io["L0_ffn_w1"]).then_inc(t.ffn_loaded, 16)
            sp.dma_start(t.w3[:, :], io["L0_ffn_w3"]).then_inc(t.ffn_loaded, 16)
            sp.dma_start(t.w2[:, :, :], io["L0_ffn_w2"].rearrange("(f p) d -> p f d", p=P)).then_inc(t.ffn_loaded, 16)

        @block.tensor
        def _(pe):
            s = Fill(pe, sl)
            for g in range(NG):
                pe.wait_ge(t.nm.ready, GT * (g + 1))

                def fill(bank):
                    for c in range(GT):
                        last = pe.transpose(bank[:, c * P:(c + 1) * P], t.xn[:, GT * g + c, :], ident[:, :])
                    return last
                s(fill)
            s.wait_emptied()
            pe.wait_ge(consts, 32)
            for n in range(NT):
                last = pe.matmul(ps_l[:, n, :], t.xnT[:, n * P:(n + 1) * P], router[:, :], start=True, stop=True)
            last.then_inc(logits_full, 1)

        @block.scalar
        def _(act):
            take = Take(act, sl)
            prime(act, sl, lambda: act.activation(scratch[:, 0:1], ident[:, 0:1], ACT.Copy))
            t.nm.scalar(act)
            for g in range(NG):
                take(lambda bank: act.activation(t.xnT[:, g * GC:(g + 1) * GC], bank, ACT.Copy))
            act.wait_ge(logits_ready, 1)
            act.activation(probs[:, :, :], logits[:, :, :], ACT.Exp).then_inc(probs_ready, 1)

        @block.vector
        def _(dve):
            step = Chain(dve, chain)
            t.nm.vector(dve, x_tok, step)
            dve.wait_ge(logits_full, 1)
            step(dve.tensor_reduce(top[:, :], ps_l[:, :, :], X, ALU.max))
            dve.tensor_tensor(logits[:, :, :], ps_l[:, :, :], over(top[:, :], E), ALU.subtract).then_inc(logits_ready, 1)
            dve.wait_ge(probs_ready, 1)
            dve.wait_ge(consts, 32)
            step(dve.tensor_reduce(total[:, :], probs[:, :, :], X, ALU.add))
            step(dve.reciprocal(total[:, :], total[:, :]))
            step(dve.tensor_tensor(probs[:, :, :], probs[:, :, :], over(total[:, :], E), ALU.mult))
            first_of_largest(dve, step, probs[:, :, :], rank, top, hit[:, :, :], order)
            step(dve.scalar_tensor_tensor(out=rest[:, :, :], in0=hit[:, :, :], scalar=-2.0, in1=probs[:, :, :],
                                          op0=ALU.mult, op1=ALU.add))
            first_of_largest(dve, step, rest[:, :, :], rank, top, hit2[:, :, :], order)
            step(dve.tensor_tensor(hit[:, :, :], hit[:, :, :], hit2[:, :, :], ALU.add))
            step(dve.tensor_tensor(t.share[:, :, :], hit[:, :, :], probs[:, :, :], ALU.mult))


def experts(nc, ident, t):
    with ExitStack() as stack:
        m = Memory(nc, stack, "experts")
        gate = m.sb("gate", [P, 2, GC])
        hidden = m.sb("hidden", [P, 2, GC])
        share = m.sb("share", [P, GT, E])
        acc = m.sb("acc", [P, 2, GT, D])
        zeros = m.sb("zeros", [P, D])
        scratch = m.sb("scratch", [P, 1])
        vl, sl = Lane(m, "vector_lane"), Lane(m, "scalar_lane")
        chain = m.sem("vector_chain")
        block = stack.enter_context(nc.Block())
        V_ORDER = [("up", 0)] + [x for e in range(1, E) for x in (("up", e), ("down", e - 1))] + [("down", E - 1)]
        VT, ST = len(V_ORDER), E

        def v_at(what):
            return V_ORDER.index(what) + 1

        @block.tensor
        def _(pe):
            v, s = Fill(pe, vl), Fill(pe, sl)
            pe.wait_ge(t.experts_loaded, t.EXPERTS)
            with pe.Fori(0, NG) as it:
                v.enter(it, VT)
                s.enter(it, ST)
                xnT = t.xnT[:, bass.ds(it * GC, GC)]

                def up(e):
                    s(lambda bank: pe.matmul(bank, t.ew1[:, e, :], xnT, start=True, stop=True))
                    v(lambda bank: pe.matmul(bank, t.ew3[:, e, :], xnT, start=True, stop=True))
                    return v.t.value() + vl.banks

                def down(e, hidden_ready):
                    pe.wait_ge(vl.free, hidden_ready)

                    def fill(bank):
                        for c in range(GT):
                            last = pe.matmul(bank[:, c * D:(c + 1) * D], hidden[:, e % 2, c * P:(c + 1) * P],
                                             t.ew2[:, e, :], start=True, stop=True)
                        return last
                    v(fill)

                ready = up(0)
                for e in range(1, E):
                    next_ready = up(e)
                    down(e - 1, ready)
                    ready = next_ready
                down(E - 1, ready)
                v.leave(NG)
                s.leave(NG)

        @block.scalar
        def _(act):
            take = Take(act, sl)
            prime(act, sl, lambda: act.activation(scratch[:, 0:1], ident[:, 0:1], ACT.Copy))
            with act.Fori(0, NG) as it:
                take.enter(it, ST)
                for e in range(E):
                    if e >= 2:
                        act.wait_ge(vl.free, it * VT + (v_at(("up", e - 2)) + vl.banks))
                    take(lambda bank: act.activation(gate[:, e % 2, :], bank, ACT.Silu))
                take.leave(NG)

        @block.vector
        def _(dve):
            take, step = Take(dve, vl), Chain(dve, chain)
            prime(dve, vl, lambda: dve.memset(zeros[:, :], 0.0))
            with dve.Fori(0, NG) as it:
                take.enter(it, VT)
                step.enter(it, 1)
                step(dve.tensor_copy(share[:, :, :], t.share[:, bass.ds(it * GT, GT), :]))
                for what, e in V_ORDER:
                    if what == "up":
                        dve.wait_ge(sl.free, it * ST + (e + 1 + sl.banks))
                        take(lambda bank: dve.tensor_tensor(hidden[:, e % 2, :], gate[:, e % 2, :], bank, ALU.mult))
                        continue
                    if e > 0:
                        take.wait_taken()

                    def out_of(bank):
                        dst = acc[:, e % 2, :, :] if e < E - 1 else t.sparse[:, bass.ds(it * GT, GT), :]
                        for c in range(GT):
                            last = dve.scalar_tensor_tensor(out=dst[:, c, :], in0=bank[:, c * D:(c + 1) * D],
                                                            scalar=share[:, c, e:e + 1],
                                                            in1=acc[:, (e + 1) % 2, c, :] if e else zeros[:, :],
                                                            op0=ALU.mult, op1=ALU.add)
                        return last
                    take(out_of)
                take.wait_taken()
                take.leave(NG)
                step.leave(NG)


def causal_attention(nc, ident, t):
    HV = HD + 1
    with ExitStack() as stack:
        m = Memory(nc, stack, "attn0")
        xnT = m.sb("xnT", [P, GC])
        qT = m.sb("qT", [P, GC])
        kT = m.sb("kT", [P, GC])
        keys = m.sb("keys", [P, 2 * GT, H, S])
        vals = m.sb("vals", [P, 2 * GT, H, HV])
        sc = m.sb("scores", [P, GT, H, S])
        mx = m.sb("max", [P, GT, H])
        ex = m.sb("exps", [P, GT, H, S])
        exT = m.sb("expsT", [P, 2, H // 2, P])
        denom = m.sb("denom", [P, GT, H])
        o = m.sb("o", [P, GT, D])
        oT = m.sb("oT", [P, GC])
        scratch = m.sb("scratch", [P, 2])
        vl, sl = Lane(m, "vector_lane", 4), Lane(m, "scalar_lane")
        chain = m.sem("vector_chain")
        xnT_ready = m.sem("xnT_ready")
        vals_preset = m.sem("vals_preset")
        keys_vector = m.sem("keys_vector")
        keys_pool = m.sem("keys_pool")
        scores_ready = m.sem("scores_ready")
        shifted = m.sem("shifted")
        exps_ready = m.sem("exps_ready")
        block = stack.enter_context(nc.Block())
        V_ORDER = ["s0", "s0", "s1", "s1", "s2", "s2", "s3", "s3", "k", "o0", "o1", "o2", "o3", "v", "v", "wo"]
        S_ORDER = ["q", "e0", "e0", "e1", "e1", "e2", "e2", "e3", "e3", "o"]
        VT, ST = len(V_ORDER), len(S_ORDER)
        PRE_V = 3

        def v_at(what):
            return PRE_V + V_ORDER.index(what) + V_ORDER.count(what)

        def write_keys(eng, c):
            src = kT[:, c * P:(c + 1) * P].rearrange("p (b k) -> p b k", b=2).unsqueeze(2).broadcast_to([P, 2, H, S])
            of_head = t.own[:, :].rearrange("p (h d) -> p h d", d=HD)[:, :, 0].unsqueeze(1).unsqueeze(3)
            return eng.tensor_tensor(keys[:, 2 * c:2 * c + 2, :, :], src, of_head.broadcast_to([P, 2, H, S]), ALU.mult)

        @block.gpsimd
        def _(pool):
            def group_steps(it, is_last):
                for c in range(GT):
                    pool.wait_ge(scores_ready, it * GT + (c + 1))
                    pool.tensor_tensor(sc[:, c, :, :], sc[:, c, :, :], over(mx[:, c, :], S),
                                       ALU.subtract).then_inc(shifted, 1)
                if not is_last:
                    pool.wait_ge(vl.free, it * VT + (v_at("k") + vl.banks))
                    write_keys(pool, 3).then_inc(keys_pool, 1)

            pool.wait_ge(vl.free, 1 + vl.banks)
            write_keys(pool, 3).then_inc(keys_pool, 1)
            groups(pool, lambda it: None, group_steps, lambda n: None)

        @block.tensor
        def _(pe):
            v, s = Fill(pe, vl), Fill(pe, sl)

            def queries_and_keys(g):
                pe.wait_ge(xnT_ready, g + 1)
                v(lambda bank: pe.matmul(bank, t.wk[:, :], xnT[:, :], start=True, stop=True))
                s(lambda bank: pe.matmul(bank, t.wq[:, :], xnT[:, :], start=True, stop=True))

            def values():
                for i in range(2):
                    def fill(bank):
                        for j in range(4):
                            b = 4 * i + j
                            for half in range(2):
                                last = pe.matmul(bank[64 * half:64 * half + 64, j * D:(j + 1) * D],
                                                 xnT[:, b * S:(b + 1) * S], t.wv[:, :], start=True, stop=True)
                        return last
                    v(fill)

            def scores(it, c):
                if c < GT - 1:
                    pe.wait_ge(keys_vector, it * (GT - 1) + (c + 1))
                else:
                    pe.wait_ge(keys_pool, it + 1)
                for half in range(2):
                    def fill(bank):
                        for u in range(2):
                            last = pe.matmul(bank[64 * u:64 * u + 64, :], qT[:, c * P + 64 * u:c * P + 64 * u + 64],
                                             flat(keys[:, 2 * c + u, half * 8:half * 8 + 8, :]), start=True, stop=True)
                        return last
                    v(fill)

            def turn_exps(it, c):
                pe.wait_ge(exps_ready, it * GT + (c + 1))
                pairs = ex[:, c, :, :].rearrange("p (j t) k -> p j (t k)", t=2)
                for half in range(2):
                    def fill(bank):
                        for i in range(4):
                            last = pe.transpose(bank[:, i * P:(i + 1) * P], pairs[:, half * 4 + i, :], ident[:, :])
                        return last
                    s(fill)
                return s.t.value() + sl.banks

            def attend(c, exT_ready):
                pe.wait_ge(sl.free, exT_ready)

                def fill(bank):
                    for j in range(H // 2):
                        for u in range(2):
                            last = pe.matmul(bank[64 * u:64 * u + 64, j * 2 * HV:(j + 1) * 2 * HV],
                                             exT[:, c % 2, j, 64 * u:64 * u + 64],
                                             flat(vals[:, 2 * c + u, 2 * j:2 * j + 2, :]), start=True, stop=True)
                    return last
                v(fill)

            def group_products(it, is_last):
                s.wait_emptied()
                for c in range(GT):
                    scores(it, c)
                if not is_last:
                    queries_and_keys(it + 1)
                ready = turn_exps(it, 0)
                for c in range(GT):
                    next_ready = turn_exps(it, c + 1) if c + 1 < GT else None
                    attend(c, ready)
                    ready = next_ready
                o_ready = v.t.value() + vl.banks
                if not is_last:
                    values()
                pe.wait_ge(vl.free, o_ready)

                def fill(bank):
                    for c in range(GT):
                        last = pe.transpose(bank[:, c * P:(c + 1) * P], o[:, c, :], ident[:, :])
                    return last
                s(fill)
                s.wait_emptied()

                def fill(bank):
                    for c in range(GT):
                        last = pe.matmul(bank[:, c * D:(c + 1) * D], oT[:, c * P:(c + 1) * P], t.wo[:, :], start=True, stop=True)
                    return last
                v(fill)

            def enter(it):
                v.enter(it, VT)
                s.enter(it, ST)

            def leave(n):
                v.leave(n)
                s.leave(n)

            pe.wait_ge(t.attention_loaded, t.ATTENTION)
            queries_and_keys(0)
            values()
            groups(pe, enter, group_products, leave)

        @block.scalar
        def _(act):
            take = Take(act, sl)

            def exps(it, c):
                act.wait_ge(shifted, it * GT + (c + 1))
                act.activation(ex[:, c, :, :], sc[:, c, :, :], ACT.Exp,
                               scale=float(1 / np.sqrt(np.float32(HD)))).then_inc(exps_ready, 1)

            def take_exps(it, c, is_last):
                if c >= 2:
                    act.wait_ge(vl.full, it * VT + v_at(f"o{c - 2}") - (1 if is_last else 0))
                for half in range(2):
                    take(lambda bank: act.activation(exT[:, c % 2, half * 4:half * 4 + 4, :],
                                                     bank.rearrange("p (j q) -> p j q", j=4), ACT.Copy))

            def take_q():
                take(lambda bank: act.activation(qT[:, :], bank, ACT.Copy))

            def group_steps(it, is_last):
                if not is_last:
                    wait_apart(act, (t.attention_loaded, t.ATTENTION), [(vl.full, it * VT + PRE_V)])
                    act.activation(xnT[:, :], t.xnT[:, bass.ds(it * GC + GC, GC)], ACT.Copy).then_inc(xnT_ready, 1)
                exps(it, 0)
                exps(it, 1)
                if not is_last:
                    take_q()
                for c in range(GT):
                    take_exps(it, c, is_last)
                    if c + 2 < GT:
                        exps(it, c + 2)
                take(lambda bank: act.activation(oT[:, :], bank, ACT.Copy))

            prime(act, sl, lambda: act.activation(scratch[:, 0:1], ident[:, 0:1], ACT.Copy))
            act.activation(xnT[:, :], t.xnT[:, 0:GC], ACT.Copy).then_inc(xnT_ready, 1)
            take_q()
            for g in range(NG):
                t.rms_sparse.squares(act, t.sparse, g)
            groups(act, lambda it: take.enter(it, ST), group_steps, take.leave)

        @block.vector
        def _(dve):
            take, step = Take(dve, vl), Chain(dve, chain)

            def take_scores(it, c):
                for half in range(2):
                    take(lambda bank: dve.tensor_tensor(sc[:, c, half * 8:half * 8 + 8, :],
                                                        bank.rearrange("p (h k) -> p h k", h=8),
                                                        under(t.causal[:, :], 8), ALU.add))
                take.wait_taken()
                dve.tensor_reduce(mx[:, c, :], sc[:, c, :, :], X, ALU.max).then_inc(scores_ready, 1)

            def take_o(c):
                def out_of(bank):
                    got = bank[:, 0:H * HV].rearrange("p (h d) -> p h d", d=HV)
                    step(dve.reciprocal(denom[:, c, :], got[:, :, HD]))
                    return dve.tensor_tensor(o[:, c, :].rearrange("p (h d) -> p h d", d=HD), got[:, :, 0:HD],
                                             over(denom[:, c, :], HD), ALU.mult)
                take(out_of)

            def take_k():
                take(lambda bank: dve.tensor_copy(kT[:, :], bank))
                take.wait_taken()

            def take_v():
                for i in range(2):
                    take(lambda bank: dve.tensor_tensor(
                        vals[:, 4 * i:4 * i + 4, :, 0:HD], bank.rearrange("p (b h d) -> p b h d", b=4, d=HD),
                        t.parity[:, :].unsqueeze(1).unsqueeze(3).broadcast_to([P, 4, H, HD]), ALU.mult))

            def keys_of(c):
                write_keys(dve, c).then_inc(keys_vector, 1)

            def group_steps(it, is_last):
                for c in range(GT):
                    take_scores(it, c)
                if not is_last:
                    take_k()
                for c in range(GT):
                    if c < GT - 1 and not is_last:
                        keys_of(c)
                    take_o(c)
                if not is_last:
                    take_v()
                proj = t.proj[:, GT * it:GT * (it + 1), :] if isinstance(it, int) else t.proj[:, bass.ds(it * GT, GT), :]
                take(lambda bank: dve.tensor_copy(proj, bank.rearrange("p (c d) -> p c d", c=GT)))

            prime(dve, vl, lambda: dve.memset(scratch[:, 1:2], 0.0))
            dve.wait_ge(t.attention_loaded, t.ATTENTION)
            dve.tensor_copy(vals[:, :, :, HD], under(t.parity[:, :], 2 * GT)).then_inc(vals_preset, 1)
            take_k()
            for c in range(GT - 1):
                keys_of(c)
            take_v()

            def enter(it):
                take.enter(it, VT)
                step.enter(it, GT)

            def leave(n):
                take.leave(n)
                step.leave(n)

            groups(dve, enter, group_steps, leave)
            dve.wait_ge(vals_preset, 1)


def feed_forward(nc, x_tok, ident, t):
    NF = FF // P
    with ExitStack() as stack:
        m = Memory(nc, stack, "ff0")
        rms_a, rms_m, rms_f = Rms(m, "rms_attn"), t.rms_sparse, Rms(m, "rms_ff")
        h = t.proj
        rest = t.sparse
        hT = m.sb("hT", [P, NT * P])
        gate = m.sb("gate", [P, NF, GC])
        hidden = m.sb("hidden", [P, NF, GC])
        ffn = m.sb("ffn", [P, NT, D])
        scratch = m.sb("scratch", [P, 2])
        vl, sl = Lane(m, "vector_lane", NF + 1), Lane(m, "scalar_lane")
        chain, pool_chain = m.sem("vector_chain"), m.sem("pool_chain")
        h_ready = m.sem("h_ready")
        rest_ready = m.sem("rest_ready")
        x_ready = m.sem("x_ready")
        block = stack.enter_context(nc.Block())
        VT, ST = NF + 1, NF

        def part(g):
            return slice(GT * g, GT * (g + 1))

        @block.gpsimd
        def _(pool):
            pool.wait_ge(rms_m.ready, NT)
            pool.tensor_tensor(rest[:, :, :], rest[:, :, :], x_tok[:, :, :], ALU.add).then_inc(pool_chain, 1)
            pool.wait_ge(pool_chain, 1)
            pool.wait_ge(h_ready, NG)
            pool.tensor_tensor(rest[:, :, :], rest[:, :, :], h[:, :, :], ALU.add).then_inc(rest_ready, 1)

        @block.tensor
        def _(pe):
            v, s = Fill(pe, vl), Fill(pe, sl)
            for g in range(NG):
                pe.wait_ge(h_ready, g + 1)

                def fill(bank):
                    for c in range(GT):
                        last = pe.transpose(bank[:, c * P:(c + 1) * P], h[:, GT * g + c, :], ident[:, :])
                    return last
                s(fill)
            s.wait_emptied()
            pe.wait_ge(t.ffn_loaded, t.FFN)
            with pe.Fori(0, NG) as it:
                v.enter(it, VT)
                s.enter(it, ST)
                for f in range(NF):
                    for lane, w in ((s, t.w1), (v, t.w3)):
                        lane(lambda bank: pe.matmul(bank, w[:, f * P:(f + 1) * P], hT[:, bass.ds(it * GC, GC)], start=True, stop=True))
                v.wait_emptied()

                def fill(bank):
                    for c in range(GT):
                        for f in range(NF):
                            last = pe.matmul(bank[:, c * D:(c + 1) * D], hidden[:, f, c * P:(c + 1) * P], t.w2[:, f, :],
                                             start=(f == 0), stop=(f == NF - 1))
                    return last
                v(fill)
                v.leave(NG)
                s.leave(NG)

        @block.scalar
        def _(act):
            take = Take(act, sl)
            prime(act, sl, lambda: act.activation(scratch[:, 0:1], ident[:, 0:1], ACT.Copy))
            rms_a.scalar(act, t.proj)
            for g in range(NG):
                take(lambda bank: act.activation(hT[:, g * GC:(g + 1) * GC], bank, ACT.Copy))
            for g in range(NG):
                rms_m.roots(act, g)
            with act.Fori(0, NG) as it:
                take.enter(it, ST)
                for f in range(NF):
                    take(lambda bank: act.activation(gate[:, f, :], bank, ACT.Silu))
                take.leave(NG)
            act.wait_ge(vl.free, NG * VT + vl.banks)
            rms_f.scalar(act, ffn)

        @block.vector
        def _(dve):
            take, step = Take(dve, vl), Chain(dve, chain)
            prime(dve, vl, lambda: dve.memset(scratch[:, 1:2], 0.0))
            dve.wait_ge(t.ffn_loaded, t.FFN)

            def add_xn(g):
                dve.wait_ge(rms_a.ready, GT * (g + 1))
                dve.tensor_tensor(h[:, part(g), :], t.proj[:, part(g), :], t.xn[:, part(g), :], ALU.add).then_inc(h_ready, 1)

            rms_a.vector(dve, t.proj, t.attn_gain[:, :], step, add_xn)
            rms_m.vector(dve, t.sparse, t.moe_gain[:, :], step)
            with dve.Fori(0, NG) as it:
                take.enter(it, VT)
                for f in range(NF):
                    dve.wait_ge(sl.free, it * ST + (NG + f + 1 + sl.banks))
                    take(lambda bank: dve.tensor_tensor(hidden[:, f, :], gate[:, f, :], bank, ALU.mult))
                take(lambda bank: dve.tensor_copy(ffn[:, bass.ds(it * GT, GT), :], bank.rearrange("p (c d) -> p c d", c=GT)))
                take.leave(NG)
            dve.wait_ge(rest_ready, 1)

            def add_rest(g):
                dve.wait_ge(rms_f.ready, GT * (g + 1))
                dve.tensor_tensor(x_tok[:, part(g), :], ffn[:, part(g), :], rest[:, part(g), :], ALU.add).then_inc(x_ready, 1)

            rms_f.vector(dve, ffn, t.ff_gain[:, :], step, add_rest)
            dve.wait_ge(x_ready, NG)


PIECES = [(c, min(512, N_CTX - c)) for c in range(0, N_CTX, 512)]
NK = N_CTX + N_CTX % 2
MASK_FILL = -float(2 ** 27)
HALF = H // 2
HC = HALF * S


def cross_attention_1(nc, io, x_tok, ident):
    NU = 2 * len(GROUPS) + (1 + HALF) * len(PIECES) + 1
    TURNS = 1
    A_HEADS = 12
    DEN = 24
    SCALE = float(np.float32(1.0) / np.sqrt(np.float32(HD)))
    with ExitStack() as stack:
        m = Memory(nc, stack, "xa1")
        wq, bq = m.sb("wq_twice", [P, 2, P]), m.sb("bq_twice", [P, 2])
        bk = m.sb("bk", [P, 1])
        wk, wv, wo = m.sb("wkT", [P, D]), m.sb("wvT", [P, D]), m.sb("woT", [P, D])
        bv, bo = m.sb("bv", [P, D]), m.sb("bo", [P, D])
        half_head = m.sb("half_head", [P, HALF])
        pair_row = m.sb("pair_row", [P, 2, 4])
        nm = Norm(m)
        att = nm.xn
        xnT = m.sb("xnT", [P, NT * P])
        q_hi = [m.sb(f"q_hi{g}", [P, NT * P], F32R) for g in range(2)]
        q_lo = [m.sb(f"q_lo{g}", [P, NT * P], F32R) for g in range(2)]
        ctx = [m.sb(f"ctx{u}", [P, NCH, D]) for u in range(2)]
        mask_row = [m.sb(f"mask_row{u}", [P, N_CTX], U8) for u in range(2)]
        mask_col = m.sb("mask_col", [P, B, FULL], U8)
        mask_tail = m.sb("mask_tail", [P, B], U8)
        key_fill = m.sb("key_fill", [P, B, NCH])
        bias = [m.sb(f"bias{u}", [P, NCH]) for u in range(2)]
        fill_row = m.sb("fill_row", [P, N_CTX])
        ctxT = m.sb("ctxT", [P, N_CTX])
        kf = m.sb("kf", [P, N_CTX])
        k_lo = m.sb("k_lo", [P, N_CTX], F32R)
        keys = [[m.sb(f"keys{u}{g}", [P, NK], F32R) for g in range(2)] for u in range(2)]
        vals = [m.sb(f"vals{u}", [P, NCH, 8, 32]) for u in range(2)]
        qb_hi = [[m.sb(f"qb_hi{u}{g}", [P, HC], F32R) for g in range(2)] for u in range(2)]
        qb_lo = [[m.sb(f"qb_lo{u}{g}", [P, HC], F32R) for g in range(2)] for u in range(2)]
        shift = [[m.sb(f"shift{u}{g}", [P, HC], BF16) for g in range(2)] for u in range(2)]
        prob = [m.sb(f"prob{i}", [P, 2 * HC]) for i in range(2)]
        junk = m.sb("junk", [P, 2, 512])
        tops = m.sb("tops", [P, 2 * HALF // 2, len(PIECES)])
        top = m.sb("top", [P, HALF])
        top_hi = m.sb("top_hi", [P, HALF], BF16)
        top_parts = m.sb("top_parts", [P, P])
        topT = m.sb("topT", [P, P], BF16)
        ones = m.sb("ones", [P, 32])
        sums = m.sb("sums", [P, 4, S])
        ones_b = m.sb("ones_b", [P, P], BF16)
        recip = m.sb("recip", [P, 4, 4])
        scratch = m.sb("scratch", [P, 2])
        sl = Lane(m, "setup_lane", 4)
        el = Lane(m, "exp_lane", 2)
        ps_o = m.psum("ps_o", [P, 4 * S])
        consts = m.sem("consts")
        chain = m.sem("vector_chain")
        pool_chain = m.sem("pool_chain")
        ctx_loaded = [m.sem(f"ctx_loaded{u}") for u in range(2)]
        presets = m.sem("presets")
        q_hi_ready = m.sem("q_hi_ready")
        key_fill_ready = m.sem("key_fill_ready")
        fill_ready = m.sem("fill_ready")
        k_hi_ready = m.sem("k_hi_ready")
        k_lo_ready = m.sem("k_lo_ready")
        keys_moved = [m.sem(f"keys_moved{g}") for g in range(2)]
        blocks_ready = m.sem("blocks_ready")
        top_ready = m.sem("top_ready")
        shift_ready = m.sem("shift_ready")
        prob_used = m.sem("prob_used")
        sums_ready = m.sem("sums_ready")
        att_ready = m.sem("att_ready")
        bias_added = m.sem("bias_added")
        mask_tail_cleared = m.sem("mask_tail_cleared")
        block = stack.enter_context(nc.Block())
        N_CONSTS = 12
        FIRST = len(GROUPS) + len(PIECES)
        QUERIES = NG + 2 * NG
        LOADS = 48

        def half_rows(g):
            return slice(64 * g, 64 * g + 64)

        def cols(b):
            return bass.ds(b * S, S)

        def batches(eng, enter, body, leave):
            body(0, 0, None, True, False)
            with eng.Fori(0, B // 2 - 1) as it:
                enter(it)
                body(it * 2 + 1, 1, it, False, False)
                body(it * 2 + 2, 0, it, False, False)
                leave(B // 2 - 1)
            body(B - 1, 1, NT - 1, False, True)

        @block.sync
        def _(sp):
            for dst, src in ((wq[:, :, :], "L1_xattn_WqT2"), (wk[:, :], "L1_xattn_WkT"), (bq[:, :], "L1_xattn_bq2"),
                             (bk[:, :], "L1_xattn_bkT"), (wv[:, :], "L1_xattn_WvT"), (wo[:, :], "L1_xattn_WoT"),
                             (half_head[:, :], "half_head"), (pair_row[:, :, :], "pair_row")):
                sp.dma_start(dst, io[src]).then_inc(consts, 16)
            load_row(sp, bv[:, :], io["L1_xattn_bv"], consts)
            load_row(sp, bo[:, :], io["L1_xattn_bo"], consts)
            sp.dma_start(mask_col[:, :, :], io["mask"][:, 0:FULL * P].rearrange("b (p j) -> p b j", j=FULL)).then_inc(consts, 16)
            sp.wait_ge(mask_tail_cleared, 1)
            sp.dma_start(mask_tail[0:TAIL, :], io["mask_tail"]).then_inc(consts, 16)

            def load(b, u):
                src = io["ctx_1024"][b] if isinstance(b, int) else io["ctx_1024"][bass.ds(b, 1)].rearrange("a t c -> (a t) c")
                row = io["mask_row"][b:b + 1, :] if isinstance(b, int) else io["mask_row"][bass.ds(b, 1), :]
                load_ctx(sp, ctx[u][:, :, :], src, ctx_loaded[u])
                sp.dma_start(mask_row[u][:, :], row.broadcast_to([P, N_CTX])).then_inc(ctx_loaded[u], 16)

            low = Tally(k_lo_ready)

            def move_keys(u):
                for g in range(2):
                    sp.wait_ge(k_lo_ready, low.next())
                    src, dst = half_rows(g), half_rows(1 - g)
                    sp.dma_start(keys[u][g][dst, 0:N_CTX].bitcast(F32), k_lo[src, :].bitcast(F32)).then_inc(keys_moved[g], 16)

            load(0, 0)
            load(1, 1)
            move_keys(0)
            with sp.Fori(0, B // 2 - 1) as it:
                low.enter(it, 4)
                for u in range(2):
                    sp.wait_ge(top_ready, it * 4 + 2 * (u + 1))
                    load(it * 2 + (2 + u), u)
                    move_keys(1 - u)
                low.leave(B // 2 - 1)
            move_keys(1)

        @block.gpsimd
        def _(pool):
            pool.memset(mask_tail[:, :], 0).then_inc(mask_tail_cleared, 1)
            loaded = [Tally(s) for s in ctx_loaded]
            step_t, tops_t, free = Tally(pool_chain), Tally(top_ready), Tally(sl.free)

            def setup(b, u, first=False, turns=TURNS):
                wait_apart(pool, (consts, 16 * N_CONSTS), [(ctx_loaded[u], loaded[u].next(LOADS))]
                           + ([] if first else [(top_ready, tops_t.next(2))]))
                pool.tensor_scalar(fill_row[:, :], mask_row[u][:, :], -1.0, -MASK_FILL, ALU.add, ALU.mult).then_inc(fill_ready, 1)
                wait_apart(pool, (consts, 16 * N_CONSTS), [(sl.free, free.value() + (1 + sl.banks))])
                for h in range(2):
                    for dst, src in ((qb_hi, q_hi), (qb_lo, q_lo)):
                        pool.tensor_tensor(
                            dst[u][h][:, :].rearrange("p (a q) -> p a q", q=S),
                            src[h][:, cols(b)].unsqueeze(1).broadcast_to([P, HALF, S]),
                            over(half_head[:, :], S), ALU.mult).then_inc(blocks_ready, 1)
                pool.tensor_copy(bias[u][:, :], key_fill[:, bass.ds(b, 1), :].rearrange("p a j -> p (a j)")).then_inc(blocks_ready, 1)
                pool.wait_ge(sl.free, free.value() + (NU - len(GROUPS) + turns + sl.banks))
                free.next(NU + turns)
                for g in range(2):
                    pool.tensor_tensor(shift[u][g][:, :].rearrange("p (a q) -> p a q", q=P), under(topT[:, :], 4),
                                       over(pair_row[:, g, :], P), ALU.mult).then_inc(shift_ready, 1)

            pool.memset(ones[:, :], 1.0).then_inc(presets, 1)
            pool.memset(ones_b[:, :], 1.0).then_inc(presets, 1)
            pool.memset(top_parts[:, :], 0.0).then_inc(presets, 1)
            for u in range(2):
                pool.memset(vals[u][:, :, :, :], 0.0).then_inc(pool_chain, 1)
                pool.wait_ge(pool_chain, step_t.next())
                pool.memset(vals[u][:, :, :, DEN:DEN + 1], 1.0).then_inc(presets, 1)
            for u in range(2):
                for g in range(2):
                    pool.memset(keys[u][g][:, N_CTX:NK].bitcast(F32), 0.0).then_inc(pool_chain, 1)
                    pool.wait_ge(pool_chain, step_t.next())
            pool.wait_ge(consts, 16 * N_CONSTS)
            pool.wait_ge(key_fill_ready, 2)
            pool.wait_ge(sl.free, FIRST + NG + 2 + sl.banks)
            free.next(QUERIES)
            setup(0, 0, first=True, turns=0)

            tallies = (tops_t, free)

            def enter(it):
                for t, per in zip(tallies, (4, 2 * (NU + TURNS))):
                    t.enter(it, per)
                for t in loaded:
                    t.enter(it, LOADS)

            def leave(n):
                for t in (*tallies, *loaded):
                    t.leave(n)

            batches(pool, enter, lambda b, u, n, first, last: None if last else setup(b + 1, 1 - u, turns=0 if first else TURNS),
                    leave)
            pool.tensor_tensor(x_tok[:, :, :], x_tok[:, :, :], under(bo[:, :], NT), ALU.add).then_inc(bias_added, 1)

        @block.tensor
        def _(pe):
            s, e = Fill(pe, sl), Fill(pe, el)
            loaded = [Tally(t) for t in ctx_loaded]
            moved = [Tally(t) for t in keys_moved]
            blocks_t, top_t, shift_t, taken_t = (Tally(t) for t in (blocks_ready, top_ready, shift_ready, sums_ready))
            pe.wait_ge(consts, 16 * N_CONSTS)
            pe.wait_ge(presets, 5)
            for _ in range(2):
                pe.matmul(ps_o[0:32, 0:32], ones[:, :], ones[:, :], start=True, stop=True).then_inc(prob_used, 1)

            def setup_parts(u):
                def turn_ctx():
                    pe.wait_ge(ctx_loaded[u], loaded[u].next(LOADS))
                    for chunks in GROUPS:
                        def fill(bank):
                            for j in chunks:
                                r = ROWS[j]
                                last = pe.transpose(bank[:, (j % 4) * P:(j % 4) * P + r], ctx[u][0:r, j, :], ident[0:r, 0:r])
                            return last
                        s(fill)

                def project_keys():
                    s.wait_emptied()
                    for c, w in PIECES:
                        s(lambda bank: pe.matmul(bank[:, 0:w], wk[:, :], ctxT[:, c:c + w], start=True, stop=True))

                def project_values():
                    for chunks in GROUPS:
                        def fill(bank):
                            for j in chunks:
                                r = ROWS[j]
                                last = pe.matmul(bank[0:r, (j % 4) * D:(j % 4 + 1) * D], ctxT[:, j * P:j * P + r], wv[:, :],
                                                 start=True, stop=True)
                            return last
                        s(fill)

                def pair_scores(pair):
                    g, a = divmod(pair, HALF // 2)
                    if pair == 0:
                        pe.wait_ge(blocks_ready, blocks_t.next(5))
                    if a == 0:
                        pe.wait_ge(keys_moved[g], moved[g].next(16))
                    for c, w in PIECES:
                        w += w % 2
                        s(lambda bank: pe.matmul(bank[:, 0:w], qb_hi[u][g][:, a * P:(a + 1) * P], keys[u][g][:, c:c + w],
                                                 start=True, stop=True))

                def turn_top():
                    pe.wait_ge(top_ready, top_t.next(2))
                    s(lambda bank: pe.transpose(bank[:, 0:P], top_parts[:, :], ident[:, :]))

                return turn_ctx, [project_keys, None, None, None, *[lambda pair=pair: pair_scores(pair) for pair in range(HALF)],
                                  lambda: (turn_top(), project_values())]

            turn_ctx, parts = setup_parts(0)
            turn_ctx()
            parts[0]()
            for g in range(NG):
                pe.wait_ge(nm.ready, GT * (g + 1))
                def fill(bank):
                    for c in range(GT):
                        last = pe.transpose(bank[:, c * P:(c + 1) * P], nm.xn[:, GT * g + c, :], ident[:, :])
                    return last
                s(fill)
            s.wait_emptied()
            for g in range(NG):
                for h in range(2):
                    s(lambda bank: pe.matmul(bank, wq[:, h, :], xnT[:, g * GC:(g + 1) * GC], start=True, stop=True))
            for part in parts[1:]:
                if part:
                    part()

            def turn_sums(u):
                rows = slice(64 * u, 64 * u + 64)

                def fill(bank):
                    for i in range(4):
                        last = pe.matmul(bank[rows, i * P:(i + 1) * P], sums[:, i, :], ident[:, :], start=True, stop=True)
                    return last
                s(fill)

            def weigh(u, c, j):
                r = ROWS[j]
                pe.wait_ge(el.free, e.t.value() + el.banks - (2 if j < NCH - 1 else 0))
                p = prob[c % 2]
                for k in range(4):
                    pe.matmul(ps_o[32 * k:32 * k + 32, 0:3 * S], vals[u][0:r, j, k, :], p[0:r, 3 * S * k:3 * S * (k + 1)],
                              start=(j == 0), stop=(j == NCH - 1), skip_group_check=True)
                for k in range(4):
                    last = pe.matmul(ps_o[32 * k:32 * k + 32, 3 * S:4 * S], vals[u][0:r, j, 4 + k, :],
                                     p[0:r, (A_HEADS + k) * S:(A_HEADS + k + 1) * S],
                                     start=False, stop=(j == NCH - 1), skip_group_check=True)
                last.then_inc(prob_used, 1)

            def attend(b, u, n, first, last):
                turn_ctx, parts = (None, [None] * NCH) if last else setup_parts(1 - u)
                if not last:
                    turn_ctx()
                pe.wait_ge(shift_ready, shift_t.next(2))
                for j in range(NCH):
                    r = ROWS[j]
                    for g in range(2):
                        def fill(bank):
                            k = keys[u][g][:, j * P:j * P + r]
                            pe.matmul(bank[0:r, :], k, qb_hi[u][g][:, :], start=True, stop=False)
                            pe.matmul(bank[0:r, :], k, qb_lo[u][g][:, :], start=False, stop=False)
                            return pe.matmul(bank[0:r, :], ones_b[:, 0:r], shift[u][g][:, :], start=False, stop=True)
                        e(fill)
                    if j == 1:
                        pe.wait_ge(sums_ready, taken_t.next())
                    if 3 < j < NCH - 1 and parts[j]:
                        parts[j]()
                    if j > 0:
                        weigh(u, u * NCH + j - 1, j - 1)
                    if j == NCH - 1:
                        weigh(u, u * NCH + j, j)
                    if (j <= 3 or j == NCH - 1) and parts[j]:
                        parts[j]()
                    if j == 1 and not first:
                        turn_sums(1 - u)

            tallies = (blocks_t, top_t, shift_t, taken_t)

            def enter(it):
                s.enter(it, 2 * (NU + TURNS))
                e.enter(it, 4 * NCH)
                for t, per in zip(tallies, (10, 4, 4, 2)):
                    t.enter(it, per)
                for t in moved:
                    t.enter(it, 32)
                for t in loaded:
                    t.enter(it, LOADS)

            def leave(n):
                for t in (s, e, *tallies, *loaded, *moved):
                    t.leave(n)

            batches(pe, enter, attend, leave)
            pe.wait_ge(sums_ready, B + 1)
            turn_sums(1)
            pe.wait_ge(att_ready, 1)
            for g in range(NG):
                def fill(bank):
                    for c in range(GT):
                        last = pe.transpose(bank[:, c * P:(c + 1) * P], att[:, GT * g + c, :], ident[:, :])
                    return last
                s(fill)
            s.wait_emptied()
            pe.wait_ge(bias_added, 1)
            for g in range(NG):
                def fill(bank):
                    pe.matmul(bank, ident[:, :], x_tok[:, GT * g:GT * (g + 1), :].rearrange("p c d -> p (c d)"),
                              start=True, stop=False, skip_group_check=True)
                    for c in range(GT):
                        n = GT * g + c
                        last = pe.matmul(bank[:, c * D:(c + 1) * D], xnT[:, n * P:(n + 1) * P], wo[:, :],
                                         start=False, stop=(c == GT - 1), skip_group_check=True)
                    return last
                s(fill)

        @block.scalar
        def _(act):
            take = Take(act, el)
            nm.scalar(act)
            for _ in range(el.banks):
                act.activation(scratch[:, 0:1], ident[:, 0:1], ACT.Copy).then_inc(el.free, 1)
                act.wait_ge(el.free, _ + 1)
            blocks_t, used, free = Tally(blocks_ready), Tally(prob_used), Tally(sl.free)

            def split_keys(u, g):
                rows = half_rows(g)
                act.wait_ge(sl.free, free.value() + (len(GROUPS) + len(PIECES) + sl.banks))
                act.activation(keys[u][g][rows, 0:N_CTX], kf[rows, :], ACT.Copy).then_inc(k_hi_ready, 1)

            for g in range(2):
                split_keys(0, g)
            for g in range(NG):
                for h in range(2):
                    k = FIRST + NG + 2 * g + h
                    act.wait_ge(sl.full, k + 1)
                    act.activation(q_hi[h][:, g * GC:(g + 1) * GC], sl.ps[:, k % sl.banks, :], ACT.Identity,
                                   bias=bq[:, h:h + 1]).then_inc(q_hi_ready, 1)
            free.next(NU + QUERIES)

            def attend(b, u, n, first, last):
                act.wait_ge(blocks_ready, blocks_t.next(5))
                for j in range(NCH):
                    r = ROWS[j]
                    i = (u * NCH + j) % 2
                    act.wait_ge(prob_used, used.next())
                    for g in range(2):
                        take(lambda bank: act.activation(prob[i][0:r, g * HC:(g + 1) * HC], bank[0:r, :], ACT.Exp,
                                                         bias=bias[u][0:r, j:j + 1], scale=SCALE))
                    if j in (1, 2) and not last:
                        split_keys(1 - u, j - 1)
                free.next((0 if last else NU) + (0 if first else TURNS))

            def enter(it):
                take.enter(it, 4 * NCH)
                blocks_t.enter(it, 10)
                used.enter(it, 2 * NCH)
                free.enter(it, 2 * (NU + TURNS))

            def leave(n):
                for t in (take, blocks_t, used, free):
                    t.leave(n)

            batches(act, enter, attend, leave)

        @block.vector
        def _(dve):
            take, step = Take(dve, sl), Chain(dve, chain)
            loaded = [Tally(t) for t in ctx_loaded]
            fill_t, o_t, hi_t = Tally(fill_ready), Tally(prob_used), Tally(k_hi_ready)
            o_t.next(2)
            for _ in range(sl.banks):
                dve.memset(scratch[:, 1:2], 0.0).then_inc(sl.free, 1)
                dve.wait_ge(sl.free, _ + 1)
            dve.memset(scratch[:, 1:2], 0.0).then_inc(sums_ready, 1)
            nm.vector(dve, x_tok, step)
            dve.wait_ge(consts, 16 * N_CONSTS)

            def take_turned(n, u):
                rows = slice(64 * u, 64 * u + 64)
                dst = att[rows, n, :] if isinstance(n, int) else att[rows, bass.ds(n, 1), :].rearrange("p a d -> p (a d)")
                dst3 = dst[:, 0:A_HEADS * HD].rearrange("p (k i d) -> p i k d", k=4, d=HD)
                dst1 = dst[:, A_HEADS * HD:D].rearrange("p (k d) -> p k d", d=HD)

                def out_of(bank):
                    b = bank[rows, :]
                    step(dve.reciprocal(recip[rows, :, :], b.rearrange("p (i k c) -> p i k c", i=4, k=4)[:, :, :, DEN]))
                    src3 = b[:, 0:3 * (P + HD)].rearrange("p (i x) -> p i x", i=3)[:, :, 0:P]
                    step(dve.tensor_tensor(dst3, src3.rearrange("p i (k c) -> p i k c", k=4)[:, :, :, 0:HD],
                                           recip[rows, 0:3, :].unsqueeze(3).broadcast_to([64, 3, 4, HD]), ALU.mult))
                    return dve.tensor_tensor(dst1, b[:, 3 * P:4 * P].rearrange("p (k c) -> p k c", k=4)[:, :, 0:HD],
                                             over(recip[rows, 3, :], HD), ALU.mult)
                take(out_of)

            def take_keys(u, before):
                for chunks in GROUPS:
                    c0, w = chunks[0] * P, sum(ROWS[j] for j in chunks)
                    take(lambda bank: dve.tensor_copy(ctxT[:, c0:c0 + w], bank[:, 0:w]))
                dve.wait_ge(ctx_loaded[u], loaded[u].next(LOADS))
                for c, w in PIECES:
                    take(lambda bank: dve.scalar_tensor_tensor(out=kf[:, c:c + w], in0=bank[:, 0:w], scalar=bk[:, 0:1],
                                                               in1=mask_row[u][:, c:c + w], op0=ALU.add, op1=ALU.mult))
                if before is not None:
                    take_turned(*before)
                for g in range(2):
                    rows = half_rows(g)
                    dve.wait_ge(k_hi_ready, hi_t.next())
                    dve.tensor_tensor(k_lo[rows, :], kf[rows, :], keys[u][g][rows, 0:N_CTX], ALU.subtract).then_inc(k_lo_ready, 1)

            def take_maxima_and_values(u):
                dve.wait_ge(fill_ready, fill_t.next())
                for pair in range(HALF):
                    for i, (c, w) in enumerate(PIECES):
                        wait_apart(dve, (consts, 16 * N_CONSTS), [(sl.full, take.t.next()), (sl.free, take.t.value() + (sl.banks - 2))])
                        dve.tensor_tensor_reduce(junk[:, take.k % 2, 0:w], sl.ps[:, take.k % sl.banks, 0:w], fill_row[:, c:c + w], 1.0,
                                                 -3.0e38, ALU.add, ALU.max, tops[:, pair, i:i + 1]).then_inc(sl.free, 1)
                        take.k += 1
                take.wait_taken()
                step(dve.tensor_reduce(top[:, :], tops[:, :, :], X, ALU.max))
                step(dve.tensor_scalar(top_hi[:, :], top[:, :], -1.0, None, ALU.mult))
                slots = top_parts[:, :].rearrange("p (g i) -> p g i", g=2)[:, :, 0:8].rearrange("p g (a part) -> p g a part", part=2)
                by_half = [ap[:, :].rearrange("p (g a) -> p g a", g=2) for ap in (top, top_hi)]
                dve.tensor_copy(slots[:, :, :, 0], by_half[1]).then_inc(top_ready, 1)
                dve.scalar_tensor_tensor(out=slots[:, :, :, 1], in0=by_half[0], scalar=-1.0, in1=by_half[1],
                                         op0=ALU.mult, op1=ALU.subtract).then_inc(top_ready, 1)
                take(lambda bank: dve.tensor_copy(topT[:, :], bank[:, 0:P]))
                for chunks in GROUPS:
                    r, w, j = ROWS[chunks[0]], len(chunks), chunks[0]

                    def out_of(bank):
                        src, dst, cut = bank[0:r, 0:w * D].rearrange("p (j d) -> p j d", j=w), vals[u][0:r, j:j + w, :, :], A_HEADS * HD
                        dve.tensor_copy(dst[:, :, 0:4, 0:3 * HD], src[:, :, 0:cut].rearrange("p j (k d) -> p j k d", k=4))
                        return dve.tensor_copy(dst[:, :, 4:8, 0:HD], src[:, :, cut:D].rearrange("p j (k d) -> p j k d", k=4))
                    take(out_of)

            take_keys(0, None)
            for g in range(NG):
                take(lambda bank: dve.tensor_copy(xnT[:, g * GC:(g + 1) * GC], bank))
            dve.tensor_scalar(key_fill[:, :, 0:FULL], mask_col[:, :, :], -1.0, -MASK_FILL * SCALE, ALU.add,
                              ALU.mult).then_inc(key_fill_ready, 1)
            dve.tensor_scalar(key_fill[:, :, FULL], mask_tail[:, :], -1.0, -MASK_FILL * SCALE, ALU.add,
                              ALU.mult).then_inc(key_fill_ready, 1)
            for g in range(NG):
                for h in range(2):
                    part = slice(g * GC, (g + 1) * GC)
                    dve.wait_ge(q_hi_ready, 2 * g + h + 1)
                    take(lambda bank: dve.scalar_tensor_tensor(out=q_lo[h][:, part], in0=bank, scalar=bq[:, h:h + 1],
                                                               in1=q_hi[h][:, part], op0=ALU.add, op1=ALU.subtract))
            dve.wait_ge(presets, 5)
            take_maxima_and_values(0)

            def attend(b, u, n, first, last):
                if last:
                    take_turned(n, 1 - u)
                else:
                    take_keys(1 - u, None if first else (n, 1 - u))
                    take_maxima_and_values(1 - u)
                dve.wait_ge(prob_used, o_t.next(NCH))
                dve.tensor_copy(flat(sums[:, :, :]), ps_o[:, :]).then_inc(sums_ready, 1)

            tallies = (take, step, *loaded, fill_t, o_t, hi_t)

            def enter(it):
                for t, per in zip(tallies, (2 * (NU + TURNS), 8, LOADS, LOADS, 2, 2 * NCH, 4)):
                    t.enter(it, per)

            def leave(n):
                for t in tallies:
                    t.leave(n)

            batches(dve, enter, attend, leave)
            take_turned(NT - 1, 1)
            take.wait_taken()
            dve.tensor_tensor(att[:, :, :], att[:, :, :], under(bv[:, :], NT), ALU.add).then_inc(att_ready, 1)
            for g in range(NG):
                take(lambda bank: dve.tensor_copy(xnT[:, g * GC:(g + 1) * GC], bank))
            for g in range(NG):
                take(lambda bank: dve.tensor_copy(x_tok[:, GT * g:GT * (g + 1), :], bank.rearrange("p (c d) -> p c d", c=GT)))


def program(nc, io):
    with ExitStack() as stack:
        m = Memory(nc, stack, "all")
        ident = m.sb("ident", [P, P])
        x_tok = m.sb("x_tok", [P, NT, D])
        loaded = m.sem("loaded")
        stored = m.sem("stored")
        x_dram = io["x"].rearrange("b s d -> (b s) d").rearrange("(n p) d -> p n d", p=P)
        with nc.Block() as block:
            @block.sync
            def _(sp):
                sp.dma_start(ident[:, :], io["ident"]).then_inc(loaded, 16)
                sp.dma_start(x_tok[:, :, :], x_dram).then_inc(loaded, 16)
                sp.wait_ge(loaded, 32)
        for part in PARTS:
            part(nc, io, x_tok, ident)
        with nc.Block() as block:
            @block.sync
            def _(sp):
                sp.dma_start(io["out"].rearrange("b s d -> (b s) d").rearrange("(n p) d -> p n d", p=P), x_tok[:, :, :]).then_inc(stored, 16)
                sp.wait_ge(stored, 16)


PARTS = (cross_attention_0, linear_attention_0, ffn_0, cross_attention_1, layer_1_end)


def constants():
    pos = np.arange(P)[:, None] % S
    freq = (1.0 / np.float32(10000.0) ** np.arange(0, HD, 2, dtype=np.float32)).astype(np.float32)
    angle = (pos.astype(np.float32) * freq[None, :]).astype(np.float32)
    rope = np.zeros((P, 2, HD), np.float32)
    rope[:, 0, 0::2] = rope[:, 0, 1::2] = np.cos(angle)
    rope[:, 1, 0::2], rope[:, 1, 1::2] = -np.sin(angle), np.sin(angle)
    head = np.arange(D) // HD
    own = (head[:, None] == head[None, :]).astype(np.float32)
    row = np.arange(P)
    half_head = (row[:, None] % 64 // HD == np.arange(H // 2)[None, :]).astype(np.float32)
    pair_row = np.zeros((P, 2, 4), np.float32)
    for g in range(2):
        for a in range(4):
            pair_row[64 * g + 2 * a:64 * g + 2 * a + 2, g, a] = 1
    causal = np.where(np.arange(S)[None, :] <= row[:, None] % S, 0.0, CAUSAL_FILL).astype(np.float32)
    parity = (np.arange(H)[None, :] % 2 == row[:, None] // 64).astype(np.float32)
    return {"causal": causal, "head_parity": parity, "half_head": half_head, "pair_row": pair_row,
            "ident": np.eye(P, dtype=np.float32), "rope": rope, "own_head": own,
            "rank": np.tile(np.arange(E, 0, -1, dtype=np.float32), (P, 1)),
            "own_head_scaled": (own / np.sqrt(np.float32(HD))).astype(np.float32)}


def layout(inputs):
    a = {k: np.asarray(v) for k, v in inputs.items()}
    for name in ("L0_xattn_Wq", "L0_xattn_Wv", "L0_xattn_Wo", "L1_attn_w_qkv", "L1_attn_w_out", "L1_ffn_gate_w", "L1_xattn_Wk",
                 "L1_xattn_Wv", "L1_xattn_Wo"):
        a[name + "T"] = np.ascontiguousarray(a.pop(name).T)
    a["L1_ffn_b1T"] = np.ascontiguousarray(a.pop("L1_ffn_b1").reshape(E, FF // P, P).transpose(2, 0, 1).reshape(P, -1))
    wt = a.pop("L1_xattn_Wq").T.reshape(D, 2, 1, D // 2)
    a["L1_xattn_WqT2"] = np.ascontiguousarray(np.repeat(wt, 2, axis=2).reshape(D, 2, D))
    bt = a.pop("L1_xattn_bq").reshape(2, 1, D // 2)
    a["L1_xattn_bq2"] = np.ascontiguousarray(np.repeat(bt, 2, axis=1).reshape(2, D).T)
    a["L1_xattn_bkT"] = a.pop("L1_xattn_bk").reshape(D, 1)
    mask = a.pop("mask_BxS2_bf1").view(np.uint8)
    full = mask[:, :FULL * P].reshape(B, P, FULL)
    a["mask_row"] = np.ascontiguousarray(np.concatenate([full.transpose(0, 2, 1).reshape(B, -1), mask[:, FULL * P:]], 1))
    a["mask"] = mask
    a["mask_tail"] = np.ascontiguousarray(mask[:, FULL * P:].T)
    return {**a, **constants()}


def kernel(**inputs):
    import concourse.bacc as bacc
    from concourse.bass_utils import run_bass_kernel_spmd

    nc = bacc.Bacc("TRN2", target_bir_lowering=False, num_devices=1)
    arrays = layout(inputs)
    io = {name: nc.dram_tensor(f"in_{name}", a.shape, mybir.dt.from_np(a.dtype), kind="ExternalInput").ap()
          for name, a in arrays.items()}
    io["out"] = nc.dram_tensor("out", (B, S, D), F32, kind="ExternalOutput").ap()
    program(nc, io)
    result = run_bass_kernel_spmd(nc, [{f"in_{name}": a for name, a in arrays.items()}], core_ids=[0])
    return result.results[0]["out"]
```
